# Optimizing a Trainium2 kernel written in Bass

```python
import numpy as np
import jax
import jax.numpy as jnp

def _softmax(x, axis=-1):
    return jax.nn.softmax(x, axis=axis)

def _gelu(x):
    return jax.nn.gelu(x, approximate=True)

def _silu(x):
    return jax.nn.silu(x)

def _sigmoid(x):
    return jax.nn.sigmoid(x)

def _layernorm(x, axis=-1, eps=1e-05):
    m = jnp.mean(x, axis=axis, keepdims=True)
    v = jnp.var(x, axis=axis, keepdims=True)
    return (x - m) / jnp.sqrt(v + eps)

def _scatter_add(tgt, idx, src, axis=0):
    return tgt.at[idx].add(src)

def _segment_sum(src, seg, n):
    return jax.ops.segment_sum(src, seg, n)
kernel_name = 'mk_seq_preln_d4_jaxref_r8_e7dad8'

def setup_inputs(seed: int=0):
    np.random.seed(seed)
    _w = jnp.asarray

    def _L0_attn_setup():
        import jax, jax.numpy as jnp
        import numpy as np
        from jax import lax
        D_MODEL = 128
        KERNEL = 5
        PAD = (KERNEL - 1) // 2
        key = jax.random.key(seed)
        k1, k2, k3, k4, k5 = jax.random.split(key, 5)
        B, T, D = (8, 512, D_MODEL)
        x = jax.random.normal(k1, (B, T, D), dtype=jnp.float32)
        decay_logit = jnp.zeros((D,), dtype=jnp.float32)
        lim = 1.0 / np.sqrt(D)
        W = jax.random.uniform(k2, (D, D), minval=-lim, maxval=lim, dtype=jnp.float32)
        b = jax.random.uniform(k3, (D,), minval=-lim, maxval=lim, dtype=jnp.float32)
        limc = 1.0 / np.sqrt(KERNEL)
        conv_w = jax.random.uniform(k4, (D, 1, KERNEL), minval=-limc, maxval=limc, dtype=jnp.float32)
        conv_b = jax.random.uniform(k5, (D,), minval=-limc, maxval=limc, dtype=jnp.float32)
        return {'x': x, 'decay_logit': decay_logit, 'W': W, 'b': b, 'conv_w': conv_w, 'conv_b': conv_b}
    _L0_attn_in = _L0_attn_setup()

    def _L0_ffn_setup():
        import jax, jax.numpy as jnp
        import numpy as np
        N_EXPERTS = 16
        TOP_K = 4
        HIDDEN = 128
        INTER = 64
        B, S = (2, 128)
        key = jax.random.key(seed)
        k1, k2, k3, k4, k5 = jax.random.split(key, 5)
        return {'hidden_states': jax.random.normal(k1, (B, S, HIDDEN), dtype=jnp.float32), 'gate_w': jax.random.normal(k2, (N_EXPERTS, HIDDEN), dtype=jnp.float32) * 0.02, 'w1': jax.random.normal(k3, (N_EXPERTS, HIDDEN, INTER), dtype=jnp.float32) * 0.02, 'w3': jax.random.normal(k4, (N_EXPERTS, HIDDEN, INTER), dtype=jnp.float32) * 0.02, 'w2': jax.random.normal(k5, (N_EXPERTS, INTER, HIDDEN), dtype=jnp.float32) * 0.02}
    _L0_ffn_in = _L0_ffn_setup()

    def _L1_attn_setup():
        import jax, jax.numpy as jnp
        import numpy as np
        NUM_HEADS = 16
        D_MODEL = 128
        HEAD_DIM = D_MODEL // NUM_HEADS
        WINDOW = 64
        SCALE = 8.0 / HEAD_DIM
        LN_EPS = 1e-05

        def _layernorm(t, gamma, beta):
            mu = jnp.mean(t, axis=-1, keepdims=True)
            var = jnp.var(t, axis=-1, keepdims=True)
            return (t - mu) * jax.lax.rsqrt(var + LN_EPS) * gamma + beta
        key = jax.random.key(seed)
        ks = jax.random.split(key, 4)
        x = jax.random.normal(ks[0], (4, 1024, D_MODEL), dtype=jnp.float32)
        W_qkv = jax.random.normal(ks[1], (D_MODEL, 3 * D_MODEL), dtype=jnp.float32) * D_MODEL ** (-0.5)
        ln_gamma = jnp.ones((HEAD_DIM,), dtype=jnp.float32)
        ln_beta = jnp.zeros((HEAD_DIM,), dtype=jnp.float32)
        W_proj = jax.random.normal(ks[2], (D_MODEL, D_MODEL), dtype=jnp.float32) * D_MODEL ** (-0.5)
        b_proj = jax.random.normal(ks[3], (D_MODEL,), dtype=jnp.float32) * 0.02
        return {'x': x, 'W_qkv': W_qkv, 'ln_gamma': ln_gamma, 'ln_beta': ln_beta, 'W_proj': W_proj, 'b_proj': b_proj}
    _L1_attn_in = _L1_attn_setup()

    def _L1_ffn_setup():
        import jax, jax.numpy as jnp
        import numpy as np
        H = 128
        M = 64
        E = 16
        TOP_K = 2
        SCALE = 2.5
        NORM_TOPK = True
        B, S = (1, 128)

        def _moe(x, gate_w, w_gate, w_up, w_down, ws_gate, ws_up, ws_down):
            T = x.shape[0]
            shared = jax.nn.silu(x @ ws_gate) * (x @ ws_up) @ ws_down
            scores = jax.nn.sigmoid(x.astype(jnp.float32) @ gate_w.T.astype(jnp.float32))
            topk_w, topk_idx = jax.lax.top_k(scores, TOP_K)
            if NORM_TOPK and TOP_K > 1:
                topk_w = topk_w / (topk_w.sum(-1, keepdims=True) + 1e-20)
            topk_w = topk_w * SCALE
            route = jnp.zeros((T, E), topk_w.dtype).at[jnp.arange(T)[:, None], topk_idx].set(topk_w)
            g = jnp.einsum('th,ehm->etm', x, w_gate)
            u = jnp.einsum('th,ehm->etm', x, w_up)
            eo = jnp.einsum('etm,emh->eth', jax.nn.silu(g) * u, w_down)
            routed = jnp.einsum('te,eth->th', route.astype(x.dtype), eo)
            return routed + shared
        key = jax.random.key(seed)
        ks = jax.random.split(key, 8)
        std = 0.02
        return {'hidden_states': jax.random.normal(ks[0], (B, S, H), jnp.float32), 'gate_w': jax.random.normal(ks[1], (E, H), jnp.float32) * std, 'w_gate': jax.random.normal(ks[2], (E, H, M), jnp.float32) * std, 'w_up': jax.random.normal(ks[3], (E, H, M), jnp.float32) * std, 'w_down': jax.random.normal(ks[4], (E, M, H), jnp.float32) * std, 'ws_gate': jax.random.normal(ks[5], (H, M), jnp.float32) * std, 'ws_up': jax.random.normal(ks[6], (H, M), jnp.float32) * std, 'ws_down': jax.random.normal(ks[7], (M, H), jnp.float32) * std}
    _L1_ffn_in = _L1_ffn_setup()

    def _L2_attn_setup():
        import jax, jax.numpy as jnp
        import numpy as np
        EPS = 1e-12

        def _rmsnorm(x, gamma):
            d = gamma.shape[0]
            norm = jnp.sqrt(jnp.sum(x * x, axis=-1, keepdims=True))
            xn = x / jnp.maximum(norm, EPS)
            return xn * jnp.sqrt(jnp.asarray(d, x.dtype)) * gamma
        key = jax.random.key(seed)
        k1, k2 = jax.random.split(key)
        B, N, D = (4, 512, 128)
        x = jax.random.normal(k1, (B, N, D), dtype=jnp.float32)
        W_qkva = jax.random.normal(k2, (3 * D, D), dtype=jnp.float32) * 0.02
        gamma = jnp.ones((D,), dtype=jnp.float32)
        return {'x': x, 'W_qkva': W_qkva, 'gamma': gamma}
    _L2_attn_in = _L2_attn_setup()

    def _L2_ffn_setup():
        import jax, jax.numpy as jnp
        import numpy as np
        D_MODEL = 128
        NUM_EXPERTS = 8
        TOP_K = 2
        B, S = (4, 256)
        key = jax.random.key(seed)
        ks = jax.random.split(key, 7)
        scale_in = 1.0 / np.sqrt(D_MODEL)
        scale_hid = 1.0 / np.sqrt(2 * D_MODEL)
        return {'x': jax.random.normal(ks[0], (B, S, D_MODEL), dtype=jnp.float32), 'Wg': jax.random.normal(ks[1], (D_MODEL, NUM_EXPERTS), dtype=jnp.float32) * scale_in, 'bg': jnp.zeros((NUM_EXPERTS,), dtype=jnp.float32), 'W1': jax.random.normal(ks[2], (NUM_EXPERTS, D_MODEL, 2 * D_MODEL), dtype=jnp.float32) * scale_in, 'b1': jnp.zeros((NUM_EXPERTS, 2 * D_MODEL), dtype=jnp.float32), 'W2': jax.random.normal(ks[3], (NUM_EXPERTS, 2 * D_MODEL, D_MODEL), dtype=jnp.float32) * scale_hid, 'b2': jnp.zeros((NUM_EXPERTS, D_MODEL), dtype=jnp.float32)}
    _L2_ffn_in = _L2_ffn_setup()

    def _L3_attn_setup():
        import jax, jax.numpy as jnp
        import numpy as np
        import math
        D_MODEL = 128
        N_HEAD = 16
        D_HEAD = D_MODEL // N_HEAD
        D_KMAP = 128
        D_INNER = 512

        def _layer_norm(x, g, b, eps=1e-05):
            mu = jnp.mean(x, axis=-1, keepdims=True)
            var = jnp.mean(jnp.square(x - mu), axis=-1, keepdims=True)
            return (x - mu) * jax.lax.rsqrt(var + eps) * g + b

        def _fourier_kernel(x, proj_mat):
            p = jnp.einsum('blhd,dm->blhm', x, proj_mat) / math.sqrt(D_HEAD)
            return jnp.concatenate([jnp.cos(p), jnp.sin(p)], axis=-1) / math.sqrt(D_KMAP)
        key = jax.random.key(seed)
        ks = jax.random.split(key, 12)
        s = 0.02
        return {'x': jax.random.normal(ks[0], (4, 512, D_MODEL), dtype=jnp.float32), 'proj_mat': jax.random.normal(ks[1], (D_HEAD, D_KMAP), dtype=jnp.float32), 'wq': jax.random.normal(ks[2], (D_MODEL, D_MODEL), dtype=jnp.float32) * s, 'bq': jnp.zeros((D_MODEL,), jnp.float32), 'wk': jax.random.normal(ks[3], (D_MODEL, D_MODEL), dtype=jnp.float32) * s, 'bk': jnp.zeros((D_MODEL,), jnp.float32), 'wv': jax.random.normal(ks[4], (D_MODEL, D_MODEL), dtype=jnp.float32) * s, 'bv': jnp.zeros((D_MODEL,), jnp.float32), 'wo': jax.random.normal(ks[5], (D_MODEL, D_MODEL), dtype=jnp.float32) * s, 'bo': jnp.zeros((D_MODEL,), jnp.float32), 'ln1_g': jnp.ones((D_MODEL,), jnp.float32), 'ln1_b': jnp.zeros((D_MODEL,), jnp.float32), 'w1': jax.random.normal(ks[6], (D_MODEL, D_INNER), dtype=jnp.float32) * s, 'b1': jnp.zeros((D_INNER,), jnp.float32), 'w2': jax.random.normal(ks[7], (D_INNER, D_MODEL), dtype=jnp.float32) * s, 'b2': jnp.zeros((D_MODEL,), jnp.float32), 'ln2_g': jnp.ones((D_MODEL,), jnp.float32), 'ln2_b': jnp.zeros((D_MODEL,), jnp.float32)}
    _L3_attn_in = _L3_attn_setup()

    def _L3_ffn_setup():
        import jax, jax.numpy as jnp
        import numpy as np
        HIDDEN = 128
        INTER = 512
        key = jax.random.key(seed)
        k1, k2, k3, k4, k5 = jax.random.split(key, 5)
        hidden_states = jax.random.normal(k1, (4, 256, HIDDEN), dtype=jnp.float32)
        W1 = jax.random.normal(k2, (HIDDEN, INTER), dtype=jnp.float32) * (1.0 / np.sqrt(HIDDEN))
        b1 = jax.random.normal(k3, (INTER,), dtype=jnp.float32) * 0.02
        W2 = jax.random.normal(k4, (INTER, HIDDEN), dtype=jnp.float32) * (1.0 / np.sqrt(INTER))
        b2 = jax.random.normal(k5, (HIDDEN,), dtype=jnp.float32) * 0.02
        return {'hidden_states': hidden_states, 'W1': W1, 'b1': b1, 'W2': W2, 'b2': b2}
    _L3_ffn_in = _L3_ffn_setup()
    _d = {'L0_attn_x': _L0_attn_in['x'], 'L0_attn_decay_logit': _L0_attn_in['decay_logit'], 'L0_attn_W': _L0_attn_in['W'], 'L0_attn_b': _L0_attn_in['b'], 'L0_attn_conv_w': _L0_attn_in['conv_w'], 'L0_attn_conv_b': _L0_attn_in['conv_b'], 'L0_ffn_gate_w': _L0_ffn_in['gate_w'], 'L0_ffn_w1': _L0_ffn_in['w1'], 'L0_ffn_w3': _L0_ffn_in['w3'], 'L0_ffn_w2': _L0_ffn_in['w2'], 'L1_attn_W_qkv': _L1_attn_in['W_qkv'], 'L1_attn_ln_gamma': _L1_attn_in['ln_gamma'], 'L1_attn_ln_beta': _L1_attn_in['ln_beta'], 'L1_attn_W_proj': _L1_attn_in['W_proj'], 'L1_attn_b_proj': _L1_attn_in['b_proj'], 'L1_ffn_gate_w': _L1_ffn_in['gate_w'], 'L1_ffn_w_gate': _L1_ffn_in['w_gate'], 'L1_ffn_w_up': _L1_ffn_in['w_up'], 'L1_ffn_w_down': _L1_ffn_in['w_down'], 'L1_ffn_ws_gate': _L1_ffn_in['ws_gate'], 'L1_ffn_ws_up': _L1_ffn_in['ws_up'], 'L1_ffn_ws_down': _L1_ffn_in['ws_down'], 'L2_attn_W_qkva': _L2_attn_in['W_qkva'], 'L2_attn_gamma': _L2_attn_in['gamma'], 'L2_ffn_Wg': _L2_ffn_in['Wg'], 'L2_ffn_bg': _L2_ffn_in['bg'], 'L2_ffn_W1': _L2_ffn_in['W1'], 'L2_ffn_b1': _L2_ffn_in['b1'], 'L2_ffn_W2': _L2_ffn_in['W2'], 'L2_ffn_b2': _L2_ffn_in['b2'], 'L3_attn_proj_mat': _L3_attn_in['proj_mat'], 'L3_attn_wq': _L3_attn_in['wq'], 'L3_attn_bq': _L3_attn_in['bq'], 'L3_attn_wk': _L3_attn_in['wk'], 'L3_attn_bk': _L3_attn_in['bk'], 'L3_attn_wv': _L3_attn_in['wv'], 'L3_attn_bv': _L3_attn_in['bv'], 'L3_attn_wo': _L3_attn_in['wo'], 'L3_attn_bo': _L3_attn_in['bo'], 'L3_attn_ln1_g': _L3_attn_in['ln1_g'], 'L3_attn_ln1_b': _L3_attn_in['ln1_b'], 'L3_attn_w1': _L3_attn_in['w1'], 'L3_attn_b1': _L3_attn_in['b1'], 'L3_attn_w2': _L3_attn_in['w2'], 'L3_attn_b2': _L3_attn_in['b2'], 'L3_attn_ln2_g': _L3_attn_in['ln2_g'], 'L3_attn_ln2_b': _L3_attn_in['ln2_b'], 'L3_ffn_W1': _L3_ffn_in['W1'], 'L3_ffn_b1': _L3_ffn_in['b1'], 'L3_ffn_W2': _L3_ffn_in['W2'], 'L3_ffn_b2': _L3_ffn_in['b2']}
    _x0 = _d['L0_attn_x']
    _d['L0_attn_x'] = jax.random.normal(jax.random.fold_in(jax.random.key(seed), 1), (1, 2048, 128), dtype=_x0.dtype)
    del _x0
    return _d

def reference(L0_attn_x, L0_attn_decay_logit, L0_attn_W, L0_attn_b, L0_attn_conv_w, L0_attn_conv_b, L0_ffn_gate_w, L0_ffn_w1, L0_ffn_w3, L0_ffn_w2, L1_attn_W_qkv, L1_attn_ln_gamma, L1_attn_ln_beta, L1_attn_W_proj, L1_attn_b_proj, L1_ffn_gate_w, L1_ffn_w_gate, L1_ffn_w_up, L1_ffn_w_down, L1_ffn_ws_gate, L1_ffn_ws_up, L1_ffn_ws_down, L2_attn_W_qkva, L2_attn_gamma, L2_ffn_Wg, L2_ffn_bg, L2_ffn_W1, L2_ffn_b1, L2_ffn_W2, L2_ffn_b2, L3_attn_proj_mat, L3_attn_wq, L3_attn_bq, L3_attn_wk, L3_attn_bk, L3_attn_wv, L3_attn_bv, L3_attn_wo, L3_attn_bo, L3_attn_ln1_g, L3_attn_ln1_b, L3_attn_w1, L3_attn_b1, L3_attn_w2, L3_attn_b2, L3_attn_ln2_g, L3_attn_ln2_b, L3_ffn_W1, L3_ffn_b1, L3_ffn_W2, L3_ffn_b2):

    def _L0_attn_ref(x, decay_logit, W, b, conv_w, conv_b):
        import jax, jax.numpy as jnp
        import numpy as np
        from jax import lax
        D_MODEL = 128
        KERNEL = 5
        PAD = (KERNEL - 1) // 2
        B, T, D = x.shape
        a = jax.nn.sigmoid(decay_logit)

        def step(s, xt):
            s = a * s + (1.0 - a) * xt
            return (s, s)
        s0 = jnp.zeros((B, D), dtype=x.dtype)
        _, S = lax.scan(step, s0, jnp.swapaxes(x, 0, 1))
        y_ret = jnp.einsum('tbd,ed->tbe', S, W) + b
        y_ret = jnp.swapaxes(y_ret, 0, 1)
        xc = jnp.swapaxes(x, 1, 2)
        y_loc = lax.conv_general_dilated(xc, conv_w, window_strides=(1,), padding=[(PAD, PAD)], feature_group_count=D)
        y_loc = y_loc + conv_b[None, :, None]
        y_loc = jnp.swapaxes(y_loc, 1, 2)
        return y_ret + y_loc

    def _L0_ffn_ref(hidden_states, gate_w, w1, w3, w2):
        import jax, jax.numpy as jnp
        import numpy as np
        N_EXPERTS = 16
        TOP_K = 4
        HIDDEN = 128
        INTER = 64
        B, S = (2, 128)
        'DeepseekV3 MoE adapter forward: router -> sparse scores -> expert GLU MLP -> combine.'
        b, s, h = hidden_states.shape
        x = hidden_states.reshape(-1, h)
        logits = jnp.einsum('th,eh->te', x, gate_w)
        probs = jax.nn.softmax(logits, axis=-1)
        topk_w, topk_idx = jax.lax.top_k(probs, TOP_K)
        topk_w = topk_w / jnp.sum(topk_w, axis=-1, keepdims=True)
        one_hot = (topk_idx[..., None] == jnp.arange(N_EXPERTS)).astype(topk_w.dtype)
        scores = jnp.einsum('tk,tke->te', topk_w, one_hot)
        g = jnp.einsum('th,ehi->tei', x, w1)
        u = jnp.einsum('th,ehi->tei', x, w3)
        act = jax.nn.silu(g) * u
        expert_out = jnp.einsum('tei,eih->teh', act, w2)
        out = jnp.einsum('teh,te->th', expert_out, scores)
        return out.reshape(b, s, h)

    def _L1_attn_ref(x, W_qkv, ln_gamma, ln_beta, W_proj, b_proj):
        import jax, jax.numpy as jnp
        import numpy as np
        NUM_HEADS = 16
        D_MODEL = 128
        HEAD_DIM = D_MODEL // NUM_HEADS
        WINDOW = 64
        SCALE = 8.0 / HEAD_DIM
        LN_EPS = 1e-05

        def _layernorm(t, gamma, beta):
            mu = jnp.mean(t, axis=-1, keepdims=True)
            var = jnp.var(t, axis=-1, keepdims=True)
            return (t - mu) * jax.lax.rsqrt(var + LN_EPS) * gamma + beta
        B, N, C = x.shape
        nw = N // WINDOW
        xw = x.reshape(B * nw, WINDOW, C)
        qkv = (xw @ W_qkv).reshape(B * nw, WINDOW, 3, NUM_HEADS, HEAD_DIM)
        q, k, v = (qkv[:, :, 0], qkv[:, :, 1], qkv[:, :, 2])
        q = _layernorm(q, ln_gamma, ln_beta)
        k = _layernorm(k, ln_gamma, ln_beta)
        attn = jnp.einsum('bqhd,bkhd->bhqk', q * SCALE, k)
        attn = jax.nn.softmax(attn, axis=-1)
        out = jnp.einsum('bhqk,bkhd->bqhd', attn, v).reshape(B * nw, WINDOW, C)
        out = out @ W_proj + b_proj
        return out.reshape(B, N, C)

    def _L1_ffn_ref(hidden_states, gate_w, w_gate, w_up, w_down, ws_gate, ws_up, ws_down):
        import jax, jax.numpy as jnp
        import numpy as np
        H = 128
        M = 64
        E = 16
        TOP_K = 2
        SCALE = 2.5
        NORM_TOPK = True
        B, S = (1, 128)

        def _moe(x, gate_w, w_gate, w_up, w_down, ws_gate, ws_up, ws_down):
            T = x.shape[0]
            shared = jax.nn.silu(x @ ws_gate) * (x @ ws_up) @ ws_down
            scores = jax.nn.sigmoid(x.astype(jnp.float32) @ gate_w.T.astype(jnp.float32))
            topk_w, topk_idx = jax.lax.top_k(scores, TOP_K)
            if NORM_TOPK and TOP_K > 1:
                topk_w = topk_w / (topk_w.sum(-1, keepdims=True) + 1e-20)
            topk_w = topk_w * SCALE
            route = jnp.zeros((T, E), topk_w.dtype).at[jnp.arange(T)[:, None], topk_idx].set(topk_w)
            g = jnp.einsum('th,ehm->etm', x, w_gate)
            u = jnp.einsum('th,ehm->etm', x, w_up)
            eo = jnp.einsum('etm,emh->eth', jax.nn.silu(g) * u, w_down)
            routed = jnp.einsum('te,eth->th', route.astype(x.dtype), eo)
            return routed + shared
        b, s, h = hidden_states.shape
        x = hidden_states.reshape(-1, h)
        out = _moe(x, gate_w, w_gate, w_up, w_down, ws_gate, ws_up, ws_down)
        return out.reshape(b, s, h)

    def _L2_attn_ref(x, W_qkva, gamma):
        import jax, jax.numpy as jnp
        import numpy as np
        EPS = 1e-12

        def _rmsnorm(x, gamma):
            d = gamma.shape[0]
            norm = jnp.sqrt(jnp.sum(x * x, axis=-1, keepdims=True))
            xn = x / jnp.maximum(norm, EPS)
            return xn * jnp.sqrt(jnp.asarray(d, x.dtype)) * gamma
        xn = _rmsnorm(x, gamma)
        qkva = jnp.einsum('bnd,ed->bne', xn, W_qkva)
        q, kv, a = jnp.split(qkva, 3, axis=-1)
        a = jax.nn.sigmoid(a)

        def op(c1, c2):
            a_i, kv_i = c1
            a_j, kv_j = c2
            return (a_j * a_i, kv_j + a_j * kv_i)
        _, kv_scan = jax.lax.associative_scan(op, (a, kv), axis=1)
        out = q * kv_scan
        return out

    def _L2_ffn_ref(x, Wg, bg, W1, b1, W2, b2):
        import jax, jax.numpy as jnp
        import numpy as np
        D_MODEL = 128
        NUM_EXPERTS = 8
        TOP_K = 2
        B, S = (4, 256)
        Bb, Ss, D = x.shape
        E = Wg.shape[1]
        xf = x.reshape(-1, D)
        logits = xf @ Wg + bg
        probs = jax.nn.softmax(logits, axis=-1)
        w, idx = jax.lax.top_k(probs, TOP_K)
        w = w / jnp.sum(w, axis=-1, keepdims=True)
        comb = jnp.sum(jax.nn.one_hot(idx, E, dtype=xf.dtype) * w[..., None], axis=1)
        h = jax.nn.relu(jnp.einsum('nd,edh->enh', xf, W1) + b1[:, None, :])
        y = jnp.einsum('enh,ehd->end', h, W2) + b2[:, None, :]
        out = jnp.einsum('end,ne->nd', y, comb)
        return out.reshape(Bb, Ss, D)

    def _L3_attn_ref(x, proj_mat, wq, bq, wk, bk, wv, bv, wo, bo, ln1_g, ln1_b, w1, b1, w2, b2, ln2_g, ln2_b):
        import jax, jax.numpy as jnp
        import numpy as np
        import math
        D_MODEL = 128
        N_HEAD = 16
        D_HEAD = D_MODEL // N_HEAD
        D_KMAP = 128
        D_INNER = 512

        def _layer_norm(x, g, b, eps=1e-05):
            mu = jnp.mean(x, axis=-1, keepdims=True)
            var = jnp.mean(jnp.square(x - mu), axis=-1, keepdims=True)
            return (x - mu) * jax.lax.rsqrt(var + eps) * g + b

        def _fourier_kernel(x, proj_mat):
            p = jnp.einsum('blhd,dm->blhm', x, proj_mat) / math.sqrt(D_HEAD)
            return jnp.concatenate([jnp.cos(p), jnp.sin(p)], axis=-1) / math.sqrt(D_KMAP)
        B, L, _ = x.shape
        x2 = _layer_norm(x, ln1_g, ln1_b)
        q = (x2 @ wq + bq).reshape(B, L, N_HEAD, D_HEAD)
        k = (x2 @ wk + bk).reshape(B, L, N_HEAD, D_HEAD)
        v = (x2 @ wv + bv).reshape(B, L, N_HEAD, D_HEAD)
        qp = _fourier_kernel(q, proj_mat)
        kp = _fourier_kernel(k, proj_mat)
        kv = jnp.einsum('blhm,blhd->bhmd', kp, v)
        attn = jnp.einsum('blhm,bhmd->blhd', qp, kv)
        attn = attn.reshape(B, L, D_MODEL) @ wo + bo
        x = x + attn
        x2 = _layer_norm(x, ln2_g, ln2_b)
        h = jax.nn.relu(x2 @ w1 + b1)
        x = x + (h @ w2 + b2)
        return x

    def _L3_ffn_ref(hidden_states, W1, b1, W2, b2):
        import jax, jax.numpy as jnp
        import numpy as np
        HIDDEN = 128
        INTER = 512
        h = jax.nn.relu(jnp.einsum('bsh,hi->bsi', hidden_states, W1) + b1)
        return jnp.einsum('bsi,ih->bsh', h, W2) + b2
    x = L0_attn_x
    x = x + _L0_attn_ref(_layernorm(x, axis=-1), L0_attn_decay_logit, L0_attn_W, L0_attn_b, L0_attn_conv_w, L0_attn_conv_b)
    x = x + _L0_ffn_ref(_layernorm(x, axis=-1), L0_ffn_gate_w, L0_ffn_w1, L0_ffn_w3, L0_ffn_w2)
    x = x + _L1_attn_ref(_layernorm(x, axis=-1), L1_attn_W_qkv, L1_attn_ln_gamma, L1_attn_ln_beta, L1_attn_W_proj, L1_attn_b_proj)
    x = x + _L1_ffn_ref(_layernorm(x, axis=-1), L1_ffn_gate_w, L1_ffn_w_gate, L1_ffn_w_up, L1_ffn_w_down, L1_ffn_ws_gate, L1_ffn_ws_up, L1_ffn_ws_down)
    x = x + _L2_attn_ref(_layernorm(x, axis=-1), L2_attn_W_qkva, L2_attn_gamma)
    x = x + _L2_ffn_ref(_layernorm(x, axis=-1), L2_ffn_Wg, L2_ffn_bg, L2_ffn_W1, L2_ffn_b1, L2_ffn_W2, L2_ffn_b2)
    x = x + _L3_attn_ref(_layernorm(x, axis=-1), L3_attn_proj_mat, L3_attn_wq, L3_attn_bq, L3_attn_wk, L3_attn_bk, L3_attn_wv, L3_attn_bv, L3_attn_wo, L3_attn_bo, L3_attn_ln1_g, L3_attn_ln1_b, L3_attn_w1, L3_attn_b1, L3_attn_w2, L3_attn_b2, L3_attn_ln2_g, L3_attn_ln2_b)
    x = x + _L3_ffn_ref(_layernorm(x, axis=-1), L3_ffn_W1, L3_ffn_b1, L3_ffn_W2, L3_ffn_b2)
    return x

_drawn_inputs = setup_inputs


def setup_inputs(seed=0):
    import zlib

    import numpy as np

    out = dict(_drawn_inputs(seed))
    spreads = {'L0_attn_decay_logit': (0.0, 0.8),
     'L1_attn_ln_gamma': (1.0, 0.6),
     'L1_attn_ln_beta': (0.0, 0.477),
     'L2_attn_gamma': (1.0, 0.6),
     'L2_ffn_bg': (0.0, 0.1),
     'L2_ffn_b1': (0.0, 0.749),
     'L2_ffn_b2': (0.0, 0.505),
     'L3_attn_bq': (0.0, 0.534),
     'L3_attn_bk': (0.0, 0.652),
     'L3_attn_bv': (0.0, 0.312),
     'L3_attn_bo': (0.0, 0.8),
     'L3_attn_ln1_g': (1.0, 0.2),
     'L3_attn_ln1_b': (0.0, 0.1),
     'L3_attn_b1': (0.0, 0.8),
     'L3_attn_b2': (0.0, 0.8),
     'L3_attn_ln2_g': (1.0, 0.6),
     'L3_attn_ln2_b': (0.0, 0.8)}
    factors = {'L0_ffn_gate_w': 8.0,
     'L0_ffn_w1': 8.0,
     'L0_ffn_w3': 8.0,
     'L0_ffn_w2': 8.0,
     'L1_ffn_gate_w': 8.0,
     'L1_ffn_w_gate': 8.0,
     'L1_ffn_w_up': 8.0,
     'L1_ffn_w_down': 8.0,
     'L1_ffn_ws_gate': 8.0,
     'L1_ffn_ws_up': 8.0,
     'L1_ffn_ws_down': 8.0,
     'L2_attn_W_qkva': 3.885,
     'L3_attn_proj_mat': 8.0,
     'L3_attn_wk': 6.769,
     'L3_attn_w1': 8.0,
     'L3_attn_w2': 8.0,
     'L3_ffn_W1': 4.246,
     'L3_ffn_b1': 8.0,
     'L3_ffn_W2': 3.989,
     'L3_ffn_b2': 44.832}
    for name, (base, spread) in spreads.items():
        noise = np.random.default_rng([zlib.crc32(name.encode()), seed]).standard_normal(out[name].shape)
        drawn = base * np.exp(spread * noise) if base else spread * noise
        out[name] = jnp.asarray(drawn.astype(out[name].dtype))
    for name, factor in factors.items():
        out[name] = (out[name] * factor).astype(out[name].dtype)
    return out
```

```python
from contextlib import ExitStack

import numpy as np

import concourse.bass as bass
from concourse import mybir

F32 = mybir.dt.float32
F32R = mybir.dt.float32r
U32 = mybir.dt.uint32
ALU = mybir.AluOpType
ACT = mybir.ActivationFunctionType
AX = mybir.AxisListType

P = 128
T = 2048
CH = 512
NC = T // CH
TL = CH // P
NH, HD = 16, 8
WIN = 64
TAPS = 5
EPS = 1e-5
ROUND = 1.5 * 2.0 ** 23
PIECE = 512
STAGES = 4

SPLIT = [
    ("gate0", 128), ("w1_0", 1024), ("w3_0", 1024), ("w2_0", 1024),
    ("wv1", 128), ("wproj", 128),
    ("gate1", 128), ("wg1", 1152), ("wu1", 1152), ("wd1", 1152),
    ("wqkva", 384),
    ("gate2", 128), ("w1_2", 2048), ("w2_2", 2048), ("b2_2", 128),
    ("wq3", 128), ("wk3", 128), ("wv3", 128), ("wo3", 128),
    ("w1_3", 512), ("w2_3", 512), ("fw1", 512), ("fw2", 512),
]
EXACT = [("sel16", 1024), ("sel8", 1024)]
RAW = [
    ("ident", 128), ("wt0", 128), ("group_mean", 128), ("wqk1", 256), ("proj", 128), ("iota", 16),
    ("head_of_4", 4), ("decay", 1), ("convw", TAPS), ("b0", 1), ("convb", 1), ("ln_g1", 1),
    ("ln_b1", 1), ("bproj", 1), ("gamma2", 1), ("bg2", 1), ("b1_2", 16), ("bq", 1), ("bk", 1),
    ("bv", 1), ("bo", 1), ("g1_3", 1), ("e1_3", 1), ("g2_3", 1), ("e2_3", 1), ("b1_3", 4),
    ("b2_3", 1), ("fb1", 4), ("fb2", 1),
]
MADE = [("wt0s", 128), ("taps", TAPS * 128), ("wqk1c", 256)]


def places(table, at=0):
    out = {}
    for name, n in table:
        out[name] = (at, n)
        at += n
    return out, at


SPLIT_AT, _end = places([s_ for s_ in SPLIT if s_[0] in (
    "gate0", "wv1", "wproj", "gate1", "wqkva", "gate2", "b2_2", "w2_2")] + MADE)
_region_a, _end_a = places([s_ for s_ in SPLIT if s_[0] in ("w1_0", "w3_0", "w2_0")], _end)
_over_a, _ = places([s_ for s_ in SPLIT if s_[0] in ("w1_2",)], _end)
_region_b, NSPLIT = places([s_ for s_ in SPLIT if s_[0] in ("wg1", "wu1", "wd1")], _end_a)
_over_b, _end_b = places([s_ for s_ in SPLIT if s_[0] in (
    "wq3", "wk3", "wv3", "wo3", "w1_3", "w2_3", "fw1", "fw2")], _end_a)
assert _end_b <= NSPLIT
SPLIT_AT = SPLIT_AT | _region_a | _over_a | _region_b | _over_b
EXACT_AT, NEXACT = places(EXACT)
RAW_AT, NRAW = places(RAW)

GROUPS = [
    ["gate0", "w1_0", "w3_0", "w2_0", "sel16"],
    ["wv1", "wproj", "gate1", "wg1", "wu1", "wd1"],
    ["wqkva", "gate2", "sel8", "b2_2", "w1_2", "w2_2"],
    ["wq3", "wk3", "wv3", "wo3", "w1_3", "w2_3", "fw1", "fw2"],
]


def pieces():
    out, packed = [], {"split": 0, "exact": 0}
    for g, names in enumerate(GROUPS):
        for name in names:
            kind = "exact" if name in EXACT_AT else "split"
            at, n = (EXACT_AT if kind == "exact" else SPLIT_AT)[name]
            for k in range(0, n, PIECE):
                w = min(PIECE, n - k)
                last = out[-1] if out else None
                if last and last[0] == g and last[1] == kind and last[3] + last[5] == at + k and last[5] + w <= PIECE:
                    out[-1] = (g, kind, last[2] + [name], last[3], last[4], last[5] + w)
                else:
                    out.append((g, kind, [name], at + k, packed[kind], w))
                packed[kind] += w
    return out


PIECES = pieces()
READY_AT = {name: i + 1 for i, p in enumerate(PIECES) for name in p[2]}


class Ffn:
    def __init__(self, key, norm, tail, experts, blocks, up, gate, down, func, topk=0, spread=0,
                 spread_every=1, plain_block=None):
        self.key, self.norm, self.tail, self.experts, self.blocks = key, norm, tail, experts, blocks
        self.up, self.gate, self.down, self.func, self.topk = up, gate, down, func, topk
        self.spread, self.spread_every, self.plain_block = spread, spread_every, plain_block


FFN0 = Ffn("ffn0", 1, 1, 16, 8, "w1_0", "w3_0", "w2_0", ACT.Silu, 4, 8)
FFN1 = Ffn("ffn1", 3, 3, 16, 9, "wg1", "wu1", "wd1", ACT.Silu, 2, 8, 1, 8)
FFN2 = Ffn("ffn2", 5, 5, 8, 16, "w1_2", None, "w2_2", ACT.Relu, 2, 8, 2)
FFN3 = Ffn("ffn3", 7, 7, 0, 4, "w1_3", None, "w2_3", ACT.Relu)
FFN4 = Ffn("ffn4", 8, 8, 0, 4, "fw1", None, "fw2", ACT.Relu)
FFNS = [FFN0, FFN1, FFN2, FFN3, FFN4]
_blk = _sp = _rt = _dn = 0
for _f in FFNS:
    _f.block0, _f.spread0, _f.router0 = _blk, _sp, _rt
    _blk += NC * _f.blocks
    _sp += NC * _f.spread
    _rt += NC * (1 if _f.experts else 0)
    _f.dense = not _f.experts
    _f.down0 = _dn
    _dn += NC * (_f.blocks - (0 if _f.experts == 8 else 1))
ROUTED = {f.norm: f for f in FFNS if f.experts}
LAST_NORM = 8


def build(nc, x_in, w_split, w_exact, w_raw, out):
    with ExitStack() as ctx:
        def sb(name, shape, dt=F32):
            return ctx.enter_context(nc.sbuf_tensor(name, shape, dt))

        def bank(name):
            return ctx.enter_context(nc.psum_tensor(name, [P, CH], F32))

        def sem(name):
            return ctx.enter_context(nc.semaphore(name))

        X = sb("X", [P, NC * TL, P])
        Z = sb("Z", [P, NC * TL, P])
        PAD = TAPS // 2
        XH = sb("XH", [P, T + 2 * PAD], F32R)
        XL = sb("XL", [P, T + 2 * PAD], F32R)
        WH = sb("WH", [P, NSPLIT], F32R)
        WL = sb("WL", [P, NSPLIT], F32R)
        WE = sb("WE", [P, NEXACT], F32R)
        WR = sb("WR", [P, NRAW])
        STG = sb("STG", [P, STAGES, PIECE])
        XN = sb("XN", [P, TL, P])
        X32 = sb("X32", [P, CH])
        YT = sb("YT", [P, CH])
        SCT = sb("SCT", [2 * NH, 2 * CH], F32R)
        QTF = sb("QTF", [P, T])
        S0 = QTF
        B = sb("B", [P, 12, CH])
        buf = [B[:, i, :] for i in range(12)]
        rbuf = [sb(f"rbuf{i}", [P, CH], F32R) for i in range(4)]
        VB = sb("VB", [P, TL, NH // 2, 2, 2, HD + 1])
        KVS = sb("KVS", [P, 2, P])
        WM = sb("WM", [P, 4, P])
        small = sb("small", [P, 1024])
        IDX = sb("IDX", [P, TL, 8], U32)
        VEC = sb("VEC", [P, 32])

        G = [bank("gate_bank0"), bank("gate_bank1")]
        U = [bank("up_bank0"), bank("up_bank1")]
        SP = bank("spread_bank")
        Y = bank("y_bank")
        TN = bank("norm_bank")
        R = bank("route_bank")

        at = 0

        def cut(n):
            nonlocal at
            at += n
            assert at <= 1024
            return small[:, at - n:at]

        stats = cut(TL * 6).rearrange("p (a b) -> p a b", a=TL)
        mv = cut(TL * 2).rearrange("p (a b) -> p a b", a=TL)
        ve = cut(TL)
        rs = cut(TL)
        rr = cut(TL)
        ss = cut(TL)
        rmax = cut(TL)
        top = cut(TL * 8).rearrange("p (a b) -> p a b", a=TL)
        idxf = cut(TL * 8).rearrange("p (a b) -> p a b", a=TL)
        den = cut(TL)
        rec = cut(TL)
        RE = cut(TL * NH)
        RM = cut(TL * NH)
        RS_ = cut(TL * NH)
        EQ = cut(TL * NH * 4)
        SC2 = cut(TL * NH * 2)
        amax = cut(16)
        orec = cut(NH)
        wmean = cut(32)
        sq_scratch = cut(P)
        mhalf = VEC[:, 0:1]
        a_dec, one_minus_a, bias0 = VEC[:, 1:2], VEC[:, 2:3], VEC[:, 3:4]
        gm = [VEC[:, 4 + j:5 + j] for j in range(4)]
        bm = [VEC[:, 8 + j:9 + j] for j in range(4)]
        gam2 = VEC[:, 12:13]
        half_pi = VEC[:, 13:14]
        carry = VEC[:, 14:15]
        epsv = VEC[:, 15:16]
        zero = VEC[:, 16:17]

        def raw(name, a=0, n=None):
            o, w = RAW_AT[name]
            return WR[:, o + a:o + a + (w - a if n is None else n)]

        ident = raw("ident")

        x_loaded = [sem(f"x_loaded{c}") for c in range(NC)]
        raw_loaded = sem("raw_loaded")
        piece_loaded = [sem(f"piece_loaded{k}") for k in range(STAGES)]
        piece_ready = sem("piece_ready")
        consts_ready = sem("consts_ready")
        decay_ready = sem("decay_ready")
        made_ready = sem("made_ready")
        pads_ready = sem("pads_ready")
        out_stored = sem("out_stored")
        dve_chain = sem("dve_chain")
        act_chain = sem("act_chain")
        pool_chain = sem("pool_chain")
        stats_ready = sem("stats_ready")
        rstd_ready = sem("rstd_ready")
        xn_ready = sem("xn_ready")
        norm_turned = sem("norm_turned")
        x32_ready = sem("x32_ready")
        xh_ready = sem("xh_ready")
        xl_ready = sem("xl_ready")
        sumsq_ready = sem("sumsq_ready")
        scale2_ready = sem("scale2_ready")
        token_squares = sem("token_squares")
        logits_t = sem("logits_t")
        logits_sb = sem("logits_sb")
        logits_tok = sem("logits_tok")
        shifted = sem("shifted")
        scored = sem("scored")
        weights_tok = sem("weights_tok")
        weights_t = sem("weights_t")
        weights_sb = sem("weights_sb")
        y_full = sem("y_full")
        yt_ready = sem("yt_ready")
        yt_turned = sem("yt_turned")
        res_done = sem("res_done")
        first_full = sem("first_full")
        second_full = sem("second_full")
        mul_done = sem("mul_done")
        spread_full = sem("spread_full")
        act_done = sem("act_done")
        h_ready = sem("h_ready")
        hh_ready = sem("hh_ready")
        hl_ready = sem("hl_ready")
        down_done = sem("down_done")
        s_ready = sem("s_ready")
        s_high = sem("s_high")
        s_low = sem("s_low")
        qkv_full = sem("qkv_full")
        squares = sem("squares")
        v_copied = sem("v_copied")
        v_turned = sem("v_turned")
        v_placed = sem("v_placed")
        var_full = sem("var_full")
        var_read = sem("var_read")
        rstd_qk = sem("rstd_qk")
        qk_read = sem("qk_read")
        qk_ready = sem("qk_ready")
        s_full = sem("scores_full")
        s_read = sem("scores_read")
        p_ready = sem("probs_ready")
        p_turned = sem("probs_turned")
        pt_ready = sem("probs_t_ready")
        o_full = sem("o_full")
        o_read = sem("o_read")
        a_turned = sem("a_turned")
        a32_ready = sem("a32_ready")
        ah_ready = sem("ah_ready")
        al_ready = sem("al_ready")
        scan_in = sem("scan_in")
        sig_ready = sem("sig_ready")
        lin_full = sem("lin_full")
        lin_sb = sem("lin_sb")
        vt_turned = sem("vt_turned")
        v4_ready = sem("v4_ready")
        t_full = sem("phase_full")
        m_ready = sem("rounded_ready")
        r_ready = sem("rest_ready")
        ab_ready = sem("abs_ready")
        trig_ready = sem("trig_ready")
        unit_used = sem("unit_used")
        kv_full = sem("kv_full")
        kv_ready = sem("kv_ready")
        qts_ready = sem("qts_ready")
        oq_full = sem("oq_full")
        oq_read = sem("oq_read")

        class Chain:

            def __init__(self, eng, s):
                self.eng, self.s, self.n = eng, s, 0

            def __call__(self, ins):
                self.n += 1
                ins.then_inc(self.s, 1)
                self.eng.wait_ge(self.s, self.n)

        def chunk(ap2, c, pad=0):
            return ap2[:, bass.ds(c * CH + pad, CH)]

        def tiles(a3, c):
            return a3[:, bass.ds(c * TL, TL), :]

        def bcast(ap, shape):
            return ap.broadcast_to(shape)

        def count(stage, c):
            return NC * stage + c

        def wh(name, a=0, n=P):
            o = SPLIT_AT[name][0] + a
            return WH[:, o:o + n], WL[:, o:o + n]

        def front_source(n):
            return Z if n == 7 else X

        def front_dve(v, chain, n, c, pos):
            m = count(n, c)
            src = front_source(n)

            def read_stats(t3, first):
                for j in range(TL):
                    i = nc.vector.bn_stats(stats[:, j, :], t3(j))
                chain(i)
                for j in range(TL):
                    i = nc.vector.bn_aggr(mv[:, j, :], stats[:, j, :])
                i.then_inc(stats_ready, 1)

            sbase = m + max(0, m - count(6, 0)) if n <= 6 else m + NC
            if pos == 0:
                if n == 0:
                    v.wait_ge(x_loaded[c], 16)
                else:
                    v.wait_ge(res_done, count(n - 1, c) + 1)
                read_stats(lambda j: src[:, c * TL + j, :], True)
            if pos == 1:
                v.wait_ge(rstd_ready, sbase + 1)
                if m:
                    v.wait_ge(norm_turned, m)
                dst = (lambda j: Z[:, c * TL + j, :]) if n == 6 else (lambda j: XN[:, j, :])
                for j in range(TL):
                    i = nc.vector.tensor_scalar(dst(j), src[:, c * TL + j, :], mv[:, j, 0:1],
                                                rs[:, j:j + 1], ALU.subtract, ALU.mult)
                if n == 6:
                    chain(i)
                    read_stats(lambda j: Z[:, c * TL + j, :], False)
                    v.wait_ge(rstd_ready, sbase + 2)
                    for j in range(TL):
                        i = nc.vector.tensor_scalar(XN[:, j, :], Z[:, c * TL + j, :], mv[:, j, 0:1],
                                                    rs[:, j:j + 1], ALU.subtract, ALU.mult)
                    i.then_inc(xn_ready, 1)
                elif n == 4:
                    i.then_inc(sumsq_ready, 1)
                    v.wait_ge(scale2_ready, c + 1)
                    for j in range(TL):
                        i = nc.vector.tensor_scalar(XN[:, j, :], XN[:, j, :], rr[:, j:j + 1], None, ALU.mult)
                    i.then_inc(xn_ready, 1)
                else:
                    i.then_inc(xn_ready, 1)
            if pos == 3:
                v.wait_ge(x32_ready, m + 1)
                nc.vector.tensor_copy(chunk(XH, c, PAD), X32[:, :]).then_inc(xh_ready, 1)
                v.wait_ge(xh_ready, m + 1)
                nc.vector.tensor_tensor(chunk(XL, c, PAD), X32[:, :], chunk(XH, c, PAD).bitcast(F32),
                                        ALU.subtract).then_inc(xl_ready, 1)
            f = ROUTED.get(n)
            if not f:
                return
            E, K = f.experts, f.topk
            r = f.router0 + c
            Rv = R[:, 0:TL * E].rearrange("p (t e) -> p t e", t=TL)
            re = RE[:, 0:TL * E].rearrange("p (t e) -> p t e", t=TL)
            rm = RM[:, 0:TL * E].rearrange("p (t e) -> p t e", t=TL)
            rw = RS_[:, 0:TL * E].rearrange("p (t e) -> p t e", t=TL)
            eq = EQ[:, 0:TL * E * K].rearrange("p (t e k) -> p t e k", t=TL, k=K)
            sc2 = SC2[:, 0:TL * E * 2].rearrange("p (t s e) -> p t s e", t=TL, s=2)
            if pos == 5 and n != 3:
                v.wait_ge(logits_tok, r + 1)
                chain(nc.vector.tensor_reduce(rmax[:, :], Rv, AX.X, ALU.max))
                nc.vector.tensor_tensor(re, Rv, bcast(rmax[:, :].unsqueeze(2), [P, TL, E]),
                                        ALU.subtract).then_inc(shifted, 1)
            if pos == 6:
                v.wait_ge(scored, r + 1)
                for j in range(TL):
                    i = nc.vector.max(top[:, j, :], re[:, j, :])
                chain(i)
                for j in range(TL):
                    i = nc.vector.max_index(IDX[:, j, :], top[:, j, :], re[:, j, :])
                chain(i)
                chain(nc.vector.tensor_copy(idxf, IDX[:, :, :]))
                for j in range(TL):
                    i = nc.vector.tensor_tensor(
                        eq[:, j, :, :], bcast(raw("iota", 0, E).unsqueeze(2), [P, E, K]),
                        bcast(idxf[:, j, 0:K].unsqueeze(1), [P, E, K]), ALU.is_equal)
                chain(i)
                chain(nc.vector.tensor_reduce(RM[:, 0:TL * E], EQ[:, 0:TL * E * K].rearrange(
                    "p (a k) -> p a k", k=K), AX.X, ALU.add))
                chain(nc.vector.tensor_reduce(den[:, :], top[:, :, 0:K], AX.X, ALU.add))
                if n == 3:
                    chain(nc.vector.tensor_scalar(den[:, :], den[:, :], 1e-20, None, ALU.add))
                chain(nc.vector.reciprocal(rec[:, :], den[:, :]))
                if n == 3:
                    chain(nc.vector.tensor_scalar(rec[:, :], rec[:, :], 2.5, None, ALU.mult))
                chain(nc.vector.tensor_tensor(rw, re, rm, ALU.mult))
                chain(nc.vector.tensor_tensor(rw, rw, bcast(rec[:, :].unsqueeze(2), [P, TL, E]), ALU.mult))
                chain(nc.vector.tensor_copy(sc2[:, :, 0, :].bitcast(F32R), rw))
                nc.vector.tensor_tensor(sc2[:, :, 1, :], rw, sc2[:, :, 0, :], ALU.subtract)\
                    .then_inc(weights_tok, 1)

        def front_pool(g, chain, n, c, pos):
            m = count(n, c)
            sbase = m + max(0, m - count(6, 0)) if n <= 6 else m + NC
            if pos == 0:
                for k in range(2 if n == 6 else 1):
                    g.wait_ge(stats_ready, sbase + k + 1)
                    chain(nc.gpsimd.tensor_scalar(ve[:, :], mv[:, :, 1], 1.0, EPS, ALU.mult, ALU.add))
                    nc.gpsimd.tensor_tensor(rs[:, :], ve[:, :], bcast(mhalf, [P, TL]), ALU.pow)\
                        .then_inc(rstd_ready, 1)
                if n == 4:
                    g.wait_ge(token_squares, c + 1)
                    chain(nc.gpsimd.tensor_scalar(ve[:, :], ss[:, :], 1e-24, None, ALU.max))
                    nc.gpsimd.tensor_tensor(rr[:, :], ve[:, :], bcast(mhalf, [P, TL]), ALU.pow)\
                        .then_inc(scale2_ready, 1)

        def front_act(a, chain, n, c, pos):
            m = count(n, c)
            if pos == 1 and n == 4:
                a.wait_ge(sumsq_ready, c + 1)
                for j in range(TL):
                    i = nc.scalar.activation(sq_scratch, XN[:, j, :], ACT.Square, accum_out=ss[:, j:j + 1])
                    if j < TL - 1:
                        chain(i)
                i.then_inc(token_squares, 1)
            if pos == 2:
                a.wait_ge(norm_turned, m + 1)
                if m:
                    a.wait_ge(xl_ready, m)
                if n == 4:
                    nc.scalar.activation(X32[:, :], TN[:, :], ACT.Copy, scale=gam2).then_inc(x32_ready, 1)
                elif n in (6, 7):
                    g_, b_ = ("g1_3", "e1_3") if n == 6 else ("g2_3", "e2_3")
                    nc.scalar.activation(X32[:, :], TN[:, :], ACT.Identity, scale=raw(g_), bias=raw(b_))\
                        .then_inc(x32_ready, 1)
                else:
                    nc.scalar.activation(X32[:, :], TN[:, :], ACT.Copy).then_inc(x32_ready, 1)
            f = ROUTED.get(n)
            if not f:
                return
            E = f.experts
            r = f.router0 + c
            if pos == 4:
                a.wait_ge(logits_t, r + 1)
                bias = raw("bg2")[0:E, :] if n == 5 else zero[0:E, :]
                nc.scalar.activation(YL[0:E, :], R[0:E, :], ACT.Identity, bias=bias).then_inc(logits_sb, 1)
            if pos == 6:
                Rv = R[:, 0:TL * E].rearrange("p (t e) -> p t e", t=TL)
                re = RE[:, 0:TL * E].rearrange("p (t e) -> p t e", t=TL)
                if n == 3:
                    a.wait_ge(logits_tok, r + 1)
                    nc.scalar.activation(re, Rv, ACT.Sigmoid).then_inc(scored, 1)
                else:
                    a.wait_ge(shifted, shift_count(n, c) + 1)
                    nc.scalar.activation(re, re, ACT.Exp).then_inc(scored, 1)
            if pos == 7:
                a.wait_ge(weights_t, r + 1)
                nc.scalar.activation(SCT[0:2 * E, bass.ds(c % 2 * CH, CH)], R[0:2 * E, :], ACT.Copy)\
                    .then_inc(weights_sb, 1)

        YL = sb("YL", [NH, CH])

        def shift_count(n, c):
            return {1: 0, 5: NC}[n] + c

        def front_pe(pe, n, c, pos):
            m = count(n, c)
            if pos == 2:
                pe.wait_ge(xn_ready, m + 1)
                if m:
                    pe.wait_ge(x32_ready, m)
                for j in range(TL):
                    i = nc.tensor.transpose(TN[:, j * P:(j + 1) * P], XN[:, j, :], ident)
                i.then_inc(norm_turned, 1)
            f = ROUTED.get(n)
            if not f:
                return
            E = f.experts
            r = f.router0 + c
            if pos == 4:
                pe.wait_ge(xl_ready, m + 1)
                pe.wait_ge(piece_ready, READY_AT[f"gate{(n - 1) // 2}"])
                if r:
                    pe.wait_ge(weights_sb, r)
                mm3(R[:, :], wh(f"gate{(n - 1) // 2}"), (chunk(XH, c, PAD), chunk(XL, c, PAD)), True, True)\
                    .then_inc(logits_t, 1)
            if pos == 5:
                pe.wait_ge(logits_sb, r + 1)
                for j in range(TL):
                    i = nc.tensor.transpose(R[:, j * E:(j + 1) * E], YL[0:E, j * P:(j + 1) * P],
                                            ident[0:E, 0:E])
                i.then_inc(logits_tok, 1)
            if pos == 7:
                pe.wait_ge(weights_tok, r + 1)
                for j in range(TL):
                    i = nc.tensor.transpose(R[0:2 * E, j * P:(j + 1) * P],
                                            SC2[:, j * 2 * E:(j + 1) * 2 * E], ident)
                i.then_inc(weights_t, 1)

        def mm3(dst, w, x, start, stop):
            nc.tensor.matmul(dst, w[0], x[0], start=start, stop=False)
            nc.tensor.matmul(dst, w[0], x[1], start=False, stop=False)
            return nc.tensor.matmul(dst, w[1], x[0], start=False, stop=stop)

        def tail_pe(pe, t, c):
            n = count(t, c)
            pe.wait_ge(yt_ready, n + 1)
            for j in range(TL):
                i = nc.tensor.transpose(Y[:, j * P:(j + 1) * P], YT[:, j * P:(j + 1) * P], ident)
            i.then_inc(yt_turned, 1)

        def tail_dve(v, chain, t, c):
            n = count(t, c)
            v.wait_ge(yt_turned, n + 1)
            Yv = Y[:, :].rearrange("p (t d) -> p t d", t=TL)
            if t == 6:
                nc.vector.tensor_tensor(tiles(Z, c), tiles(Z, c), Yv, ALU.add).then_inc(res_done, 1)
            elif t == 7:
                chain(nc.vector.tensor_tensor(tiles(Z, c), tiles(Z, c), Yv, ALU.add))
                nc.vector.tensor_tensor(tiles(X, c), tiles(X, c), tiles(Z, c), ALU.add).then_inc(res_done, 1)
            else:
                nc.vector.tensor_tensor(tiles(X, c), tiles(X, c), Yv, ALU.add).then_inc(res_done, 1)

        def y_bank_free(pe, t, c):
            if count(t, c):
                pe.wait_ge(res_done, count(t, c))

        def yt_free(eng, t, c):
            if count(t, c):
                eng.wait_ge(yt_turned, count(t, c))

        def block_no(f, c, b):
            return f.block0 + f.blocks * c + b

        def before(f, c, b):
            return block_no(f, c, b) - (1 if b else 0)

        def body_start(eng, t, c):
            if count(t, c):
                eng.wait_ge(yt_ready, count(t, c))

        def count_y(t, c):
            return count(t, c) - (NC if t > 4 else 0)

        def hooks(f, b, hook):
            if b == 1:
                hook(-1)
            for pos in range(b * 8 // f.blocks, (b + 1) * 8 // f.blocks):
                hook(pos)

        def ffn_pe(pe, f, c, hook):
            xs = (chunk(XH, c, PAD), chunk(XL, c, PAD))
            if c == 0:
                body_start(pe, f.tail, 0)
                for name in [f.up, f.gate, f.down]:
                    if name:
                        pe.wait_ge(piece_ready, READY_AT[name])
                if f.experts:
                    pe.wait_ge(piece_ready, READY_AT["sel16" if f.experts == 16 else "sel8"])
                if f.experts == 8:
                    pe.wait_ge(piece_ready, READY_AT["b2_2"])
            pe.wait_ge(xl_ready, count(f.norm, c) + 1)
            if f.experts:
                pe.wait_ge(weights_sb, f.router0 + c + 1)

            def up(b):
                e = b % 2
                if before(f, c, b) > 0:
                    pe.wait_ge(act_done, before(f, c, b))
                mm3(G[e][:, :], wh(f.up, b * P), xs, True, True).then_inc(first_full, 1)
                if f.gate:
                    if before(f, c, b) > 0:
                        pe.wait_ge(mul_done, before(f, c, b))
                    mm3(U[e][:, :], wh(f.gate, b * P), xs, True, True).then_inc(second_full, 1)

            def spread(b):
                if f.dense or b == f.plain_block or b % f.spread_every:
                    return
                if block_no(f, c, b):
                    pe.wait_ge(h_ready, block_no(f, c, b))
                E = f.experts
                o = EXACT_AT["sel16" if E == 16 else "sel8"][0] + b // f.spread_every * P
                nc.tensor.matmul(SP[:, :], WE[0:2 * E, o:o + P], SCT[0:2 * E, bass.ds(c % 2 * CH, CH)],
                                 start=True, stop=True).then_inc(spread_full, 1)

            def down(b):
                if b == 0:
                    y_bank_free(pe, f.tail, c)
                pe.wait_ge(hl_ready, block_no(f, c, b) + 1)
                last = b == f.blocks - 1
                bias = f.experts == 8
                mm3(Y[:, :], wh(f.down, b * P), (rbuf[b % 2][:, :], rbuf[2 + b % 2][:, :]),
                    b == 0, last and not bias).then_inc(*((y_full, 1) if last and not bias else (down_done, 1)))
                if last and bias:
                    s = SCT[0:2 * f.experts, bass.ds(c % 2 * CH, CH)]
                    bh, bl = wh("b2_2")
                    nc.tensor.matmul(Y[:, :], bh[0:2 * f.experts, :], s, start=False, stop=False)
                    nc.tensor.matmul(Y[:, :], bl[0:2 * f.experts, :], s, start=False, stop=True)\
                        .then_inc(y_full, 1)

            for b in range(f.blocks):
                up(b)
                if b >= 2:
                    down(b - 2)
                spread(b)
                hooks(f, b, hook)
            down(f.blocks - 2)
            down(f.blocks - 1)

        def downs(f, c, b):
            per = f.blocks - (0 if f.experts == 8 else 1)
            return f.down0 + per * c + b

        def rows_used(eng, f, c, b):
            if b >= 2:
                eng.wait_ge(down_done, downs(f, c, b - 1))
            elif count_y(f.tail, c):
                eng.wait_ge(y_full, count_y(f.tail, c))

        def ffn_act(a, chain, f, c, hook):
            if c == 0:
                body_start(a, f.tail, 0)

            def first(b):
                e = b % 2
                a.wait_ge(first_full, block_no(f, c, b) + 1)
                if f.dense:
                    if before(f, c, b) > 0:
                        a.wait_ge(hl_ready, before(f, c, b))
                    nc.scalar.activation(buf[2 + e][:, :], G[e][:, :], ACT.Relu,
                                         bias=raw("b1_3" if f is FFN3 else "fb1", b, 1)).then_inc(act_done, 1)
                    return
                if before(f, c, b) > 0:
                    a.wait_ge(h_ready, before(f, c, b))
                if f.gate:
                    nc.scalar.activation(buf[e][:, :], G[e][:, :], ACT.Silu).then_inc(act_done, 1)
                else:
                    nc.scalar.activation(buf[e][:, :], G[e][:, :], ACT.Relu, bias=raw("b1_2", b, 1))\
                        .then_inc(act_done, 1)

            def high(b):
                if f.dense:
                    return
                a.wait_ge(h_ready, block_no(f, c, b) + 1)
                rows_used(a, f, c, b)
                nc.scalar.activation(rbuf[b % 2][:, :], buf[2 + b % 2][:, :], ACT.Copy).then_inc(hh_ready, 1)

            for b in range(f.blocks):
                first(b)
                if b:
                    high(b - 1)
                hooks(f, b, hook)
            high(f.blocks - 1)
            yt_free(a, f.tail, c)
            a.wait_ge(y_full, count_y(f.tail, c) + 1)
            bias = {"ffn3": raw("b2_3"), "ffn4": raw("fb2")}.get(f.key, zero)
            nc.scalar.activation(YT[:, :], Y[:, :], ACT.Identity, bias=bias).then_inc(yt_ready, 1)

        def ffn_dve(v, chain, f, c, hook):
            if c == 0:
                body_start(v, f.tail, 0)
            for b in range(f.blocks):
                e = b % 2
                n = block_no(f, c, b)
                v.wait_ge(act_done, n + 1)
                if not f.dense:
                    src = buf[e]
                    if f.gate:
                        v.wait_ge(second_full, n + 1)
                        nc.vector.tensor_tensor(buf[4 + e][:, :], buf[e][:, :], U[e][:, :], ALU.mult)\
                            .then_inc(mul_done, 1)
                        v.wait_ge(mul_done, n + 1)
                        src = buf[4 + e]
                    if before(f, c, b) > 0:
                        v.wait_ge(hl_ready, before(f, c, b))
                    if b == f.plain_block:
                        nc.vector.tensor_copy(buf[2 + e][:, :], src[:, :]).then_inc(h_ready, 1)
                    else:
                        v.wait_ge(spread_full, f.spread0 + f.spread * c + b // f.spread_every + 1)
                        nc.vector.tensor_tensor(buf[2 + e][:, :], src[:, :], SP[:, :], ALU.mult)\
                            .then_inc(h_ready, 1)
                else:
                    rows_used(v, f, c, b)
                    nc.vector.tensor_copy(rbuf[e][:, :], buf[2 + e][:, :]).then_inc(hh_ready, 1)
                if not f.gate:
                    if b and not f.dense:
                        low(nc.vector, v, f, c, b - 1)
                    if f.dense:
                        low(nc.vector, v, f, c, b)
                hooks(f, b, hook)
            if f is FFN2:
                low(nc.vector, v, f, c, f.blocks - 1)

        def low(e_, eng, f, c, b):
            eng.wait_ge(hh_ready, block_no(f, c, b) + 1)
            e = b % 2
            e_.tensor_tensor(rbuf[2 + e][:, :], buf[2 + e][:, :], rbuf[e][:, :].bitcast(F32),
                             ALU.subtract).then_inc(hl_ready, 1)

        def ffn_pool(g, chain, f, c, hook, work):
            for b in range(f.blocks):
                if f.gate:
                    low(nc.gpsimd, g, f, c, b)
                    work()
                hooks(f, b, hook)


        def stage0_pe(pe, c, hook):
            if c == 0:
                pe.wait_ge(made_ready, 1)
                pe.wait_ge(xl_ready, NC)
            y_bank_free(pe, 0, c)
            for k in range(TAPS):
                mm3(Y[:, :], wh("taps", k * P), (chunk(XH, c, k), chunk(XL, c, k)), k == 0, False)
            pe.wait_ge(s_low, c + 1)
            mm3(Y[:, :], wh("wt0s"), (rbuf[0][:, :], rbuf[1][:, :]), False, True).then_inc(y_full, 1)

        def stage0_act(a, chain, c, hook):
            yt_free(a, 0, c)
            a.wait_ge(y_full, c + 1)
            nc.scalar.activation(YT[:, :], Y[:, :], ACT.Identity, bias=bias0).then_inc(yt_ready, 1)

        def stage0_dve(v, chain, c, hook):
            if c:
                v.wait_ge(y_full, c)
            nc.vector.tensor_copy(rbuf[0][:, :], chunk(S0, c)).then_inc(s_high, 1)
            v.wait_ge(s_high, c + 1)
            nc.vector.tensor_tensor(rbuf[1][:, :], chunk(S0, c), rbuf[0][:, :].bitcast(F32), ALU.subtract)\
                .then_inc(s_low, 1)

        UN = 2 * TL
        rows_done = sem("rows_done")
        sqq, sqk, veq, vek, rq, rk, qn, kn, QN = (buf[i] for i in (0, 1, 2, 3, 4, 5, 0, 1, 2))
        KM = [buf[6 + j] for j in range(4)]
        VTD = B[:, 10:12, :].rearrange("p a b -> p (a b)").rearrange("p (w s t) -> p w s t", s=2, t=WIN)
        PRB = [buf[0], buf[1]]
        PT = [buf[3], buf[4]]
        AT = buf[5]
        HU = NH // 2

        def attn_pe(pe, c, hook):
            t = 2
            body_start(pe, t, c)
            xs = (chunk(XH, c, PAD), chunk(XL, c, PAD))
            if c == 0:
                pe.wait_ge(made_ready, 1)
                pe.wait_ge(piece_ready, READY_AT["wv1"])
            pe.wait_ge(xl_ready, count(2, c) + 1)
            mm3(G[0][:, :], wh("wqk1c", 0), xs, True, True).then_inc(qkv_full, 1)
            mm3(G[1][:, :], wh("wqk1c", P), xs, True, True).then_inc(qkv_full, 1)
            mm3(U[0][:, :], wh("wv1"), xs, True, True).then_inc(qkv_full, 1)
            pe.wait_ge(squares, 2 * c + 1)
            nc.tensor.matmul(U[1][:, :], raw("group_mean"), sqq, start=True, stop=True).then_inc(var_full, 1)
            pe.wait_ge(squares, 2 * c + 2)
            nc.tensor.matmul(SP[:, :], raw("group_mean"), sqk, start=True, stop=True).then_inc(var_full, 1)
            pe.wait_ge(v_copied, c + 1)
            pe.wait_ge(var_read, 2 * c + 1)
            for w in range(CH // WIN):
                i = nc.tensor.transpose(U[w // 4][:, w % 4 * P:(w % 4 + 1) * P],
                                        VTD[:, w, :, :].rearrange("p s t -> p (s t)"), ident)
            i.then_inc(v_turned, 1)

            def scores(n):
                i_, u = n // 2, n % 2
                if n == 0:
                    pe.wait_ge(qk_ready, c + 1)
                if n >= 2:
                    pe.wait_ge(s_read, c * UN + n - 1)
                for hl in range(HU):
                    h = HU * u + hl
                    g_, j = h // 4, h % 4
                    if hl == 4:
                        i.then_inc(rows_done, 1)
                        pe.wait_ge(rows_done, c * UN + n + 1)
                    for w in range(2):
                        tok = slice(i_ * P + w * WIN, i_ * P + (w + 1) * WIN)
                        i = nc.tensor.matmul(G[u][w * WIN:(w + 1) * WIN, hl * WIN:(hl + 1) * WIN],
                                             QN[32 * g_:32 * g_ + 32, tok], KM[j][32 * g_:32 * g_ + 32, tok],
                                             start=True, stop=True)
                i.then_inc(s_full, 1)

            def turn(n):
                u = n % 2
                pe.wait_ge(p_ready, c * UN + n + 1)
                if n == 0:
                    pe.wait_ge(v_placed, c + 1)
                if n >= 2:
                    pe.wait_ge(pt_ready, c * UN + n - 1)
                for q in range(4):
                    i = nc.tensor.transpose(U[u][:, q * P:(q + 1) * P], PRB[u][:, q * P:(q + 1) * P], ident)
                i.then_inc(p_turned, 1)

            def weigh(n):
                i_, u = n // 2, n % 2
                pe.wait_ge(pt_ready, c * UN + n + 1)
                if u == 0 and i_:
                    pe.wait_ge(o_read, c * TL + i_)
                for q in range(4):
                    pr = 4 * u + q
                    i = nc.tensor.matmul(SP[:, pr * 36:(pr + 1) * 36], PT[u][:, q * P:(q + 1) * P],
                                         VB[:, i_, pr, :, :, :].rearrange("p a b d -> p (a b d)"),
                                         start=True, stop=True)
                i.then_inc(o_full, 1)

            scores(0)
            for n in range(UN):
                if n + 1 < UN:
                    scores(n + 1)
                turn(n)
                if n:
                    weigh(n - 1)
                if n == 1:
                    hook(-1)
                hook(n)
            weigh(UN - 1)
            project_pe(pe, t, c, 0, o_read, (c + 1) * TL, "wproj", c * UN + UN)

        def project_pe(pe, t, c, k0, ready, value, w, scores_read):
            pe.wait_ge(ready, value)
            if scores_read:
                pe.wait_ge(s_read, scores_read)
            for j in range(TL):
                i = nc.tensor.transpose(G[0][:, j * P:(j + 1) * P], AT[:, j * P:(j + 1) * P], ident)
            i.then_inc(a_turned, 1)
            pe.wait_ge(piece_ready, READY_AT[w])
            y_bank_free(pe, t, c)
            pe.wait_ge(al_ready, k0 + c + 1)
            mm3(Y[:, :], wh(w), (rbuf[0][:, :], rbuf[1][:, :]), True, True).then_inc(y_full, 1)

        def project_act(a, t, c, k0, bias):
            a.wait_ge(a_turned, k0 + c + 1)
            nc.scalar.activation(buf[11], G[0][:, :], ACT.Copy).then_inc(a32_ready, 1)
            yt_free(a, t, c)
            a.wait_ge(y_full, count_y(t, c) + 1)
            nc.scalar.activation(YT[:, :], Y[:, :], ACT.Identity, bias=bias).then_inc(yt_ready, 1)

        def project_dve(v, t, c, k0):
            v.wait_ge(a32_ready, k0 + c + 1)
            nc.vector.tensor_copy(rbuf[0][:, :], buf[11]).then_inc(ah_ready, 1)
            v.wait_ge(ah_ready, k0 + c + 1)
            nc.vector.tensor_tensor(rbuf[1][:, :], buf[11], rbuf[0][:, :].bitcast(F32), ALU.subtract)\
                .then_inc(al_ready, 1)

        def attn_act(a, chain, c, hook):
            body_start(a, 2, c)
            a.wait_ge(qkv_full, 3 * c + 1)
            nc.scalar.activation(sqq, G[0][:, :], ACT.Square).then_inc(squares, 1)
            a.wait_ge(qkv_full, 3 * c + 2)
            nc.scalar.activation(sqk, G[1][:, :], ACT.Square).then_inc(squares, 1)
            a.wait_ge(qkv_full, 3 * c + 3)
            for s_ in range(2):
                i = nc.scalar.activation(VTD[:, :, s_, :], U[0][:, :].rearrange("p (w t) -> p w t", t=WIN), ACT.Copy)
            i.then_inc(v_copied, 1)
            a.wait_ge(var_full, 2 * c + 1)
            nc.scalar.activation(veq, U[1][:, :], ACT.Identity, bias=epsv).then_inc(var_read, 1)
            a.wait_ge(var_full, 2 * c + 2)
            nc.scalar.activation(vek, SP[:, :], ACT.Identity, bias=epsv).then_inc(var_read, 1)
            a.wait_ge(v_turned, c + 1)
            for b_ in range(2):
                src = U[b_][:, :].rearrange("p (i w q h d) -> p i w q h d", i=2, w=2, q=HU, h=2)
                for s_ in range(2):
                    rows = slice(64 * s_, 64 * s_ + 64)
                    for i_ in range(2):
                        for w in range(2):
                            i = nc.scalar.activation(VB[rows, 2 * b_ + i_, :, w, s_, 0:HD],
                                                     src[rows, i_, w, :, s_, :], ACT.Copy)
            i.then_inc(v_placed, 1)

            def probs(n):
                a.wait_ge(sub_done, c * UN + n + 1)
                nc.scalar.activation(PRB[n % 2], PRB[n % 2], ACT.Exp).then_inc(p_ready, 1)

            def evac(n):
                a.wait_ge(p_turned, c * UN + n + 1)
                if n >= 2:
                    a.wait_ge(o_full, c * UN + n - 1)
                nc.scalar.activation(PT[n % 2], U[n % 2][:, :], ACT.Copy).then_inc(pt_ready, 1)

            probs(0)
            for n in range(UN):
                if n + 1 < UN:
                    probs(n + 1)
                evac(n)
                if n == 1:
                    hook(-1)
                hook(n)
            project_act(a, 2, c, 0, raw("bproj"))

        sub_done = s_read

        def attn_dve(v, chain, c, hook):
            body_start(v, 2, c)
            v.wait_ge(rstd_qk, 2 * c + 1)
            nc.vector.tensor_tensor(qn, G[0][:, :], rq, ALU.mult).then_inc(qk_read, 1)
            v.wait_ge(qk_read, 2 * c + 1)
            nc.vector.tensor_scalar(QN, qn, raw("ln_g1"), raw("ln_b1"), ALU.mult, ALU.add)
            v.wait_ge(rstd_qk, 2 * c + 2)
            nc.vector.tensor_tensor(kn, G[1][:, :], rk, ALU.mult).then_inc(qk_read, 1)
            v.wait_ge(qk_read, 2 * c + 2)
            for j in range(4):
                i = nc.vector.tensor_scalar(KM[j], kn, gm[j], bm[j], ALU.mult, ALU.add)
            i.then_inc(qk_ready, 1)
            v.wait_ge(qk_ready, c + 1)

            def finish(i_):
                v.wait_ge(o_full, c * UN + 2 * i_ + 2)
                O = SP[:, 0:HU * 36].rearrange("p (q w h d) -> p q w h d", q=HU, w=2, h=2)
                for w in range(2):
                    rows = slice(64 * w, 64 * w + 64)
                    i = nc.vector.reciprocal(orec[rows, :].rearrange("p (q h) -> p q h", h=2),
                                             O[rows, :, w, :, HD])
                chain(i)
                for w in range(2):
                    rows = slice(64 * w, 64 * w + 64)
                    for h2 in range(2):
                        i = nc.vector.tensor_tensor(
                            AT[rows, i_ * P:(i_ + 1) * P].rearrange("p (q h d) -> p q h d", h=2, d=HD)[:, :, h2, :],
                            O[rows, :, w, h2, 0:HD],
                            bcast(orec[rows, :].rearrange("p (q h) -> p q h", h=2)[:, :, h2].unsqueeze(2),
                                  [64, HU, HD]), ALU.mult)
                i.then_inc(o_read, 1)

            for n in range(UN):
                u = n % 2
                v.wait_ge(s_full, c * UN + n + 1)
                Sv = G[u][:, :].rearrange("p (h k) -> p h k", k=WIN)
                chain(nc.vector.tensor_reduce(amax[:, HU * u:HU * u + HU], Sv, AX.X, ALU.max))
                if n >= 2:
                    v.wait_ge(p_turned, c * UN + n - 1)
                nc.vector.tensor_tensor(PRB[u].rearrange("p (h k) -> p h k", k=WIN), Sv,
                                        bcast(amax[:, HU * u:HU * u + HU].unsqueeze(2), [P, HU, WIN]), ALU.subtract)\
                    .then_inc(s_read, 1)
                if n == 1:
                    hook(-1)
                if n:
                    hook(n - 1)
                if u == 1 and n > 1:
                    finish(n // 2 - 1)
            hook(UN - 1)
            finish(TL - 1)
            project_dve(v, 2, c, 0)

        def attn_pool(g, chain, c, hook, work):
            for k, (src, dst) in enumerate(((veq, rq), (vek, rk))):
                g.wait_ge(var_read, 2 * c + k + 1)
                if c:
                    g.wait_ge(yt_ready, count(2, c))
                nc.gpsimd.tensor_tensor(dst, src, bcast(mhalf, [P, CH]), ALU.pow).then_inc(rstd_qk, 1)
            for n in range(UN):
                hook(n)
                work()

        def scan_pe(pe, c, hook):
            body_start(pe, 4, c)
            xs = (chunk(XH, c, PAD), chunk(XL, c, PAD))
            pe.wait_ge(piece_ready, READY_AT["wqkva"])
            pe.wait_ge(xl_ready, count(4, c) + 1)
            mm3(U[0][:, :], wh("wqkva", 2 * P), xs, True, True).then_inc(scan_in, 1)
            mm3(G[1][:, :], wh("wqkva", P), xs, True, True).then_inc(scan_in, 1)
            mm3(G[0][:, :], wh("wqkva", 0), xs, True, True).then_inc(scan_in, 1)

        def scan_act(a, chain, c, hook):
            body_start(a, 4, c)
            a.wait_ge(scan_in, 3 * c + 1)
            nc.scalar.activation(buf[0], U[0][:, :], ACT.Sigmoid).then_inc(sig_ready, 1)

        def scan_dve(v, chain, c, hook):
            body_start(v, 4, c)
            v.wait_ge(sig_ready, c + 1)
            v.wait_ge(scan_in, 3 * c + 2)
            chain(nc.vector.tensor_tensor_scan(buf[1], buf[0], G[1][:, :], 0.0 if c == 0 else carry,
                                               ALU.mult, ALU.add))
            chain(nc.vector.tensor_copy(carry, buf[1][:, CH - 1:CH]))
            v.wait_ge(scan_in, 3 * c + 3)
            yt_free(v, 4, c)
            nc.vector.tensor_tensor(YT[:, :], buf[1], G[0][:, :], ALU.mult).then_inc(yt_ready, 1)

        UL = 16
        TB = [G[0], G[1], U[0], U[1]]
        MB = [buf[0], buf[1]]
        RB = [buf[2], buf[3]]
        AB = [buf[4], buf[5]]
        SN = [buf[6], buf[7]]
        CS = [buf[8], buf[9]]
        KT = buf[10]
        V4 = buf[11]
        TURN = 2.0 * float(np.pi)

        def on_act(n):
            return n % 2 == 0

        def unit_act(a, first, n):
            q = first + n
            if on_act(n):
                a.wait_ge(t_full, q + 1)
                if q >= 2:
                    a.wait_ge(r_ready, q - 1)
                nc.scalar.activation(MB[n % 2], TB[n % 4][:, :], ACT.Identity, bias=roundv).then_inc(m_ready, 1)

        def trig_act(a, first, n):
            q = first + n
            a.wait_ge(ab_ready, q + 1)
            if q >= 2:
                a.wait_ge(unit_used, q - 1)
            nc.scalar.activation(SN[n % 2], RB[n % 2], ACT.Sin, scale=-TURN)
            nc.scalar.activation(CS[n % 2], AB[n % 2], ACT.Sin, scale=-TURN, bias=half_pi).then_inc(trig_ready, 1)

        def unit_dve(v, chain, first, n):
            q = first + n
            if on_act(n):
                v.wait_ge(m_ready, q // 2 + 1)
            else:
                v.wait_ge(t_full, q + 1)
                chain(nc.vector.tensor_scalar(MB[n % 2], TB[n % 4][:, :], ROUND, None, ALU.add))
            if q >= 2:
                v.wait_ge(trig_ready, q - 1)
            nc.vector.scalar_tensor_tensor(RB[n % 2], MB[n % 2], ROUND, TB[n % 4][:, :],
                                           ALU.subtract, ALU.subtract).then_inc(r_ready, 1)
            v.wait_ge(r_ready, q + 1)
            nc.vector.scalar_tensor_tensor(AB[n % 2], RB[n % 2], -1.0, RB[n % 2], ALU.mult, ALU.max).then_inc(ab_ready, 1)

        def keys_pe(pe, c, hook):
            xs = (chunk(XH, c, PAD), chunk(XL, c, PAD))
            if c == 0:
                body_start(pe, 6, 0)
                pe.wait_ge(piece_ready, READY_AT["wo3"])
                pe.wait_ge(consts_ready, 1)
                nc.tensor.matmul(SP[:, 0:2 * P], ZERO[:, 0:P], B0[:, 0:2 * P], start=True, stop=False,
                                 skip_group_check=True)
            else:
                pe.wait_ge(r_ready, UL * c)
            pe.wait_ge(xl_ready, count(6, c) + 1)
            mm3(G[0][:, :], wh("wk3"), xs, True, True).then_inc(lin_full, 1)
            mm3(G[1][:, :], wh("wq3"), xs, True, True).then_inc(lin_full, 1)
            mm3(U[0][:, :], wh("wv3"), xs, True, True).then_inc(lin_full, 1)
            pe.wait_ge(lin_sb, 3 * c + 3)
            for j in range(TL):
                i = nc.tensor.transpose(U[1][:, j * P:(j + 1) * P], VT3[:, j * P:(j + 1) * P], ident)
            i.then_inc(vt_turned, 1)

            def phases(n):
                i_, g_ = n // 4, n % 4
                if n >= 4:
                    pe.wait_ge(r_ready, UL * c + n - 3)
                elif n == 3:
                    pe.wait_ge(v4_ready, c + 1)
                nc.tensor.matmul(TB[n % 4][:, :], KT[32 * g_:32 * g_ + 32, i_ * P:(i_ + 1) * P],
                                 WM[32 * g_:32 * g_ + 32, :, :].rearrange("p j m -> p (j m)"),
                                 start=True, stop=True).then_inc(t_full, 1)

            def gather(n):
                i_, g_ = n // 4, n % 4
                pe.wait_ge(trig_ready, UL * c + n + 1)
                pe.wait_ge(v4_ready, c + 1)
                for j in range(4):
                    h = 4 * g_ + j
                    for s_, src in enumerate((CS, SN)):
                        last = n == UL - 1 and j == 3 and s_ == 1
                        i = nc.tensor.matmul(SP[:, s_ * P + h * HD:s_ * P + (h + 1) * HD],
                                             src[n % 2][:, j * P:(j + 1) * P],
                                             V4[:, i_ * P + h * HD:i_ * P + (h + 1) * HD],
                                             start=False, stop=False, skip_group_check=True)
                i.then_inc(unit_used, 1)

            phases(0)
            phases(1)
            for n in range(UL):
                if n + 2 < UL:
                    phases(n + 2)
                gather(n)
                if n == 1:
                    hook(-1)
                if n % 2:
                    hook(n // 2)

        def keys_act(a, chain, c, hook):
            if c == 0:
                body_start(a, 6, 0)
            else:
                a.wait_ge(unit_used, UL * c)
            a.wait_ge(lin_full, 3 * c + 1)
            nc.scalar.activation(KT, G[0][:, :], ACT.Identity, bias=raw("bk")).then_inc(lin_sb, 1)
            a.wait_ge(lin_full, 3 * c + 2)
            nc.scalar.activation(chunk(QTF, c), G[1][:, :], ACT.Identity, bias=raw("bq")).then_inc(lin_sb, 1)
            a.wait_ge(lin_full, 3 * c + 3)
            nc.scalar.activation(VT3[:, :], U[0][:, :], ACT.Identity, bias=raw("bv")).then_inc(lin_sb, 1)
            a.wait_ge(vt_turned, c + 1)
            nc.scalar.activation(V4, U[1][:, :], ACT.Copy).then_inc(v4_ready, 1)
            units_act(a, UL * c, hook)

        def units_act(a, first, hook):
            unit_act(a, first, 0)
            for n in range(UL):
                if n + 1 < UL:
                    unit_act(a, first, n + 1)
                trig_act(a, first, n)
                if n == 1:
                    hook(-1)
                if n % 2:
                    hook(n // 2)

        def units_dve(v, chain, first, hook):
            for n in range(UL):
                unit_dve(v, chain, first, n)
                if n == 1:
                    hook(-1)
                if n % 2:
                    hook(n // 2)

        def keys_dve(v, chain, c, hook):
            if c == 0:
                body_start(v, 6, 0)
            units_dve(v, chain, UL * c, hook)

        QU = UL * NC

        def queries_pe(pe, c, hook):
            body_start(pe, 6, c)
            if c == 0:
                nc.tensor.matmul(SP[:, 0:2 * P], ZERO[:, 0:P], B0[:, 0:2 * P], start=False, stop=True,
                                 skip_group_check=True).then_inc(kv_full, 1)
                pe.wait_ge(r_ready, QU)
                pe.wait_ge(kv_ready, 1)
            pe.wait_ge(qts_ready, c + 1)

            def phases(n):
                if n >= 4:
                    pe.wait_ge(r_ready, QU + UL * c + n - 3)
                g_, j = n // 4, n % 4
                nc.tensor.matmul(TB[n % 4][:, :], WM[32 * g_:32 * g_ + 32, j, :], KT[32 * g_:32 * g_ + 32, :],
                                 start=True, stop=True).then_inc(t_full, 1)

            def apply(n):
                pe.wait_ge(trig_ready, QU + UL * c + n + 1)
                if n == 0 and c:
                    pe.wait_ge(oq_read, c)
                for i_ in range(TL):
                    for s_, src in enumerate((CS, SN)):
                        i = nc.tensor.matmul(SP[:, i_ * P + n * HD:i_ * P + (n + 1) * HD],
                                             src[n % 2][:, i_ * P:(i_ + 1) * P],
                                             KVS[:, s_, n * HD:(n + 1) * HD], start=s_ == 0, stop=s_ == 1)
                i.then_inc(unit_used, 1)

            phases(0)
            phases(1)
            for n in range(UL):
                if n + 2 < UL:
                    phases(n + 2)
                apply(n)
                if n == 1:
                    hook(-1)
                if n % 2:
                    hook(n // 2)
            project_pe(pe, 6, c, NC, oq_read, c + 1, "wo3", 0)

        def queries_act(a, chain, c, hook):
            if c == 0:
                a.wait_ge(kv_full, 1)
                nc.scalar.activation(KVS[:, :, :].rearrange("p s d -> p (s d)"), SP[:, 0:2 * P], ACT.Copy,
                                     scale=1.0 / P).then_inc(kv_ready, 1)
            body_start(a, 6, c)
            nc.scalar.activation(KT, chunk(QTF, c), ACT.Copy).then_inc(qts_ready, 1)
            units_act(a, QU + UL * c, hook)
            a.wait_ge(unit_used, QU + UL * (c + 1))
            nc.scalar.activation(AT, SP[:, :], ACT.Copy).then_inc(oq_read, 1)
            project_act(a, 6, c, NC, raw("bo"))

        def queries_dve(v, chain, c, hook):
            if c:
                body_start(v, 6, c)
            units_dve(v, chain, QU + UL * c, hook)
            project_dve(v, 6, c, NC)

        VT3 = sb("VT3", [P, CH])
        ZERO = sb("ZERO", [P, P])
        B0 = WR
        roundv = VEC[:, 17:18]

        STAGES_ = [
            ("stage0", 0, 0), (FFN0, 1, 1), ("attn", 2, 2), (FFN1, 3, 3), ("scan", 4, 4), (FFN2, 5, 5),
            ("keys", None, 6), ("queries", 6, None), (FFN3, 7, 7), (FFN4, 8, 8),
        ]

        def slots():
            tails = []
            for s_, (body, t, n) in enumerate(STAGES_):
                for c in range(NC):
                    tail = tails.pop() if tails else None
                    if t is not None:
                        tails.append((t, c))
                    if c < NC - 1:
                        front = (n, c + 1) if n is not None and n > 0 else None
                    else:
                        nxt = STAGES_[s_ + 1][2] if s_ + 1 < len(STAGES_) else None
                        front = (nxt, 0) if nxt is not None else None
                    yield body, c, tail, front

        BODY = {
            "stage0": (stage0_pe, stage0_act, stage0_dve), "attn": (attn_pe, attn_act, attn_dve),
            "scan": (scan_pe, scan_act, scan_dve), "keys": (keys_pe, keys_act, keys_dve),
            "queries": (queries_pe, queries_act, queries_dve),
        }
        HOOKED = ("attn", "keys", "queries")

        def walk(which, eng, chain, do_front, do_tail):
            for body, c, tail, front in slots():
                def hook(pos):
                    if pos == -1:
                        if tail:
                            do_tail(*tail)
                    elif front:
                        do_front(*front, pos)
                if isinstance(body, Ffn):
                    (ffn_pe, ffn_act, ffn_dve)[which](*([eng] + ([chain] if which else []) + [body, c, hook]))
                else:
                    if body not in HOOKED:
                        hook(-1)
                    BODY[body][which](*([eng] + ([chain] if which else []) + [c, hook]))
                    if body not in HOOKED:
                        for pos in range(8):
                            hook(pos)

        block = ctx.enter_context(nc.Block())

        @block.sync
        def _(sp):
            for c in range(NC):
                sp.dma_start(tiles(X, c), x_in[bass.ts(c, CH), :].rearrange("(t p) d -> p t d", p=P))\
                    .then_inc(x_loaded[c], 16)
                if c == 0:
                    sp.dma_start(WR[:, :], w_raw).then_inc(raw_loaded, 16)
            for i, (_, kind, _, _, col, n) in enumerate(PIECES):
                if i >= STAGES:
                    sp.wait_ge(piece_ready, i - STAGES + 1)
                src = w_split if kind == "split" else w_exact
                sp.dma_start(STG[:, i % STAGES, 0:n], src[:, col:col + n]).then_inc(piece_loaded[i % STAGES], 16)
            for c in range(NC):
                sp.wait_ge(res_done, count(8, c) + 1)
                sp.dma_start(out[bass.ts(c, CH), :].rearrange("(t p) d -> p t d", p=P), tiles(X, c))\
                    .then_inc(out_stored, 16)
            sp.wait_ge(out_stored, 16 * NC)

        @block.gpsimd
        def _(g):
            chain = Chain(g, pool_chain)
            state = [0]

            def work(limit):
                i = state[0]
                if i >= len(PIECES) or PIECES[i][0] > limit:
                    return
                state[0] += 1
                _, kind, _, at_, _, n = PIECES[i]
                g.wait_ge(piece_loaded[i % STAGES], 16 * (i // STAGES + 1))
                if PIECES[i][0] == 2:
                    g.wait_ge(yt_ready, count(1, 3) + 1)
                if PIECES[i][0] == 3:
                    g.wait_ge(yt_ready, count(3, 3) + 1)
                s_ = STG[:, i % STAGES, 0:n]
                if kind == "exact":
                    nc.gpsimd.tensor_scalar(WE[:, at_:at_ + n], s_, 1.0, 0.0, ALU.mult, ALU.add)\
                        .then_inc(piece_ready, 1)
                else:
                    hi = WH[:, at_:at_ + n]
                    chain(nc.gpsimd.tensor_scalar(hi, s_, 1.0, 0.0, ALU.mult, ALU.add))
                    nc.gpsimd.tensor_tensor(WL[:, at_:at_ + n], s_, hi.bitcast(F32), ALU.subtract)\
                        .then_inc(piece_ready, 1)

            g.wait_ge(consts_ready, 1)
            for c in range(NC):
                front_pool(g, chain, 0, c, 0)
                work(0)
                work(0)
            while state[0] < len(PIECES) and PIECES[state[0]][0] == 0:
                work(0)
            for body, c, tail, front in slots():
                def hook(pos):
                    if pos >= 0 and front:
                        front_pool(g, chain, *front, pos)
                limit = {"stage0": 0, FFN0: 1, "attn": 2, FFN1: 2, "scan": 2, FFN2: 3}.get(body, 3)
                if isinstance(body, Ffn):
                    ffn_pool(g, chain, body, c, hook, lambda: None)
                    for _ in range(3):
                        work(limit)
                elif body == "attn":
                    attn_pool(g, chain, c, hook, lambda: work(limit))
                else:
                    for pos in range(8):
                        hook(pos)
                if c == NC - 1:
                    while state[0] < len(PIECES) and PIECES[state[0]][0] <= limit:
                        work(limit)

        @block.scalar
        def _(a):
            chain = Chain(a, act_chain)
            a.wait_ge(raw_loaded, 16)
            nc.scalar.activation(a_dec, raw("decay"), ACT.Sigmoid).then_inc(decay_ready, 1)
            a.wait_ge(consts_ready, 1)
            for c in range(NC):
                for pos in range(8):
                    front_act(a, chain, 0, c, pos)
            walk(1, a, chain, lambda n, c, pos: front_act(a, chain, n, c, pos), lambda t, c: None)

        @block.vector
        def _(v):
            chain = Chain(v, dve_chain)
            for ap, value in ((mhalf, -0.5), (half_pi, float(np.pi / 2)), (epsv, EPS), (zero, 0.0), (roundv, ROUND)):
                nc.vector.memset(ap, value)
            nc.vector.memset(ZERO[:, :], 0.0)
            nc.vector.memset(VB[:, :, :, :, :, :].rearrange("p i q w h d -> p (i q w h d)"), 0.0)
            for t_ in (XH, XL):
                nc.vector.memset(t_[:, 0:PAD].bitcast(F32), 0.0)
                chain(nc.vector.memset(t_[:, T + PAD:T + 2 * PAD].bitcast(F32), 0.0))
            for s_ in range(2):
                nc.vector.memset(VB[64 * s_:64 * s_ + 64, :, :, :, s_, HD].rearrange("p i q w -> p (i q) w"), 1.0)
            v.wait_ge(raw_loaded, 16)
            for j in range(4):
                mask = raw("head_of_4", j, 1)
                nc.vector.tensor_scalar(gm[j], raw("ln_g1"), mask, None, ALU.mult)
                nc.vector.tensor_scalar(bm[j], raw("ln_b1"), mask, None, ALU.mult)
                nc.vector.tensor_scalar(WM[:, j, :], raw("proj"), mask,
                                        1.0 / (float(np.sqrt(HD)) * 2.0 * float(np.pi)), ALU.mult, ALU.mult)
            nc.vector.tensor_scalar(gam2, raw("gamma2"), float(np.sqrt(P)), None, ALU.mult)
            nc.vector.tensor_tensor(bias0, raw("b0"), raw("convb"), ALU.add).then_inc(consts_ready, 1)
            made = B[:, 0:2, :].rearrange("p a b -> p (a b)")
            for k in range(TAPS):
                nc.vector.tensor_scalar(made[:, P * (1 + k):P * (2 + k)], ident, raw("convw", k, 1), None, ALU.mult)
            w3 = raw("wqk1").rearrange("p (g d) -> p g d", d=HD)
            chain(nc.vector.tensor_reduce(wmean[:, :], w3, AX.X, ALU.add))
            chain(nc.vector.tensor_scalar(wmean[:, :], wmean[:, :], 1.0 / HD, None, ALU.mult))
            nc.vector.tensor_tensor(made[:, P * 6:P * 8].rearrange("p (g d) -> p g d", d=HD), w3,
                                    bcast(wmean[:, :].unsqueeze(2), [P, 32, HD]), ALU.subtract)
            v.wait_ge(decay_ready, 1)
            chain(nc.vector.tensor_scalar(one_minus_a, a_dec, -1.0, 1.0, ALU.mult, ALU.add))
            chain(nc.vector.tensor_scalar(made[:, 0:P], raw("wt0"), one_minus_a, None, ALU.mult))
            o = SPLIT_AT["wt0s"][0]
            chain(nc.vector.tensor_copy(WH[:, o:o + 2 * CH], made))
            nc.vector.tensor_tensor(WL[:, o:o + 2 * CH], made, WH[:, o:o + 2 * CH].bitcast(F32), ALU.subtract)\
                .then_inc(made_ready, 1)
            for c in range(NC):
                for pos in range(8):
                    front_dve(v, chain, 0, c, pos)
                chain(nc.vector.tensor_tensor_scan(S0[:, c * CH:(c + 1) * CH], bcast(a_dec, [P, CH]), X32[:, :],
                                                   0.0 if c == 0 else S0[:, c * CH - 1:c * CH], ALU.mult, ALU.add))
            walk(2, v, chain, lambda n, c, pos: front_dve(v, chain, n, c, pos),
                 lambda t, c: tail_dve(v, chain, t, c))
            tail_dve(v, chain, 8, NC - 1)

        @block.tensor
        def _(pe):
            pe.wait_ge(raw_loaded, 16)
            for c in range(NC):
                for pos in range(8):
                    front_pe(pe, 0, c, pos)
            walk(0, pe, None, lambda n, c, pos: front_pe(pe, n, c, pos), lambda t, c: tail_pe(pe, t, c))
            tail_pe(pe, 8, NC - 1)


def kernel(**inputs):
    import concourse.bacc as _bacc
    from concourse.bass_utils import run_bass_kernel_spmd as _run

    f = {k: np.asarray(v) for k, v in inputs.items()}

    def rows(a):
        a = a.reshape(a.shape[0], -1)
        return np.concatenate([a, np.zeros((P - a.shape[0], a.shape[1]), a.dtype)]) if a.shape[0] < P else a

    def wide(a):
        return np.concatenate([a, np.zeros((a.shape[0], P - a.shape[1]), a.dtype)], axis=1)

    def experts(a):
        return a.transpose(1, 0, 2).reshape(a.shape[1], -1)

    def blocks(a):
        return a.reshape(-1, P, a.shape[-1]).transpose(1, 0, 2).reshape(P, -1)

    def cols(a):
        return a.reshape(-1, P).T

    qkv = f["L1_attn_W_qkv"]
    z64 = np.zeros((P, 64), np.float32)
    w = {
        "gate0": wide(f["L0_ffn_gate_w"].T), "w1_0": experts(f["L0_ffn_w1"]), "w3_0": experts(f["L0_ffn_w3"]),
        "w2_0": blocks(f["L0_ffn_w2"].reshape(-1, P)),
        "wqk1": qkv[:, 0:2 * P], "wv1": qkv[:, 2 * P:], "wproj": f["L1_attn_W_proj"],
        "gate1": wide(f["L1_ffn_gate_w"].T),
        "wg1": np.concatenate([experts(f["L1_ffn_w_gate"]), f["L1_ffn_ws_gate"], z64], axis=1),
        "wu1": np.concatenate([experts(f["L1_ffn_w_up"]), f["L1_ffn_ws_up"], z64], axis=1),
        "wd1": blocks(np.concatenate([f["L1_ffn_w_down"].reshape(-1, P), f["L1_ffn_ws_down"], z64.T], axis=0)),
        "wqkva": f["L2_attn_W_qkva"].T, "gate2": wide(f["L2_ffn_Wg"]), "w1_2": experts(f["L2_ffn_W1"]),
        "w2_2": blocks(f["L2_ffn_W2"].reshape(-1, P)),
        "b2_2": rows(np.concatenate([f["L2_ffn_b2"], f["L2_ffn_b2"]])),
        "wq3": f["L3_attn_wq"], "wk3": f["L3_attn_wk"], "wv3": f["L3_attn_wv"], "wo3": f["L3_attn_wo"],
        "w1_3": f["L3_attn_w1"], "w2_3": blocks(f["L3_attn_w2"]), "fw1": f["L3_ffn_W1"], "fw2": blocks(f["L3_ffn_W2"]),
        "wt0": f["L0_attn_W"].T, "proj": np.tile(f["L3_attn_proj_mat"], (NH, 1)),
        "decay": cols(f["L0_attn_decay_logit"]), "convw": f["L0_attn_conv_w"].reshape(P, TAPS),
        "b0": cols(f["L0_attn_b"]), "convb": cols(f["L0_attn_conv_b"]),
        "ln_g1": cols(np.tile(f["L1_attn_ln_gamma"], NH)), "ln_b1": cols(np.tile(f["L1_attn_ln_beta"], NH)),
        "bproj": cols(f["L1_attn_b_proj"]), "gamma2": cols(f["L2_attn_gamma"]),
        "bg2": rows(f["L2_ffn_bg"].reshape(-1, 1)), "b1_2": cols(f["L2_ffn_b1"].reshape(-1)),
        "bq": cols(f["L3_attn_bq"]), "bk": cols(f["L3_attn_bk"]), "bv": cols(f["L3_attn_bv"]),
        "bo": cols(f["L3_attn_bo"]), "g1_3": cols(f["L3_attn_ln1_g"]), "e1_3": cols(f["L3_attn_ln1_b"]),
        "g2_3": cols(f["L3_attn_ln2_g"]), "e2_3": cols(f["L3_attn_ln2_b"]), "b1_3": cols(f["L3_attn_b1"]),
        "b2_3": cols(f["L3_attn_b2"]), "fb1": cols(f["L3_ffn_b1"]), "fb2": cols(f["L3_ffn_b2"]),
    }
    k = np.arange(P)
    w["ident"] = np.eye(P, dtype=np.float32)
    w["group_mean"] = (k[:, None] // HD == k[None, :] // HD).astype(np.float32) / HD
    w["iota"] = np.tile(np.arange(16, dtype=np.float32), (P, 1))
    w["head_of_4"] = (k[:, None] // HD % 4 == np.arange(4)[None, :]).astype(np.float32)
    for name, E, per in (("sel16", 16, 2), ("sel8", 8, 1)):
        col = np.arange(8 * P)
        expert = col // P * per + col % P * per // P
        w[name] = rows(((k[:2 * E, None] % E) == expert[None, :]).astype(np.float32))

    def pack(names, table):
        sizes = dict(table)
        for n in names:
            assert w[n].shape == (P, sizes[n]), (n, w[n].shape, sizes[n])
        return np.ascontiguousarray(np.concatenate([w[n] for n in names], axis=1))

    order = [n for g in GROUPS for n in g]
    arrays = {
        "in_x": np.ascontiguousarray(f["L0_attn_x"].reshape(T, P)),
        "in_w_split": pack([n for n in order if n not in EXACT_AT], SPLIT),
        "in_w_exact": pack([n for n in order if n in EXACT_AT], EXACT),
        "in_w_raw": pack([n for n, _ in RAW], RAW),
    }
    nc = _bacc.Bacc("TRN2", target_bir_lowering=False, num_devices=1)
    args = [nc.dram_tensor(n, a.shape, mybir.dt.from_np(a.dtype), kind="ExternalInput").ap()
            for n, a in arrays.items()]
    out = nc.dram_tensor("out_0", (T, P), F32, kind="ExternalOutput").ap()
    build(nc, *args, out)
    r = _run(nc, [arrays], core_ids=[0])
    return r.results[0]["out_0"].reshape(1, T, P)
```

```python
from contextlib import ExitStack

import numpy as np

import concourse.bass as bass
from concourse import mybir

F32 = mybir.dt.float32
F32R = mybir.dt.float32r
U32 = mybir.dt.uint32
ALU = mybir.AluOpType
ACT = mybir.ActivationFunctionType
AX = mybir.AxisListType

P = 128
T = 2048
CH = 512
NC = T // CH
TL = CH // P
NH, HD = 16, 8
WIN = 64
TAPS = 5
EPS = 1e-5
ROUND = 1.5 * 2.0 ** 23
PIECE = 512
STAGES = 4

SPLIT = [
    ("gate0", 128), ("w1_0", 1024), ("w3_0", 1024), ("w2_0", 1024),
    ("wv1", 128), ("wproj", 128),
    ("gate1", 128), ("wg1", 1152), ("wu1", 1152), ("wd1", 1152),
    ("wqkva", 384),
    ("gate2", 128), ("w1_2", 2048), ("w2_2", 2048), ("b2_2", 128),
    ("wq3", 512), ("wk3", 512), ("wv3", 128), ("wo3", 128),
    ("w1_3", 512), ("w2_3", 512), ("fw1", 512), ("fw2", 512),
]
EXACT = [("sel16", 1024)]
RAW = [
    ("ident", 128), ("wt0", 128), ("mean_q", 32), ("mean_k", 32), ("spread_q", 128), ("spread_k", 128), ("wqk1", 256), ("proj", 128), ("iota", 16),
    ("head_of_4", 4), ("decay", 1), ("convw", TAPS), ("b0", 1), ("convb", 1), ("ln_g1", 1),
    ("ln_b1", 1), ("bproj", 1), ("gamma2", 1), ("bg2", 1), ("b1_2", 16), ("bq4", 4), ("bk4", 4),
    ("bv", 1), ("bo", 1), ("g1_3", 1), ("e1_3", 1), ("g2_3", 1), ("e2_3", 1), ("b1_3", 4),
    ("b2_3", 1), ("fb1", 4), ("fb2", 1),
]
MADE = [("wt0s", 128), ("taps", TAPS * 128), ("wqk1c", 256)]


def places(table, at=0):
    out = {}
    for name, n in table:
        out[name] = (at, n)
        at += n
    return out, at


SPLIT_AT, _end = places([s_ for s_ in SPLIT if s_[0] in (
    "gate0", "wv1", "wproj", "gate1", "wqkva", "gate2", "b2_2", "w2_2")] + MADE)
_region_a, _end_a = places([s_ for s_ in SPLIT if s_[0] in ("w1_0", "w3_0", "w2_0")], _end)
_over_a, _ = places([s_ for s_ in SPLIT if s_[0] in ("w1_2",)], _end)
_region_b, NSPLIT = places([s_ for s_ in SPLIT if s_[0] in ("wg1", "wu1", "wd1")], _end_a)
_over_b, _end_b = places([s_ for s_ in SPLIT if s_[0] in (
    "wq3", "wk3", "wv3", "wo3", "w1_3", "w2_3", "fw1", "fw2")], _end_a)
assert _end_b <= NSPLIT
SPLIT_AT = SPLIT_AT | _region_a | _over_a | _region_b | _over_b
EXACT_AT, NEXACT = places(EXACT)
RAW_AT, NRAW = places(RAW)

GROUPS = [
    ["gate0", "w1_0", "w3_0", "w2_0", "sel16"],
    ["wv1", "wproj", "gate1", "wg1", "wu1", "wd1"],
    ["wqkva", "gate2", "b2_2", "w1_2", "w2_2"],
    ["wq3", "wk3", "wv3", "wo3", "w1_3", "w2_3", "fw1", "fw2"],
]


def pieces():
    out, packed = [], {"split": 0, "exact": 0}
    for g, names in enumerate(GROUPS):
        for name in names:
            kind = "exact" if name in EXACT_AT else "split"
            at, n = (EXACT_AT if kind == "exact" else SPLIT_AT)[name]
            for k in range(0, n, PIECE):
                w = min(PIECE, n - k)
                last = out[-1] if out else None
                if last and last[0] == g and last[1] == kind and last[3] + last[5] == at + k and last[5] + w <= PIECE:
                    out[-1] = (g, kind, last[2] + [name], last[3], last[4], last[5] + w)
                else:
                    out.append((g, kind, [name], at + k, packed[kind], w))
                packed[kind] += w
    return out


PIECES = pieces()
READY_AT = {name: i + 1 for i, p in enumerate(PIECES) for name in p[2]}


class Ffn:
    def __init__(self, key, norm, tail, experts, blocks, up, gate, down, func, topk=0, spread=0,
                 spread_every=1, plain_block=None):
        self.key, self.norm, self.tail, self.experts, self.blocks = key, norm, tail, experts, blocks
        self.up, self.gate, self.down, self.func, self.topk = up, gate, down, func, topk
        self.spread, self.spread_every, self.plain_block = spread, spread_every, plain_block


FFN0 = Ffn("ffn0", 1, 1, 16, 8, "w1_0", "w3_0", "w2_0", ACT.Silu, 4, 8)
FFN1 = Ffn("ffn1", 3, 3, 16, 9, "wg1", "wu1", "wd1", ACT.Silu, 2, 8, 1, 8)
FFN2 = Ffn("ffn2", 5, 5, 8, 16, "w1_2", None, "w2_2", ACT.Relu, 2, 8, 2)
FFN3 = Ffn("ffn3", 7, 7, 0, 4, "w1_3", None, "w2_3", ACT.Relu)
FFN4 = Ffn("ffn4", 8, 8, 0, 4, "fw1", None, "fw2", ACT.Relu)
FFNS = [FFN0, FFN1, FFN2, FFN3, FFN4]
_blk = _sp = _rt = 0
for _f in FFNS:
    _f.block0, _f.spread0, _f.router0 = _blk, _sp, _rt
    _blk += NC * _f.blocks
    _sp += NC * _f.spread
    _rt += NC * (1 if _f.experts else 0)
    _f.dense = not _f.experts
    _f.lag = 2 if _f.dense else 3
    _f.early = 0
ROUTED = {f.norm: f for f in FFNS if f.experts}
LAST_NORM = 8


def build(nc, x_in, w_split, w_exact, w_raw, out):
    with ExitStack() as ctx:
        def sb(name, shape, dt=F32):
            return ctx.enter_context(nc.sbuf_tensor(name, shape, dt))

        def bank(name):
            return ctx.enter_context(nc.psum_tensor(name, [P, CH], F32))

        def sem(name):
            return ctx.enter_context(nc.semaphore(name))

        X = sb("X", [P, NC * TL, P])
        Z = sb("Z", [P, NC * TL, P])
        PAD = TAPS // 2
        XH = sb("XH", [P, T + 2 * PAD], F32R)
        XL = sb("XL", [P, T + 2 * PAD], F32R)
        WH = sb("WH", [P, NSPLIT], F32R)
        WL = sb("WL", [P, NSPLIT], F32R)
        WE = sb("WE", [P, NEXACT], F32R)
        WR = sb("WR", [P, NRAW])
        STG = sb("STG", [P, STAGES, PIECE])
        XN = sb("XN", [P, TL, P])
        X32 = sb("X32", [P, CH])
        YT = sb("YT", [P, CH])
        SCT = sb("SCT", [2 * NH, 2 * CH], F32R)
        S0 = sb("S0", [P, T])
        B = sb("B", [P, 12, CH])
        buf = [B[:, i, :] for i in range(12)]
        rbuf = [sb(f"rbuf{i}", [P, CH], F32R) for i in range(4)]
        VB = sb("VB", [P, TL, NH // 2, 2, 2, HD + 1])
        KVT = sb("KVT", [P, 2, 4, P])
        WM = sb("WM", [P, 4, P], F32R)
        small = sb("small", [P, 1024])
        IDX = sb("IDX", [P, TL, 8], U32)
        VEC = sb("VEC", [P, 32])

        G = [bank("gate_bank0"), bank("gate_bank1")]
        U = [bank("up_bank0"), bank("up_bank1")]
        SP = bank("spread_bank")
        Y = bank("y_bank")
        TN = bank("norm_bank")
        R = bank("route_bank")

        at = 0

        def cut(n):
            nonlocal at
            at += n
            assert at <= 1024
            return small[:, at - n:at]

        stats = cut(TL * 6).rearrange("p (a b) -> p a b", a=TL)
        mv = cut(TL * 2).rearrange("p (a b) -> p a b", a=TL)
        ve = cut(TL)
        rs = cut(TL)
        rr = cut(TL)
        ss = cut(TL)
        rmax = cut(TL)
        top = cut(TL * 8).rearrange("p (a b) -> p a b", a=TL)
        idxf = cut(TL * 8).rearrange("p (a b) -> p a b", a=TL)
        den = cut(TL)
        rec = cut(TL)
        RE = cut(TL * NH)
        RM = cut(TL * NH)
        RS_ = cut(TL * NH)
        EQ = cut(TL * NH * 4)
        SC2 = cut(TL * NH * 2)
        amax = cut(16)
        orec = cut(NH)
        wmean = cut(32)
        sq_scratch = cut(P)
        mhalf = VEC[:, 0:1]
        a_dec, one_minus_a, bias0 = VEC[:, 1:2], VEC[:, 2:3], VEC[:, 3:4]
        gm = [VEC[:, 4 + j:5 + j] for j in range(4)]
        bm = [VEC[:, 8 + j:9 + j] for j in range(4)]
        gam2 = VEC[:, 12:13]
        half_pi = VEC[:, 13:14]
        carry = VEC[:, 14:15]
        epsv = VEC[:, 15:16]
        zero = VEC[:, 16:17]

        def raw(name, a=0, n=None):
            o, w = RAW_AT[name]
            return WR[:, o + a:o + a + (w - a if n is None else n)]

        ident = raw("ident")

        x_loaded = [sem(f"x_loaded{c}") for c in range(NC)]
        raw_loaded = sem("raw_loaded")
        piece_loaded = [sem(f"piece_loaded{k}") for k in range(STAGES)]
        piece_ready = sem("piece_ready")
        consts_ready = sem("consts_ready")
        decay_ready = sem("decay_ready")
        made_ready = sem("made_ready")
        pads_ready = sem("pads_ready")
        out_stored = sem("out_stored")
        dve_chain = sem("dve_chain")
        act_chain = sem("act_chain")
        pool_chain = sem("pool_chain")
        stats_ready = sem("stats_ready")
        rstd_ready = sem("rstd_ready")
        xn_ready = sem("xn_ready")
        norm_turned = sem("norm_turned")
        x32_ready = sem("x32_ready")
        xh_ready = sem("xh_ready")
        xl_ready = sem("xl_ready")
        sumsq_ready = sem("sumsq_ready")
        scale2_ready = sem("scale2_ready")
        token_squares = sem("token_squares")
        logits_t = sem("logits_t")
        logits_sb = sem("logits_sb")
        logits_tok = sem("logits_tok")
        shifted = sem("shifted")
        scored = sem("scored")
        weights_tok = sem("weights_tok")
        weights_t = sem("weights_t")
        weights_sb = sem("weights_sb")
        y_full = sem("y_full")
        yt_ready = sem("yt_ready")
        yt_turned = sem("yt_turned")
        res_done = sem("res_done")
        first_full = sem("first_full")
        second_full = sem("second_full")
        mul_done = sem("mul_done")
        spread_full = sem("spread_full")
        act_done = sem("act_done")
        h_ready = sem("h_ready")
        hh_ready = sem("hh_ready")
        hl_ready = sem("hl_ready")
        down_done = sem("down_done")
        s_ready = sem("s_ready")
        s_high = sem("s_high")
        s_low = sem("s_low")
        qkv_full = sem("qkv_full")
        squares = sem("squares")
        v_copied = sem("v_copied")
        v_turned = sem("v_turned")
        v_placed = sem("v_placed")
        var_full = sem("var_full")
        var_read = sem("var_read")
        rstd_qk = sem("rstd_qk")
        rstd_full = sem("rstd_full")
        centred = sem("centred")
        qk_read = sem("qk_read")
        qk_ready = sem("qk_ready")
        s_full = sem("scores_full")
        s_read = sem("scores_read")
        p_ready = sem("probs_ready")
        p_turned = sem("probs_turned")
        pt_ready = sem("probs_t_ready")
        o_full = sem("o_full")
        o_read = sem("o_read")
        a_turned = sem("a_turned")
        a32_ready = sem("a32_ready")
        ah_ready = sem("ah_ready")
        al_ready = sem("al_ready")
        scan_in = sem("scan_in")
        sig_ready = sem("sig_ready")
        phase_weights = sem("phase_weights")
        proj_full = sem("proj_full")
        proj_sb = sem("proj_sb")
        ks_high = sem("ks_high")
        ks_ready = sem("ks_ready")
        vt_turned = sem("vt_turned")
        v4_ready = sem("v4_ready")
        t_full = sem("phase_full")
        m_ready = sem("rounded_ready")
        m_ready_dve = sem("rounded_ready_dve")
        r_ready = sem("rest_ready")
        ab_ready = sem("abs_ready")
        cos_ready = sem("cos_ready")
        sin_ready = sem("sin_ready")
        unit_used = sem("unit_used")
        kvf_ready = sem("kvf_ready")
        kv_turned = sem("kv_turned")
        kv_ready = sem("kv_ready")
        oq_read = sem("oq_read")

        class Chain:

            def __init__(self, eng, s):
                self.eng, self.s, self.n = eng, s, 0

            def __call__(self, ins):
                self.n += 1
                ins.then_inc(self.s, 1)
                self.eng.wait_ge(self.s, self.n)

        def chunk(ap2, c, pad=0):
            return ap2[:, bass.ds(c * CH + pad, CH)]

        def tiles(a3, c):
            return a3[:, bass.ds(c * TL, TL), :]

        def bcast(ap, shape):
            return ap.broadcast_to(shape)

        def count(stage, c):
            return NC * stage + c

        def wh(name, a=0, n=P):
            o = SPLIT_AT[name][0] + a
            return WH[:, o:o + n], WL[:, o:o + n]

        turned = {"norms": 0, "tails": 0}

        def front_source(n):
            return Z if n == 7 else X

        def front_dve(v, chain, n, c, pos):
            m = count(n, c)
            src = front_source(n)

            def read_stats(t3, first):
                for j in range(TL):
                    i = nc.vector.bn_stats(stats[:, j, :], t3(j))
                chain(i)
                for j in range(TL):
                    i = nc.vector.bn_aggr(mv[:, j, :], stats[:, j, :])
                i.then_inc(stats_ready, 1)

            sbase = m + max(0, m - count(6, 0)) if n <= 6 else m + NC
            if pos == 0:
                if n == 0:
                    v.wait_ge(x_loaded[c], 16)
                else:
                    v.wait_ge(res_done, count(n - 1, c) + 1)
                read_stats(lambda j: src[:, c * TL + j, :], True)
            if pos == 1:
                v.wait_ge(rstd_ready, sbase + 1)
                if m:
                    v.wait_ge(norm_turned, m)
                dst = (lambda j: Z[:, c * TL + j, :]) if n == 6 else (lambda j: XN[:, j, :])
                for j in range(TL):
                    i = nc.vector.tensor_scalar(dst(j), src[:, c * TL + j, :], mv[:, j, 0:1],
                                                rs[:, j:j + 1], ALU.subtract, ALU.mult)
                if n == 6:
                    chain(i)
                    read_stats(lambda j: Z[:, c * TL + j, :], False)
                    v.wait_ge(rstd_ready, sbase + 2)
                    for j in range(TL):
                        i = nc.vector.tensor_scalar(XN[:, j, :], Z[:, c * TL + j, :], mv[:, j, 0:1],
                                                    rs[:, j:j + 1], ALU.subtract, ALU.mult)
                    i.then_inc(xn_ready, 1)
                elif n == 4:
                    i.then_inc(sumsq_ready, 1)
                    v.wait_ge(scale2_ready, c + 1)
                    for j in range(TL):
                        i = nc.vector.tensor_scalar(XN[:, j, :], XN[:, j, :], rr[:, j:j + 1], None, ALU.mult)
                    i.then_inc(xn_ready, 1)
                else:
                    i.then_inc(xn_ready, 1)
            if pos == 3:
                v.wait_ge(x32_ready, m + 1)
                nc.vector.tensor_copy(chunk(XH, c, PAD), X32[:, :]).then_inc(xh_ready, 1)
                v.wait_ge(xh_ready, m + 1)
                nc.vector.tensor_tensor(chunk(XL, c, PAD), X32[:, :], chunk(XH, c, PAD).bitcast(F32),
                                        ALU.subtract).then_inc(xl_ready, 1)
            f = ROUTED.get(n)
            if not f:
                return
            E, K = f.experts, f.topk
            r = f.router0 + c
            Rv = R[:, 0:TL * E].rearrange("p (t e) -> p t e", t=TL)
            re = RE[:, 0:TL * E].rearrange("p (t e) -> p t e", t=TL)
            rm = RM[:, 0:TL * E].rearrange("p (t e) -> p t e", t=TL)
            rw = RS_[:, 0:TL * E].rearrange("p (t e) -> p t e", t=TL)
            eq = EQ[:, 0:TL * E * K].rearrange("p (t e k) -> p t e k", t=TL, k=K)
            D_ = NH // E
            sc2 = SC2[:, :].rearrange("p (t s e d) -> p t s e d", t=TL, s=2, d=D_)
            rwd = bcast(rw.unsqueeze(3), [P, TL, E, D_])
            if pos == 5 and n != 3:
                v.wait_ge(logits_tok, r + 1)
                chain(nc.vector.tensor_reduce(rmax[:, :], Rv, AX.X, ALU.max))
                nc.vector.tensor_tensor(re, Rv, bcast(rmax[:, :].unsqueeze(2), [P, TL, E]),
                                        ALU.subtract).then_inc(shifted, 1)
            if pos == 6:
                v.wait_ge(scored, r + 1)
                for j in range(TL):
                    i = nc.vector.max(top[:, j, :], re[:, j, :])
                chain(i)
                for j in range(TL):
                    i = nc.vector.max_index(IDX[:, j, :], top[:, j, :], re[:, j, :])
                chain(i)
                chain(nc.vector.tensor_copy(idxf, IDX[:, :, :]))
                for j in range(TL):
                    i = nc.vector.tensor_tensor(
                        eq[:, j, :, :], bcast(raw("iota", 0, E).unsqueeze(2), [P, E, K]),
                        bcast(idxf[:, j, 0:K].unsqueeze(1), [P, E, K]), ALU.is_equal)
                chain(i)
                chain(nc.vector.tensor_reduce(RM[:, 0:TL * E], EQ[:, 0:TL * E * K].rearrange(
                    "p (a k) -> p a k", k=K), AX.X, ALU.add))
                chain(nc.vector.tensor_reduce(den[:, :], top[:, :, 0:K], AX.X, ALU.add))
                if n == 3:
                    chain(nc.vector.tensor_scalar(den[:, :], den[:, :], 1e-20, None, ALU.add))
                chain(nc.vector.reciprocal(rec[:, :], den[:, :]))
                if n == 3:
                    chain(nc.vector.tensor_scalar(rec[:, :], rec[:, :], 2.5, None, ALU.mult))
                chain(nc.vector.tensor_tensor(rw, re, rm, ALU.mult))
                chain(nc.vector.tensor_tensor(rw, rw, bcast(rec[:, :].unsqueeze(2), [P, TL, E]), ALU.mult))
                for k in range(TL):
                    i = nc.vector.tensor_copy(sc2[:, k, 0, :, :].bitcast(F32R), rwd[:, k, :, :])
                chain(i)
                for k in range(TL):
                    i = nc.vector.tensor_tensor(sc2[:, k, 1, :, :], rwd[:, k, :, :], sc2[:, k, 0, :, :], ALU.subtract)
                i.then_inc(weights_tok, 1)

        def front_pool(g, chain, n, c, pos):
            m = count(n, c)
            sbase = m + max(0, m - count(6, 0)) if n <= 6 else m + NC
            if pos == 0 or pos == 1 and n == 6:
                g.wait_ge(stats_ready, sbase + pos + 1)
                chain(nc.gpsimd.tensor_scalar(ve[:, :], mv[:, :, 1], 1.0, EPS, ALU.mult, ALU.add))
                nc.gpsimd.tensor_tensor(rs[:, :], ve[:, :], bcast(mhalf, [P, TL]), ALU.pow)\
                    .then_inc(rstd_ready, 1)
                if n == 4:
                    g.wait_ge(token_squares, c + 1)
                    chain(nc.gpsimd.tensor_scalar(ve[:, :], ss[:, :], 1e-24, None, ALU.max))
                    nc.gpsimd.tensor_tensor(rr[:, :], ve[:, :], bcast(mhalf, [P, TL]), ALU.pow)\
                        .then_inc(scale2_ready, 1)

        def front_act(a, chain, n, c, pos):
            m = count(n, c)
            if pos == 1 and n == 4:
                a.wait_ge(sumsq_ready, c + 1)
                for j in range(TL):
                    i = nc.scalar.activation(sq_scratch, XN[:, j, :], ACT.Square, accum_out=ss[:, j:j + 1])
                    if j < TL - 1:
                        chain(i)
                i.then_inc(token_squares, 1)
            if pos == 2:
                a.wait_ge(norm_turned, m + 1)
                if m:
                    a.wait_ge(xl_ready, m)
                if n == 4:
                    nc.scalar.activation(X32[:, :], TN[:, :], ACT.Copy, scale=gam2).then_inc(x32_ready, 1)
                elif n in (6, 7):
                    g_, b_ = ("g1_3", "e1_3") if n == 6 else ("g2_3", "e2_3")
                    nc.scalar.activation(X32[:, :], TN[:, :], ACT.Identity, scale=raw(g_), bias=raw(b_))\
                        .then_inc(x32_ready, 1)
                else:
                    nc.scalar.activation(X32[:, :], TN[:, :], ACT.Copy).then_inc(x32_ready, 1)
            f = ROUTED.get(n)
            if not f:
                return
            E = f.experts
            r = f.router0 + c
            if pos == 4:
                a.wait_ge(logits_t, r + 1)
                bias = raw("bg2")[0:E, :] if n == 5 else zero[0:E, :]
                nc.scalar.activation(YL[0:E, :], R[0:E, :], ACT.Identity, bias=bias).then_inc(logits_sb, 1)
            if pos == 6:
                Rv = R[:, 0:TL * E].rearrange("p (t e) -> p t e", t=TL)
                re = RE[:, 0:TL * E].rearrange("p (t e) -> p t e", t=TL)
                if n == 3:
                    a.wait_ge(logits_tok, r + 1)
                    nc.scalar.activation(re, Rv, ACT.Sigmoid).then_inc(scored, 1)
                else:
                    a.wait_ge(shifted, shift_count(n, c) + 1)
                    nc.scalar.activation(re, re, ACT.Exp).then_inc(scored, 1)
            if pos == 7:
                a.wait_ge(weights_t, r + 1)
                nc.scalar.activation(SCT[0:2 * NH, bass.ds(c % 2 * CH, CH)], R[0:2 * NH, :], ACT.Copy)\
                    .then_inc(weights_sb, 1)

        YL = sb("YL", [NH, CH])

        def shift_count(n, c):
            return {1: 0, 5: NC}[n] + c

        def front_pe(pe, n, c, pos):
            m = count(n, c)
            if pos == 2:
                pe.wait_ge(xn_ready, m + 1)
                if m:
                    pe.wait_ge(x32_ready, m)
                if turned["tails"]:
                    pe.wait_ge(res_done, turned["tails"])
                turned["norms"] += 1
                for j in range(TL):
                    i = nc.tensor.transpose(TN[:, j * P:(j + 1) * P], XN[:, j, :], ident)
                i.then_inc(norm_turned, 1)
            f = ROUTED.get(n)
            if not f:
                return
            E = f.experts
            r = f.router0 + c
            if pos == 4:
                pe.wait_ge(xl_ready, m + 1)
                pe.wait_ge(piece_ready, READY_AT[f"gate{(n - 1) // 2}"])
                if r:
                    pe.wait_ge(weights_sb, r)
                mm3(R[:, :], wh(f"gate{(n - 1) // 2}"), (chunk(XH, c, PAD), chunk(XL, c, PAD)), True, True)\
                    .then_inc(logits_t, 1)
            if pos == 5:
                pe.wait_ge(logits_sb, r + 1)
                for j in range(TL):
                    i = nc.tensor.transpose(R[:, j * E:(j + 1) * E], YL[0:E, j * P:(j + 1) * P],
                                            ident[0:E, 0:E])
                i.then_inc(logits_tok, 1)
            if pos == 7:
                pe.wait_ge(weights_tok, r + 1)
                for j in range(TL):
                    i = nc.tensor.transpose(R[0:2 * NH, j * P:(j + 1) * P],
                                            SC2[:, j * 2 * NH:(j + 1) * 2 * NH], ident)
                i.then_inc(weights_t, 1)

        def mm3(dst, w, x, start, stop):
            nc.tensor.matmul(dst, w[0], x[0], start=start, stop=False)
            nc.tensor.matmul(dst, w[0], x[1], start=False, stop=False)
            return nc.tensor.matmul(dst, w[1], x[0], start=False, stop=stop)

        def tail_pe(pe, t, c):
            n = count(t, c)
            pe.wait_ge(yt_ready, n + 1)
            if turned["norms"]:
                pe.wait_ge(x32_ready, turned["norms"])
            if n:
                pe.wait_ge(res_done, n)
            turned["tails"] += 1
            for j in range(TL):
                i = nc.tensor.transpose(TN[:, j * P:(j + 1) * P], YT[:, j * P:(j + 1) * P], ident)
            i.then_inc(yt_turned, 1)

        def tail_dve(v, chain, t, c):
            n = count(t, c)
            v.wait_ge(yt_turned, n + 1)
            Yv = TN[:, :].rearrange("p (t d) -> p t d", t=TL)
            if t == 6:
                nc.vector.tensor_tensor(tiles(Z, c), tiles(Z, c), Yv, ALU.add).then_inc(res_done, 1)
            elif t == 7:
                chain(nc.vector.tensor_tensor(tiles(Z, c), tiles(Z, c), Yv, ALU.add))
                nc.vector.tensor_tensor(tiles(X, c), tiles(X, c), tiles(Z, c), ALU.add).then_inc(res_done, 1)
            else:
                nc.vector.tensor_tensor(tiles(X, c), tiles(X, c), Yv, ALU.add).then_inc(res_done, 1)

        def y_bank_free(pe, t, c):
            if count(t, c):
                pe.wait_ge(yt_ready, count(t, c))

        def yt_free(eng, t, c):
            if count(t, c):
                eng.wait_ge(yt_turned, count(t, c))

        def block_no(f, c, b):
            return f.block0 + f.blocks * c + b

        AO = [buf[0], buf[1]]
        MO = [buf[2], buf[3]]
        HO = [buf[4], buf[5], buf[6]]

        def body_start(eng, t, c):
            if count(t, c):
                eng.wait_ge(yt_ready, count(t, c))

        def count_y(t, c):
            return {0: 0, 2: NC, 6: 2 * NC}[t] + c

        def ffn_steps(f):
            return [(c * f.blocks + b, c, b) for c in range(NC) for b in range(f.blocks)]

        def lagged(f, c, b, lag):
            k = c * f.blocks + b
            last = k == NC * f.blocks - 1
            return [divmod(i, f.blocks) for i in range(k - lag, k + (1 if last else -lag + 1)) if i >= 0]

        def in_stage(f, c, b, depth):
            return c * f.blocks + b >= depth

        def hooks(f, c, b, hook, tail_late):
            if b == (min(f.lag + tail_late, f.blocks - 1) if c else tail_late):
                hook(-1)
            per = 8 / min(f.blocks, 8) if f.blocks < 16 else 1 / 2
            for pos in range(int(b * per), min(int((b + 1) * per), 8)):
                hook(pos)

        def ffn_pe(pe, f, c, hook):
            if c == 0:
                body_start(pe, f.tail, 0)
                for name in [f.up, f.gate, f.down]:
                    if name:
                        pe.wait_ge(piece_ready, READY_AT[name])
                if f.experts:
                    pe.wait_ge(piece_ready, READY_AT["sel16"])
                if f.experts == 8:
                    pe.wait_ge(piece_ready, READY_AT["b2_2"])
            pe.wait_ge(xl_ready, count(f.norm, c) + 1)

            def up(c, b):
                n = block_no(f, c, b)
                xs = (chunk(XH, c, PAD), chunk(XL, c, PAD))
                if in_stage(f, c, b, 2):
                    pe.wait_ge(act_done, n - 1)
                mm3(G[n % 2][:, :], wh(f.up, b * P), xs, True, True).then_inc(first_full, 1)
                if f.gate:
                    if in_stage(f, c, b, 2):
                        pe.wait_ge(mul_done, n - 1)
                    mm3(U[n % 2][:, :], wh(f.gate, b * P), xs, True, True).then_inc(second_full, 1)

            def spread(c, b):
                if f.dense or b == f.plain_block or b % f.spread_every:
                    return
                n = block_no(f, c, b)
                if b == 0:
                    pe.wait_ge(weights_sb, f.router0 + c + 1)
                if in_stage(f, c, b, 1):
                    pe.wait_ge(h_ready, n)
                o = EXACT_AT["sel16"][0] + b // f.spread_every * P
                nc.tensor.matmul(SP[:, :], WE[0:2 * NH, o:o + P], SCT[0:2 * NH, bass.ds(c % 2 * CH, CH)],
                                 start=True, stop=True).then_inc(spread_full, 1)

            def down(c, b):
                n = block_no(f, c, b)
                if b == 0:
                    y_bank_free(pe, f.tail, c)
                    if f.experts == 8:
                        s = SCT[0:2 * NH, bass.ds(c % 2 * CH, CH)]
                        bh, bl = wh("b2_2")
                        nc.tensor.matmul(Y[:, :], bh[0:2 * NH, :], s, start=True, stop=False)
                        nc.tensor.matmul(Y[:, :], bl[0:2 * NH, :], s, start=False, stop=False)
                pe.wait_ge(hl_ready, n + 1)
                mm3(Y[:, :], wh(f.down, b * P), (rbuf[n % 2][:, :], rbuf[2 + n % 2][:, :]),
                    b == 0 and f.experts != 8, b == f.blocks - 1).then_inc(down_done, 1)

            for b in range(f.blocks):
                up(c, b)
                for at_ in lagged(f, c, b, 1 if f.gate else 0):
                    spread(*at_)
                for at_ in lagged(f, c, b, f.lag):
                    down(*at_)
                hooks(f, c, b, hook, 0)

        def ffn_act(a, chain, f, c, hook):
            if c == 0:
                body_start(a, f.tail, 0)

            def act(c, b):
                n = block_no(f, c, b)
                a.wait_ge(first_full, n + 1)
                if in_stage(f, c, b, 2):
                    a.wait_ge(hl_ready if f.dense else mul_done if f.gate else h_ready, n - 1)
                if f.gate:
                    nc.scalar.activation(AO[n % 2], G[n % 2][:, :], ACT.Silu).then_inc(act_done, 1)
                else:
                    bias = {"ffn2": "b1_2", "ffn3": "b1_3", "ffn4": "fb1"}[f.key]
                    nc.scalar.activation(AO[n % 2], G[n % 2][:, :], ACT.Relu, bias=raw(bias, b, 1))\
                        .then_inc(act_done, 1)

            def high(c, b):
                n = block_no(f, c, b)
                a.wait_ge(h_ready, n + 1)
                if in_stage(f, c, b, 2):
                    a.wait_ge(down_done, n - 1)
                nc.scalar.activation(rbuf[n % 2][:, :], HO[n % 3], ACT.Copy).then_inc(hh_ready, 1)

            def result(c):
                yt_free(a, f.tail, c)
                a.wait_ge(down_done, block_no(f, c, f.blocks - 1) + 1)
                bias = {"ffn3": raw("b2_3"), "ffn4": raw("fb2")}.get(f.key, zero)
                nc.scalar.activation(YT[:, :], Y[:, :], ACT.Identity, bias=bias).then_inc(yt_ready, 1)

            for b in range(f.blocks):
                act(c, b)
                if c and b == f.lag - f.early:
                    result(c - 1)
                if not f.dense:
                    for at_ in lagged(f, c, b, 2 if f.gate else 1):
                        high(*at_)
                hooks(f, c, b, hook, 0)
            if c == NC - 1:
                result(c)

        def ffn_dve(v, chain, f, c, hook):
            if c == 0:
                body_start(v, f.tail, 0)

            def gate(c, b):
                n = block_no(f, c, b)
                v.wait_ge(act_done, n + 1)
                v.wait_ge(second_full, n + 1)
                if in_stage(f, c, b, 2):
                    v.wait_ge(h_ready, n - 1)
                nc.vector.tensor_tensor(MO[n % 2], AO[n % 2], U[n % 2][:, :], ALU.mult).then_inc(mul_done, 1)

            def weigh(c, b):
                n = block_no(f, c, b)
                v.wait_ge(mul_done if f.gate else act_done, n + 1)
                if in_stage(f, c, b, 3):
                    v.wait_ge(hl_ready, n - 2)
                src = MO[n % 2] if f.gate else AO[n % 2]
                if b == f.plain_block:
                    nc.vector.tensor_copy(HO[n % 3], src).then_inc(h_ready, 1)
                else:
                    v.wait_ge(spread_full, f.spread0 + f.spread * c + b // f.spread_every + 1)
                    nc.vector.tensor_tensor(HO[n % 3], src, SP[:, :], ALU.mult).then_inc(h_ready, 1)

            def split(c, b):
                n = block_no(f, c, b)
                v.wait_ge(act_done, n + 1)
                if in_stage(f, c, b, 2):
                    v.wait_ge(down_done, n - 1)
                nc.vector.tensor_copy(rbuf[n % 2][:, :], AO[n % 2]).then_inc(hh_ready, 1)
                low(nc.vector, v, f, n)

            for b in range(f.blocks):
                if f.gate:
                    gate(c, b)
                    for at_ in lagged(f, c, b, 1):
                        weigh(*at_)
                elif f.dense:
                    split(c, b)
                else:
                    weigh(c, b)
                hooks(f, c, b, hook, 1)

        def low(e_, eng, f, n):
            eng.wait_ge(hh_ready, n + 1)
            e_.tensor_tensor(rbuf[2 + n % 2][:, :], AO[n % 2] if f.dense else HO[n % 3],
                             rbuf[n % 2][:, :].bitcast(F32), ALU.subtract).then_inc(hl_ready, 1)

        def ffn_pool(g, chain, f, c, hook, work):
            for b in range(f.blocks):
                if not f.dense:
                    for at_ in lagged(f, c, b, 2):
                        low(nc.gpsimd, g, f, block_no(f, *at_))
                hooks(f, c, b, hook, 0)


        def stage0_pe(pe, c, hook):
            if c == 0:
                pe.wait_ge(made_ready, 1)
                pe.wait_ge(xl_ready, NC)
            y_bank_free(pe, 0, c)
            for k in range(TAPS):
                mm3(Y[:, :], wh("taps", k * P), (chunk(XH, c, k), chunk(XL, c, k)), k == 0, False)
            pe.wait_ge(s_low, c + 1)
            mm3(Y[:, :], wh("wt0s"), (rbuf[0][:, :], rbuf[1][:, :]), False, True).then_inc(y_full, 1)

        def stage0_act(a, chain, c, hook):
            yt_free(a, 0, c)
            a.wait_ge(y_full, c + 1)
            nc.scalar.activation(YT[:, :], Y[:, :], ACT.Identity, bias=bias0).then_inc(yt_ready, 1)

        def stage0_dve(v, chain, c, hook):
            if c:
                v.wait_ge(y_full, c)
            nc.vector.tensor_copy(rbuf[0][:, :], chunk(S0, c)).then_inc(s_high, 1)
            v.wait_ge(s_high, c + 1)
            nc.vector.tensor_tensor(rbuf[1][:, :], chunk(S0, c), rbuf[0][:, :].bitcast(F32), ALU.subtract)\
                .then_inc(s_low, 1)

        UN = 2 * TL
        rows_done = sem("rows_done")
        GR = 2 * NH
        sqq, sqk, qn, kn, QN, qc, kc = (buf[i_] for i_ in (0, 1, 0, 1, 2, 4, 5))
        sdev, rstd = buf[3][0:GR, :], buf[6][0:GR, :]
        KM = [buf[6 + j] for j in range(4)]
        VTD = B[:, 10:12, :].rearrange("p a b -> p (a b)").rearrange("p (w s t) -> p w s t", s=2, t=WIN)
        PRB = [buf[0], buf[1]]
        PT = [buf[3], buf[4]]
        AT = buf[5]
        HU = NH // 2

        def attn_pe(pe, c, hook):
            t = 2
            body_start(pe, t, c)
            hook(-1)
            y_bank_free(pe, t, c)
            xs = (chunk(XH, c, PAD), chunk(XL, c, PAD))
            if c == 0:
                pe.wait_ge(made_ready, 1)
                pe.wait_ge(piece_ready, READY_AT["wv1"])
            pe.wait_ge(xl_ready, count(2, c) + 1)
            mm3(G[0][:, :], wh("wqk1c", 0), xs, True, True).then_inc(qkv_full, 1)
            mm3(G[1][:, :], wh("wqk1c", P), xs, True, True).then_inc(qkv_full, 1)
            mm3(U[0][:, :], wh("wv1"), xs, True, True).then_inc(qkv_full, 1)
            pe.wait_ge(squares, 2 * c + 1)
            nc.tensor.matmul(U[1][0:GR, :], raw("mean_q"), sqq, start=True, stop=False)
            pe.wait_ge(squares, 2 * c + 2)
            nc.tensor.matmul(U[1][0:GR, :], raw("mean_k"), sqk, start=False, stop=True).then_inc(var_full, 1)
            pe.wait_ge(v_copied, c + 1)
            pe.wait_ge(var_read, c + 1)
            for w in range(CH // WIN):
                i = nc.tensor.transpose(U[w // 4][:, w % 4 * P:(w % 4 + 1) * P],
                                        VTD[:, w, :, :].rearrange("p s t -> p (s t)"), ident)
            i.then_inc(v_turned, 1)
            pe.wait_ge(rstd_qk, c + 1)
            nc.tensor.matmul(SP[:, :], raw("spread_q")[0:GR, :], rstd, start=True, stop=True).then_inc(rstd_full, 1)
            nc.tensor.matmul(Y[:, :], raw("spread_k")[0:GR, :], rstd, start=True, stop=True).then_inc(rstd_full, 1)

            def scores(n):
                i_, u = n // 2, n % 2
                if n == 0:
                    pe.wait_ge(qk_ready, c + 1)
                if n >= 2:
                    pe.wait_ge(s_read, c * UN + n - 1)
                for hl in range(HU):
                    h = HU * u + hl
                    g_, j = h // 4, h % 4
                    if hl == 4:
                        i.then_inc(rows_done, 1)
                        pe.wait_ge(rows_done, c * UN + n + 1)
                    for w in range(2):
                        tok = slice(i_ * P + w * WIN, i_ * P + (w + 1) * WIN)
                        i = nc.tensor.matmul(G[u][w * WIN:(w + 1) * WIN, hl * WIN:(hl + 1) * WIN],
                                             QN[32 * g_:32 * g_ + 32, tok], KM[j][32 * g_:32 * g_ + 32, tok],
                                             start=True, stop=True)
                i.then_inc(s_full, 1)

            def turn(n):
                u = n % 2
                pe.wait_ge(p_ready, c * UN + n + 1)
                if n == 0:
                    pe.wait_ge(v_placed, c + 1)
                if n >= 2:
                    pe.wait_ge(pt_ready, c * UN + n - 1)
                for q in range(4):
                    i = nc.tensor.transpose(U[u][:, q * P:(q + 1) * P], PRB[u][:, q * P:(q + 1) * P], ident)
                i.then_inc(p_turned, 1)

            def weigh(n):
                i_, u = n // 2, n % 2
                pe.wait_ge(pt_ready, c * UN + n + 1)
                if u == 0 and i_:
                    pe.wait_ge(o_read, c * TL + i_)
                for q in range(4):
                    pr = 4 * u + q
                    i = nc.tensor.matmul(SP[:, pr * 36:(pr + 1) * 36], PT[u][:, q * P:(q + 1) * P],
                                         VB[:, i_, pr, :, :, :].rearrange("p a b d -> p (a b d)"),
                                         start=True, stop=True)
                i.then_inc(o_full, 1)

            scores(0)
            for n in range(UN):
                if n + 1 < UN:
                    scores(n + 1)
                turn(n)
                if n:
                    weigh(n - 1)
                hook(n)
            weigh(UN - 1)
            attn_project_pe(pe, c)

        def attn_project_pe(pe, c):
            pe.wait_ge(o_read, (c + 1) * TL)
            pe.wait_ge(s_read, (c + 1) * UN)
            for j in range(TL):
                i = nc.tensor.transpose(G[0][:, j * P:(j + 1) * P], AT[:, j * P:(j + 1) * P], ident)
            i.then_inc(a_turned, 1)
            pe.wait_ge(piece_ready, READY_AT["wproj"])
            y_bank_free(pe, 2, c)
            pe.wait_ge(al_ready, c + 1)
            mm3(Y[:, :], wh("wproj"), (rbuf[0][:, :], rbuf[1][:, :]), True, True).then_inc(y_full, 1)

        def attn_project_act(a, c):
            a.wait_ge(a_turned, c + 1)
            nc.scalar.activation(buf[11], G[0][:, :], ACT.Copy).then_inc(a32_ready, 1)
            yt_free(a, 2, c)
            a.wait_ge(y_full, count_y(2, c) + 1)
            nc.scalar.activation(YT[:, :], Y[:, :], ACT.Identity, bias=raw("bproj")).then_inc(yt_ready, 1)

        def attn_project_dve(v, c):
            v.wait_ge(a32_ready, c + 1)
            nc.vector.tensor_copy(rbuf[0][:, :], buf[11]).then_inc(ah_ready, 1)
            v.wait_ge(ah_ready, c + 1)
            nc.vector.tensor_tensor(rbuf[1][:, :], buf[11], rbuf[0][:, :].bitcast(F32), ALU.subtract)\
                .then_inc(al_ready, 1)

        def attn_act(a, chain, c, hook):
            body_start(a, 2, c)
            a.wait_ge(qkv_full, 3 * c + 1)
            nc.scalar.activation(sqq, G[0][:, :], ACT.Square).then_inc(squares, 1)
            nc.scalar.activation(qc, G[0][:, :], ACT.Copy)
            a.wait_ge(qkv_full, 3 * c + 2)
            nc.scalar.activation(sqk, G[1][:, :], ACT.Square).then_inc(squares, 1)
            nc.scalar.activation(kc, G[1][:, :], ACT.Copy).then_inc(centred, 1)
            a.wait_ge(qkv_full, 3 * c + 3)
            for s_ in range(2):
                i = nc.scalar.activation(VTD[:, :, s_, :], U[0][:, :].rearrange("p (w t) -> p w t", t=WIN), ACT.Copy)
            i.then_inc(v_copied, 1)
            a.wait_ge(var_full, c + 1)
            nc.scalar.activation(sdev, U[1][0:GR, :], ACT.Sqrt, bias=epsv[0:GR, :]).then_inc(var_read, 1)
            a.wait_ge(v_turned, c + 1)
            for b_ in range(2):
                src = U[b_][:, :].rearrange("p (i w q h d) -> p i w q h d", i=2, w=2, q=HU, h=2)
                for s_ in range(2):
                    rows = slice(64 * s_, 64 * s_ + 64)
                    for i_ in range(2):
                        for w in range(2):
                            i = nc.scalar.activation(VB[rows, 2 * b_ + i_, :, w, s_, 0:HD],
                                                     src[rows, i_, w, :, s_, :], ACT.Copy)
            i.then_inc(v_placed, 1)

            def probs(n):
                a.wait_ge(sub_done, c * UN + n + 1)
                nc.scalar.activation(PRB[n % 2], PRB[n % 2], ACT.Exp).then_inc(p_ready, 1)

            def evac(n):
                a.wait_ge(p_turned, c * UN + n + 1)
                if n >= 2:
                    a.wait_ge(o_full, c * UN + n - 1)
                nc.scalar.activation(PT[n % 2], U[n % 2][:, :], ACT.Copy).then_inc(pt_ready, 1)

            probs(0)
            for n in range(UN):
                if n + 1 < UN:
                    probs(n + 1)
                evac(n)
                hook(n)
            attn_project_act(a, c)

        sub_done = s_read

        def attn_dve(v, chain, c, hook):
            body_start(v, 2, c)
            hook(-1)
            v.wait_ge(var_read, c + 1)
            nc.vector.reciprocal(rstd, sdev).then_inc(rstd_qk, 1)
            v.wait_ge(centred, c + 1)
            v.wait_ge(rstd_full, 2 * c + 1)
            nc.vector.tensor_tensor(qn, qc, SP[:, :], ALU.mult).then_inc(qk_read, 1)
            v.wait_ge(qk_read, 2 * c + 1)
            nc.vector.tensor_scalar(QN, qn, raw("ln_g1"), raw("ln_b1"), ALU.mult, ALU.add)
            v.wait_ge(rstd_full, 2 * c + 2)
            nc.vector.tensor_tensor(kn, kc, Y[:, :], ALU.mult).then_inc(qk_read, 1)
            v.wait_ge(qk_read, 2 * c + 2)
            for j in range(4):
                i = nc.vector.tensor_scalar(KM[j], kn, gm[j], bm[j], ALU.mult, ALU.add)
            i.then_inc(qk_ready, 1)
            v.wait_ge(qk_ready, c + 1)

            def finish(i_):
                v.wait_ge(o_full, c * UN + 2 * i_ + 2)
                O = SP[:, 0:HU * 36].rearrange("p (q w h d) -> p q w h d", q=HU, w=2, h=2)
                for w in range(2):
                    rows = slice(64 * w, 64 * w + 64)
                    i = nc.vector.reciprocal(orec[rows, :].rearrange("p (q h) -> p q h", h=2),
                                             O[rows, :, w, :, HD])
                chain(i)
                for w in range(2):
                    rows = slice(64 * w, 64 * w + 64)
                    for h2 in range(2):
                        i = nc.vector.tensor_tensor(
                            AT[rows, i_ * P:(i_ + 1) * P].rearrange("p (q h d) -> p q h d", h=2, d=HD)[:, :, h2, :],
                            O[rows, :, w, h2, 0:HD],
                            bcast(orec[rows, :].rearrange("p (q h) -> p q h", h=2)[:, :, h2].unsqueeze(2),
                                  [64, HU, HD]), ALU.mult)
                i.then_inc(o_read, 1)

            for n in range(UN):
                u = n % 2
                v.wait_ge(s_full, c * UN + n + 1)
                Sv = G[u][:, :].rearrange("p (h k) -> p h k", k=WIN)
                chain(nc.vector.tensor_reduce(amax[:, HU * u:HU * u + HU], Sv, AX.X, ALU.max))
                if n >= 2:
                    v.wait_ge(p_turned, c * UN + n - 1)
                nc.vector.tensor_tensor(PRB[u].rearrange("p (h k) -> p h k", k=WIN), Sv,
                                        bcast(amax[:, HU * u:HU * u + HU].unsqueeze(2), [P, HU, WIN]), ALU.subtract)\
                    .then_inc(s_read, 1)
                if n:
                    hook(n - 1)
                if u == 1 and n > 1:
                    finish(n // 2 - 1)
            hook(UN - 1)
            finish(TL - 1)
            attn_project_dve(v, c)

        def attn_pool(g, chain, c, hook, work):
            for n in range(UN):
                hook(n)
                work()

        def scan_pe(pe, c, hook):
            body_start(pe, 4, c)
            xs = (chunk(XH, c, PAD), chunk(XL, c, PAD))
            pe.wait_ge(piece_ready, READY_AT["wqkva"])
            pe.wait_ge(xl_ready, count(4, c) + 1)
            mm3(U[0][:, :], wh("wqkva", 2 * P), xs, True, True).then_inc(scan_in, 1)
            mm3(G[1][:, :], wh("wqkva", P), xs, True, True).then_inc(scan_in, 1)
            mm3(G[0][:, :], wh("wqkva", 0), xs, True, True).then_inc(scan_in, 1)

        def scan_act(a, chain, c, hook):
            body_start(a, 4, c)
            a.wait_ge(scan_in, 3 * c + 1)
            nc.scalar.activation(buf[0], U[0][:, :], ACT.Sigmoid).then_inc(sig_ready, 1)

        def scan_dve(v, chain, c, hook):
            body_start(v, 4, c)
            v.wait_ge(sig_ready, c + 1)
            v.wait_ge(scan_in, 3 * c + 2)
            chain(nc.vector.tensor_tensor_scan(buf[1], buf[0], G[1][:, :], 0.0 if c == 0 else carry,
                                               ALU.mult, ALU.add))
            chain(nc.vector.tensor_copy(carry, buf[1][:, CH - 1:CH]))
            v.wait_ge(scan_in, 3 * c + 3)
            yt_free(v, 4, c)
            nc.vector.tensor_tensor(YT[:, :], buf[1], G[0][:, :], ALU.mult).then_inc(yt_ready, 1)

        UL = 16
        UALL = 2 * NC * UL
        TB = [G[0], G[1], U[0]]
        AHEAD = len(TB)
        PB = U[1]
        TURNED = [PB, TN]
        KVB = [SP, R]
        OB = [SP, R]
        MB = [buf[0], buf[1]]
        RB = [buf[2], buf[3]]
        AB = [buf[4], buf[5]]
        SN = [buf[6], buf[7]]
        CS = [buf[8], buf[9]]
        P32 = [buf[10], buf[11]]
        FH, FL = wh("w1_2", 0, 4 * CH)
        V4 = STG[:, 0:2, :]
        A32 = VT3 = STG[:, 2, :]
        KS = [FL.rearrange("p (g t) -> p g t", g=4),
              FH.rearrange("p (g t) -> p g t", g=4)]
        TURN = 2.0 * float(np.pi)
        VSTEP = 4

        def proj_no(cp, s_):
            return min(cp, NC) * 5 + max(0, cp - NC) * 4 + s_

        def lin_proj_pe(pe, cp, s_):
            c = cp % NC
            xs = (chunk(XH, c, PAD), chunk(XL, c, PAD))
            k = proj_no(cp, s_)
            if s_ == 0:
                pe.wait_ge(xl_ready, count(6, c) + 1)
            if k:
                pe.wait_ge(proj_sb, k)
            if cp and s_ == 0:
                pe.wait_ge(v4_ready, min(cp, NC))
            if s_ == VSTEP:
                mm3(PB[:, :], wh("wv3"), xs, True, True).then_inc(proj_full, 1)
            else:
                mm3(PB[:, :], wh("wk3" if cp < NC else "wq3", s_ * P), xs, True, True).then_inc(proj_full, 1)

        def lin_turn_pe(pe, cp):
            k = proj_no(cp, VSTEP)
            pe.wait_ge(proj_sb, k + 1)
            for j in range(TL):
                i = nc.tensor.transpose(PB[:, j * P:(j + 1) * P], VT3[:, j * P:(j + 1) * P], ident)
            i.then_inc(vt_turned, 1)

        def lin_turn_act(a, cp):
            k = proj_no(cp, VSTEP)
            a.wait_ge(vt_turned, cp + 1)
            if cp >= 2:
                a.wait_ge(unit_used, UL * (cp - 1))
            nc.scalar.activation(V4[:, cp % 2, :], PB[:, :], ACT.Copy).then_inc(v4_ready, 1)

        def lin_proj_act(a, cp, s_):
            k = proj_no(cp, s_)
            a.wait_ge(proj_full, k + 1)
            if s_ == VSTEP:
                if cp >= 1:
                    a.wait_ge(vt_turned, cp)
                nc.scalar.activation(VT3[:, :], PB[:, :], ACT.Identity, bias=raw("bv")).then_inc(proj_sb, 1)
                return
            if 4 * cp + s_ >= 2:
                a.wait_ge(ks_ready, 4 * cp + s_ - 1)
            nc.scalar.activation(P32[s_ % 2], PB[:, :], ACT.Identity,
                                 bias=raw("bk4" if cp < NC else "bq4", s_, 1)).then_inc(proj_sb, 1)

        def lin_split(g, cp, s_):
            if s_ == VSTEP:
                return
            g.wait_ge(proj_sb, proj_no(cp, s_) + 1)
            if cp >= 2 and s_ == 0:
                g.wait_ge(t_full, UL * (cp - 1))
            dst, lo = KS[cp % 2][:, s_, :], slice(P // 2, P)
            nc.gpsimd.tensor_scalar(dst, P32[s_ % 2], 1.0, 0.0, ALU.mult, ALU.add).then_inc(ks_high, 1)
            g.wait_ge(ks_high, 4 * cp + s_ + 1)
            nc.gpsimd.tensor_tensor(dst[lo, :], P32[s_ % 2][lo, :], dst[lo, :].bitcast(F32), ALU.subtract)\
                .then_inc(ks_ready, 1)
            g.wait_ge(ks_ready, 4 * cp + s_ + 1)

        def lin_phases(pe, q):
            cp, n = q // UL, q % UL
            if q >= UALL:
                return
            pe.wait_ge(ks_ready, 4 * cp + (4 if n else 1) if cp >= NC or n == 0 else 4 * cp + 4)
            if q >= AHEAD:
                pe.wait_ge(r_ready, q - AHEAD + 1)
            if cp < NC:
                i_, g_ = n // 4, n % 4
                nc.tensor.matmul(TB[q % AHEAD][:, :], KS[cp % 2][:, g_, i_ * P:(i_ + 1) * P],
                                 WM[:, :, :].rearrange("p j m -> p (j m)"),
                                 start=True, stop=True).then_inc(t_full, 1)
            else:
                g_, j = n // 4, n % 4
                nc.tensor.matmul(TB[q % AHEAD][:, :], WM[:, j, :], KS[cp % 2][:, g_, :],
                                 start=True, stop=True).then_inc(t_full, 1)

        def lin_use(pe, q):
            cp, n = q // UL, q % UL
            if cp < NC:
                i_, g_ = n // 4, n % 4
                rows = slice(32 * g_, 32 * g_ + 32)
                if n == 0:
                    pe.wait_ge(v4_ready, cp + 1)
                for s_, src in enumerate((CS, SN)):
                    if s_ == 0:
                        pe.wait_ge(cos_ready, q + 1)
                    else:
                        pe.wait_ge(sin_ready, q + 1)
                    i = nc.tensor.matmul(KVB[s_][rows, :], V4[:, cp % 2, i_ * P + 32 * g_:i_ * P + 32 * g_ + 32],
                                         src[q % 2], start=q < 4, stop=q >= NC * UL - 4)
                i.then_inc(unit_used, 1)
            else:
                c, g_, j = cp - NC, n // 4, n % 4
                rows = slice(32 * g_, 32 * g_ + 32)
                if n == 0:
                    if c == 0:
                        pe.wait_ge(kv_ready, 1)
                    if c >= 2:
                        pe.wait_ge(oq_read, c - 1)
                for s_, src in enumerate((CS, SN)):
                    if s_ == 0:
                        pe.wait_ge(cos_ready, q + 1)
                    else:
                        pe.wait_ge(sin_ready, q + 1)
                    i = nc.tensor.matmul(OB[c % 2][rows, :], KVT[:, s_, j, rows], src[q % 2],
                                         start=j == 0 and s_ == 0, stop=j == 3 and s_ == 1)
                i.then_inc(unit_used, 1)

        def rounds_on_act(q):
            return q % 2 == 0

        def lin_round_act(a, q):
            if q < UALL and rounds_on_act(q):
                a.wait_ge(t_full, q + 1)
                if q >= 2:
                    a.wait_ge(r_ready, q - 1)
                nc.scalar.activation(MB[q % 2], TB[q % AHEAD][:, :], ACT.Identity, bias=roundv).then_inc(m_ready, 1)

        def lin_round_dve(v, q):
            if q < UALL and not rounds_on_act(q):
                v.wait_ge(t_full, q + 1)
                if q >= 2:
                    v.wait_ge(r_ready, q - 1)
                nc.vector.tensor_scalar(MB[q % 2], TB[q % AHEAD][:, :], ROUND, None, ALU.add).then_inc(m_ready_dve, 1)

        def rounded(v, q):
            acts = (q + 2) // 2
            if rounds_on_act(q):
                v.wait_ge(m_ready, acts)
            else:
                v.wait_ge(m_ready_dve, q + 1 - acts)

        def lin_abs(v, q):
            v.wait_ge(r_ready, q + 1)
            if q >= 2:
                v.wait_ge(cos_ready, q - 1)
            nc.vector.tensor_scalar(AB[q % 2].bitcast(U32), RB[q % 2].bitcast(U32), 0x7fffffff, None,
                                    ALU.bitwise_and).then_inc(ab_ready, 1)

        def lin_pool(g, cp, hook):
            if cp == 0:
                body_start(g, 6, 0)
                for s_ in lin_projects(0):
                    lin_split(g, 0, s_)
            for n in range(UL):
                if n - 2 in PROJ_AT and PROJ_AT[n - 2] in lin_projects(cp + 1):
                    lin_split(g, cp + 1, PROJ_AT[n - 2])
                lin_hooks(n, hook, 2)

        def lin_trig(a, q):
            a.wait_ge(ab_ready, q + 1)
            if q >= 2:
                a.wait_ge(unit_used, q - 1)
            nc.scalar.activation(CS[q % 2], AB[q % 2], ACT.Sin, scale=-TURN, bias=half_pi).then_inc(cos_ready, 1)
            nc.scalar.activation(SN[q % 2], RB[q % 2], ACT.Sin, scale=-TURN).then_inc(sin_ready, 1)

        def lin_rest(v, chain, q):
            rounded(v, q)
            if q >= 2:
                v.wait_ge(sin_ready, q - 1)
            nc.vector.scalar_tensor_tensor(RB[q % 2], MB[q % 2], ROUND, TB[q % AHEAD][:, :],
                                           ALU.subtract, ALU.subtract).then_inc(r_ready, 1)
            lin_round_dve(v, q + 1)
            lin_abs(v, q)

        PROJ_AT = {8 + s_: s_ for s_ in range(5)}

        def lin_projects(cp):
            return range(5 if cp < NC else 4) if cp < 2 * NC else range(0)

        def lin_hooks(n, hook, tail_at):
            if n == tail_at:
                hook(-1)
            if n % 2 and n < 8 or n in (8, 10, 12, 14):
                hook({1: 0, 3: 1, 5: 2, 7: 3}.get(n, n // 2))

        def lin_pe(pe, cp, hook):
            if cp == 0:
                body_start(pe, 6, 0)
                pe.wait_ge(piece_ready, READY_AT["wo3"])
                pe.wait_ge(phase_weights, 1)
                for s_ in lin_projects(0):
                    lin_proj_pe(pe, 0, s_)
                lin_turn_pe(pe, 0)
                for q in range(AHEAD):
                    lin_phases(pe, q)
            for n in range(UL):
                q = UL * cp + n
                if cp == NC and n == 0:
                    pe.wait_ge(kvf_ready, 1)
                    pe.wait_ge(proj_sb, proj_no(NC, 4))
                    pe.wait_ge(x32_ready, turned["norms"])
                    pe.wait_ge(res_done, turned["tails"])
                    for s_ in range(2):
                        for j in range(4):
                            i = nc.tensor.transpose(TURNED[s_][:, j * P:(j + 1) * P], V4[:, s_, j * P:(j + 1) * P], ident)
                    i.then_inc(kv_turned, 1)
                lin_phases(pe, q + AHEAD)
                lin_use(pe, q)
                if n in PROJ_AT and PROJ_AT[n] in lin_projects(cp + 1):
                    if cp == NC and n == 8:
                        pe.wait_ge(kv_ready, 1)
                    lin_proj_pe(pe, cp + 1, PROJ_AT[n])
                if n == 14 and cp + 1 < NC:
                    lin_turn_pe(pe, cp + 1)
                if n == 2 and cp > NC:
                    project_pe(pe, cp - NC - 1)
                lin_hooks(n, hook, 6 if cp > NC else 1)
            if cp == 2 * NC - 1:
                project_pe(pe, NC - 1)

        def lin_act(a, cp, hook):
            if cp == 0:
                body_start(a, 6, 0)
                a.wait_ge(piece_ready, len(PIECES))
                for s_ in lin_projects(0):
                    lin_proj_act(a, 0, s_)
                lin_turn_act(a, 0)
                for q in range(2):
                    lin_round_act(a, q)
            if cp == NC:
                a.wait_ge(unit_used, NC * UL)
                for s_ in range(2):
                    i = nc.scalar.activation(V4[:, s_, :], KVB[s_][:, :], ACT.Copy, scale=1.0 / P)
                i.then_inc(kvf_ready, 1)
            for n in range(UL):
                q = UL * cp + n
                lin_round_act(a, q + 2)
                lin_trig(a, q)
                if n - 1 in PROJ_AT and PROJ_AT[n - 1] in lin_projects(cp + 1):
                    lin_proj_act(a, cp + 1, PROJ_AT[n - 1])
                if n == 15 and cp + 1 < NC:
                    lin_turn_act(a, cp + 1)
                if n == 1 and cp > NC:
                    output_act(a, cp - NC - 1)
                if n == 4 and cp > NC:
                    project_act(a, cp - NC - 1)
                lin_hooks(n, hook, 6)
            if cp == 2 * NC - 1:
                output_act(a, NC - 1)
                project_act(a, NC - 1)

        def lin_dve(v, chain, cp, hook):
            if cp == 0:
                body_start(v, 6, 0)
            for n in range(UL):
                q = UL * cp + n
                if q == 0:
                    lin_round_dve(v, 0)
                lin_rest(v, chain, q)
                if cp == NC and n == 1:
                    v.wait_ge(kv_turned, 1)
                    for s_ in range(2):
                        for j in range(4):
                            at_ = lambda ap2: ap2.rearrange("p (g k d) -> p g k d", g=4, d=HD)[:, :, j, :]
                            i = nc.vector.tensor_copy(at_(KVT[:, s_, j, :]), at_(TURNED[s_][:, j * P:(j + 1) * P]))
                    i.then_inc(kv_ready, 1)
                if n == 2 and cp > NC:
                    project_dve(v, cp - NC - 1)
                lin_hooks(n, hook, 7 if cp > NC else 2)
            if cp == 2 * NC - 1:
                project_dve(v, NC - 1)

        def output_act(a, c):
            a.wait_ge(unit_used, UL * (NC + c + 1))
            if c == 0:
                a.wait_ge(vt_turned, NC)
            else:
                a.wait_ge(al_ready, NC + c)
            nc.scalar.activation(A32[:, :], OB[c % 2][:, :], ACT.Copy).then_inc(oq_read, 1)

        def project_pe(pe, c):
            y_bank_free(pe, 6, c)
            pe.wait_ge(al_ready, NC + c + 1)
            mm3(Y[:, :], wh("wo3"), (rbuf[0][:, :], rbuf[1][:, :]), True, True).then_inc(y_full, 1)

        def project_act(a, c):
            yt_free(a, 6, c)
            a.wait_ge(y_full, count_y(6, c) + 1)
            nc.scalar.activation(YT[:, :], Y[:, :], ACT.Identity, bias=raw("bo")).then_inc(yt_ready, 1)

        def project_dve(v, c):
            v.wait_ge(oq_read, c + 1)
            if c:
                v.wait_ge(y_full, count_y(6, c))
            nc.vector.tensor_copy(rbuf[0][:, :], A32[:, :]).then_inc(ah_ready, 1)
            v.wait_ge(ah_ready, NC + c + 1)
            nc.vector.tensor_tensor(rbuf[1][:, :], A32[:, :], rbuf[0][:, :].bitcast(F32), ALU.subtract)\
                .then_inc(al_ready, 1)

        roundv = VEC[:, 17:18]

        STAGES_ = [
            ("stage0", 0, 0), (FFN0, 1, 1), ("attn", 2, 2), (FFN1, 3, 3), ("scan", 4, 4), (FFN2, 5, 5),
            ("keys", None, 6), ("queries", 6, None), (FFN3, 7, 7), (FFN4, 8, 8),
        ]

        def slots():
            tails = []
            for s_, (body, t, n) in enumerate(STAGES_):
                for c in range(NC):
                    tail = tails.pop() if tails else None
                    if t is not None:
                        tails.append((t, c))
                    if c < NC - 1:
                        front = (n, c + 1) if n is not None and n > 0 else None
                    else:
                        nxt = STAGES_[s_ + 1][2] if s_ + 1 < len(STAGES_) else None
                        front = (nxt, 0) if nxt is not None else None
                    yield body, c, tail, front

        BODY = {
            "stage0": (stage0_pe, stage0_act, stage0_dve), "attn": (attn_pe, attn_act, attn_dve),
            "scan": (scan_pe, scan_act, scan_dve),
            "keys": (lin_pe, lin_act, lin_dve),
            "queries": tuple((lambda *args, f_=f_: f_(*args[:-2], NC + args[-2], args[-1]))
                             for f_ in (lin_pe, lin_act, lin_dve)),
        }
        HOOKED = ("attn", "keys", "queries")

        def walk(which, eng, chain, do_front, do_tail):
            for body, c, tail, front in slots():
                def hook(pos):
                    if pos == -1:
                        if tail:
                            do_tail(*tail)
                    elif front:
                        do_front(*front, pos)
                if isinstance(body, Ffn):
                    (ffn_pe, ffn_act, ffn_dve)[which](*([eng] + ([chain] if which else []) + [body, c, hook]))
                else:
                    if body not in HOOKED:
                        hook(-1)
                    args = [c, hook]
                    BODY[body][which](*([eng] + ([chain] if which == 2 or which == 1 and body not in ("keys", "queries") else []) + args))
                    if body not in HOOKED:
                        for pos in range(8):
                            hook(pos)

        block = ctx.enter_context(nc.Block())

        @block.sync
        def _(sp):
            for c in range(NC):
                sp.dma_start(tiles(X, c), x_in[bass.ts(c, CH), :].rearrange("(t p) d -> p t d", p=P))\
                    .then_inc(x_loaded[c], 16)
                if c == 0:
                    sp.dma_start(WR[:, :], w_raw).then_inc(raw_loaded, 16)
            for i, (_, kind, _, _, col, n) in enumerate(PIECES):
                if i >= STAGES:
                    sp.wait_ge(piece_ready, i - STAGES + 1)
                src = w_split if kind == "split" else w_exact
                sp.dma_start(STG[:, i % STAGES, 0:n], src[:, col:col + n]).then_inc(piece_loaded[i % STAGES], 16)
            for c in range(NC):
                sp.wait_ge(res_done, count(8, c) + 1)
                sp.dma_start(out[bass.ts(c, CH), :].rearrange("(t p) d -> p t d", p=P), tiles(X, c))\
                    .then_inc(out_stored, 16)
            sp.wait_ge(out_stored, 16 * NC)

        @block.gpsimd
        def _(g):
            chain = Chain(g, pool_chain)
            state = [0]

            def work(limit):
                i = state[0]
                if i >= len(PIECES) or PIECES[i][0] > limit:
                    return
                state[0] += 1
                _, kind, _, at_, _, n = PIECES[i]
                g.wait_ge(piece_loaded[i % STAGES], 16 * (i // STAGES + 1))
                if PIECES[i][0] == 2:
                    g.wait_ge(yt_ready, count(1, 3) + 1)
                if PIECES[i][0] == 3:
                    g.wait_ge(yt_ready, count(3, 3) + 1)
                s_ = STG[:, i % STAGES, 0:n]
                if kind == "exact":
                    nc.gpsimd.tensor_scalar(WE[:, at_:at_ + n], s_, 1.0, 0.0, ALU.mult, ALU.add)\
                        .then_inc(piece_ready, 1)
                else:
                    hi = WH[:, at_:at_ + n]
                    chain(nc.gpsimd.tensor_scalar(hi, s_, 1.0, 0.0, ALU.mult, ALU.add))
                    nc.gpsimd.tensor_tensor(WL[:, at_:at_ + n], s_, hi.bitcast(F32), ALU.subtract)\
                        .then_inc(piece_ready, 1)

            g.wait_ge(consts_ready, 1)
            for c in range(NC):
                front_pool(g, chain, 0, c, 0)
                work(0)
                work(0)
            while state[0] < len(PIECES) and PIECES[state[0]][0] == 0:
                work(0)
            for body, c, tail, front in slots():
                def hook(pos):
                    if pos >= 0 and front:
                        front_pool(g, chain, *front, pos)
                limit = {"stage0": 0, FFN0: 1, "attn": 2, FFN1: 2, "scan": 2, FFN2: 3}.get(body, 3)
                if isinstance(body, Ffn):
                    ffn_pool(g, chain, body, c, hook, lambda: None)
                    for _ in range(3):
                        work(limit)
                elif body in ("keys", "queries"):
                    lin_pool(g, c + (NC if body == "queries" else 0), hook)
                elif body == "attn":
                    attn_pool(g, chain, c, hook, lambda: work(limit))
                else:
                    for pos in range(8):
                        hook(pos)
                if c == NC - 1:
                    while state[0] < len(PIECES) and PIECES[state[0]][0] <= limit:
                        work(limit)

        @block.scalar
        def _(a):
            chain = Chain(a, act_chain)
            a.wait_ge(raw_loaded, 16)
            nc.scalar.activation(a_dec, raw("decay"), ACT.Sigmoid).then_inc(decay_ready, 1)
            a.wait_ge(consts_ready, 1)
            for c in range(NC):
                for pos in range(8):
                    front_act(a, chain, 0, c, pos)
            walk(1, a, chain, lambda n, c, pos: front_act(a, chain, n, c, pos), lambda t, c: None)

        @block.vector
        def _(v):
            chain = Chain(v, dve_chain)
            for ap, value in ((mhalf, -0.5), (half_pi, float(np.pi / 2)), (epsv, EPS), (zero, 0.0), (roundv, ROUND)):
                nc.vector.memset(ap, value)
            nc.vector.memset(KVT[:, :, :, :].rearrange("p s j m -> p (s j m)"), 0.0)
            WM32 = buf[11]
            nc.vector.memset(VB[:, :, :, :, :, :].rearrange("p i q w h d -> p (i q w h d)"), 0.0)
            for t_ in (XH, XL):
                nc.vector.memset(t_[:, 0:PAD].bitcast(F32), 0.0)
                chain(nc.vector.memset(t_[:, T + PAD:T + 2 * PAD].bitcast(F32), 0.0))
            for s_ in range(2):
                nc.vector.memset(VB[64 * s_:64 * s_ + 64, :, :, :, s_, HD].rearrange("p i q w -> p (i q) w"), 1.0)
            v.wait_ge(raw_loaded, 16)
            for j in range(4):
                mask = raw("head_of_4", j, 1)
                nc.vector.tensor_scalar(gm[j], raw("ln_g1"), mask, None, ALU.mult)
                nc.vector.tensor_scalar(bm[j], raw("ln_b1"), mask, None, ALU.mult)
                i = nc.vector.tensor_scalar(WM32[:, j * P:(j + 1) * P], raw("proj"), mask,
                                            1.0 / (float(np.sqrt(HD)) * 2.0 * float(np.pi)), ALU.mult, ALU.mult)
            chain(i)
            wm = WM[:, :, :].rearrange("p j m -> p (j m)")
            chain(nc.vector.tensor_copy(wm, WM32))
            for r_ in (32, 96):
                i = nc.vector.tensor_tensor(wm[r_:r_ + 32, :], WM32[r_:r_ + 32, :], wm[r_:r_ + 32, :].bitcast(F32),
                                            ALU.subtract)
            i.then_inc(phase_weights, 1)
            nc.vector.tensor_scalar(gam2, raw("gamma2"), float(np.sqrt(P)), None, ALU.mult)
            nc.vector.tensor_tensor(bias0, raw("b0"), raw("convb"), ALU.add).then_inc(consts_ready, 1)
            made = B[:, 0:2, :].rearrange("p a b -> p (a b)")
            for k in range(TAPS):
                nc.vector.tensor_scalar(made[:, P * (1 + k):P * (2 + k)], ident, raw("convw", k, 1), None, ALU.mult)
            w3 = raw("wqk1").rearrange("p (g d) -> p g d", d=HD)
            chain(nc.vector.tensor_reduce(wmean[:, :], w3, AX.X, ALU.add))
            chain(nc.vector.tensor_scalar(wmean[:, :], wmean[:, :], 1.0 / HD, None, ALU.mult))
            nc.vector.tensor_tensor(made[:, P * 6:P * 8].rearrange("p (g d) -> p g d", d=HD), w3,
                                    bcast(wmean[:, :].unsqueeze(2), [P, 32, HD]), ALU.subtract)
            v.wait_ge(decay_ready, 1)
            chain(nc.vector.tensor_scalar(one_minus_a, a_dec, -1.0, 1.0, ALU.mult, ALU.add))
            chain(nc.vector.tensor_scalar(made[:, 0:P], raw("wt0"), one_minus_a, None, ALU.mult))
            o = SPLIT_AT["wt0s"][0]
            chain(nc.vector.tensor_copy(WH[:, o:o + 2 * CH], made))
            nc.vector.tensor_tensor(WL[:, o:o + 2 * CH], made, WH[:, o:o + 2 * CH].bitcast(F32), ALU.subtract)\
                .then_inc(made_ready, 1)
            for c in range(NC):
                for pos in range(8):
                    front_dve(v, chain, 0, c, pos)
                chain(nc.vector.tensor_tensor_scan(S0[:, c * CH:(c + 1) * CH], bcast(a_dec, [P, CH]), X32[:, :],
                                                   0.0 if c == 0 else S0[:, c * CH - 1:c * CH], ALU.mult, ALU.add))
            walk(2, v, chain, lambda n, c, pos: front_dve(v, chain, n, c, pos),
                 lambda t, c: tail_dve(v, chain, t, c))
            tail_dve(v, chain, 8, NC - 1)

        @block.tensor
        def _(pe):
            pe.wait_ge(raw_loaded, 16)
            for c in range(NC):
                for pos in range(8):
                    front_pe(pe, 0, c, pos)
            walk(0, pe, None, lambda n, c, pos: front_pe(pe, n, c, pos), lambda t, c: tail_pe(pe, t, c))
            tail_pe(pe, 8, NC - 1)


def kernel(**inputs):
    import concourse.bacc as _bacc
    from concourse.bass_utils import run_bass_kernel_spmd as _run

    f = {k: np.asarray(v) for k, v in inputs.items()}

    def rows(a):
        a = a.reshape(a.shape[0], -1)
        return np.concatenate([a, np.zeros((P - a.shape[0], a.shape[1]), a.dtype)]) if a.shape[0] < P else a

    def wide(a):
        return np.concatenate([a, np.zeros((a.shape[0], P - a.shape[1]), a.dtype)], axis=1)

    def experts(a):
        return a.transpose(1, 0, 2).reshape(a.shape[1], -1)

    def blocks(a):
        return a.reshape(-1, P, a.shape[-1]).transpose(1, 0, 2).reshape(P, -1)

    def cols(a):
        return a.reshape(-1, P).T

    def four_times(a):
        return np.tile(a.reshape(-1, 4, 1, P // 4), (1, 1, 4, 1)).reshape(-1, 4 * P)

    qkv = f["L1_attn_W_qkv"]
    z64 = np.zeros((P, 64), np.float32)
    w = {
        "gate0": wide(f["L0_ffn_gate_w"].T), "w1_0": experts(f["L0_ffn_w1"]), "w3_0": experts(f["L0_ffn_w3"]),
        "w2_0": blocks(f["L0_ffn_w2"].reshape(-1, P)),
        "wqk1": qkv[:, 0:2 * P], "wv1": qkv[:, 2 * P:], "wproj": f["L1_attn_W_proj"],
        "gate1": wide(f["L1_ffn_gate_w"].T),
        "wg1": np.concatenate([experts(f["L1_ffn_w_gate"]), f["L1_ffn_ws_gate"], z64], axis=1),
        "wu1": np.concatenate([experts(f["L1_ffn_w_up"]), f["L1_ffn_ws_up"], z64], axis=1),
        "wd1": blocks(np.concatenate([f["L1_ffn_w_down"].reshape(-1, P), f["L1_ffn_ws_down"], z64.T], axis=0)),
        "wqkva": f["L2_attn_W_qkva"].T, "gate2": wide(f["L2_ffn_Wg"]), "w1_2": experts(f["L2_ffn_W1"]),
        "w2_2": blocks(f["L2_ffn_W2"].reshape(-1, P)),
        "b2_2": rows(np.tile(np.stack([f["L2_ffn_b2"], np.zeros_like(f["L2_ffn_b2"])], axis=1).reshape(NH, P), (2, 1))),
        "wq3": four_times(f["L3_attn_wq"]), "wk3": four_times(f["L3_attn_wk"]), "wv3": f["L3_attn_wv"], "wo3": f["L3_attn_wo"],
        "w1_3": f["L3_attn_w1"], "w2_3": blocks(f["L3_attn_w2"]), "fw1": f["L3_ffn_W1"], "fw2": blocks(f["L3_ffn_W2"]),
        "wt0": f["L0_attn_W"].T, "proj": np.tile(f["L3_attn_proj_mat"], (NH, 1)),
        "decay": cols(f["L0_attn_decay_logit"]), "convw": f["L0_attn_conv_w"].reshape(P, TAPS),
        "b0": cols(f["L0_attn_b"]), "convb": cols(f["L0_attn_conv_b"]),
        "ln_g1": cols(np.tile(f["L1_attn_ln_gamma"], NH)), "ln_b1": cols(np.tile(f["L1_attn_ln_beta"], NH)),
        "bproj": cols(f["L1_attn_b_proj"]), "gamma2": cols(f["L2_attn_gamma"]),
        "bg2": rows(f["L2_ffn_bg"].reshape(-1, 1)), "b1_2": cols(f["L2_ffn_b1"].reshape(-1)),
        "bq4": four_times(f["L3_attn_bq"].reshape(1, P)).reshape(4, P).T,
        "bk4": four_times(f["L3_attn_bk"].reshape(1, P)).reshape(4, P).T, "bv": cols(f["L3_attn_bv"]),
        "bo": cols(f["L3_attn_bo"]), "g1_3": cols(f["L3_attn_ln1_g"]), "e1_3": cols(f["L3_attn_ln1_b"]),
        "g2_3": cols(f["L3_attn_ln2_g"]), "e2_3": cols(f["L3_attn_ln2_b"]), "b1_3": cols(f["L3_attn_b1"]),
        "b2_3": cols(f["L3_attn_b2"]), "fb1": cols(f["L3_ffn_b1"]), "fb2": cols(f["L3_ffn_b2"]),
    }
    k = np.arange(P)
    w["ident"] = np.eye(P, dtype=np.float32)
    for at_, name in ((0, "q"), (NH, "k")):
        w["mean_" + name] = (k[:, None] // HD + at_ == k[None, :2 * NH]).astype(np.float32) / HD
        w["spread_" + name] = rows((k[:2 * NH, None] == k[None, :] // HD + at_).astype(np.float32))
    w["iota"] = np.tile(np.arange(16, dtype=np.float32), (P, 1))
    w["head_of_4"] = (k[:, None] // HD % 4 == np.arange(4)[None, :]).astype(np.float32)
    w["sel16"] = rows(((k[:2 * NH, None] % NH) == np.arange(8 * P)[None, :] // (P // 2)).astype(np.float32))

    def pack(names, table):
        sizes = dict(table)
        for n in names:
            assert w[n].shape == (P, sizes[n]), (n, w[n].shape, sizes[n])
        return np.ascontiguousarray(np.concatenate([w[n] for n in names], axis=1))

    order = [n for g in GROUPS for n in g]
    arrays = {
        "in_x": np.ascontiguousarray(f["L0_attn_x"].reshape(T, P)),
        "in_w_split": pack([n for n in order if n not in EXACT_AT], SPLIT),
        "in_w_exact": pack([n for n in order if n in EXACT_AT], EXACT),
        "in_w_raw": pack([n for n, _ in RAW], RAW),
    }
    nc = _bacc.Bacc("TRN2", target_bir_lowering=False, num_devices=1)
    args = [nc.dram_tensor(n, a.shape, mybir.dt.from_np(a.dtype), kind="ExternalInput").ap()
            for n, a in arrays.items()]
    out = nc.dram_tensor("out_0", (T, P), F32, kind="ExternalOutput").ap()
    build(nc, *args, out)
    r = _run(nc, [arrays], core_ids=[0])
    return r.results[0]["out_0"].reshape(1, T, P)
```

```python
from contextlib import ExitStack

import numpy as np

import concourse.bass as bass
from concourse import mybir

F32 = mybir.dt.float32
F32R = mybir.dt.float32r
U32 = mybir.dt.uint32
ALU = mybir.AluOpType
ACT = mybir.ActivationFunctionType
AX = mybir.AxisListType

P = 128
T = 2048
CH = 512
NC = T // CH
TL = CH // P
NH, HD = 16, 8
WIN = 64
TAPS = 5
EPS = 1e-5
ROUND = 1.5 * 2.0 ** 23
PIECE = 512
STAGES = 4

SPLIT = [
    ("gate0", 128), ("w1_0", 1024), ("w3_0", 1024), ("w2_0", 1024),
    ("wv1", 128), ("wproj", 128),
    ("gate1", 128), ("wg1", 1152), ("wu1", 1152), ("wd1", 1152),
    ("wqkva", 384),
    ("gate2", 128), ("w1_2", 2048), ("w2_2", 2048), ("b2_2", 128),
    ("wq3", 512), ("wk3", 512), ("wv3", 128), ("wo3", 128),
    ("w1_3", 512), ("w2_3", 512), ("fw1", 512), ("fw2", 512),
]
EXACT = [("sel16", 1024)]
RAW = [
    ("ident", 128), ("wt0", 128), ("mean_q", 32), ("mean_k", 32), ("spread_q", 128), ("spread_k", 128), ("wqk1", 256), ("proj", 128), ("iota", 16),
    ("head_of_4", 4), ("head_mask", NH), ("decay", 1), ("convw", TAPS), ("b0", 1), ("convb", 1), ("ln_g1", 1),
    ("ln_b1", 1), ("bproj", 1), ("gamma2", 1), ("bg2", 1), ("b1_2", 16), ("bq4", 4), ("bk4", 4),
    ("bv", 1), ("bo", 1), ("g1_3", 1), ("e1_3", 1), ("g2_3", 1), ("e2_3", 1), ("b1_3", 4),
    ("b2_3", 1), ("fb1", 4), ("fb2", 1),
]
MADE = [("wt0s", 128), ("taps", TAPS * 128), ("wqk1c", 256)]


def places(table, at=0):
    out = {}
    for name, n in table:
        out[name] = (at, n)
        at += n
    return out, at


SPLIT_AT, _end = places([s_ for s_ in SPLIT if s_[0] in (
    "gate0", "wv1", "wproj", "gate1", "wqkva", "gate2", "b2_2", "w2_2")] + MADE)
_region_a, _end_a = places([s_ for s_ in SPLIT if s_[0] in ("w1_0", "w3_0", "w2_0")], _end)
_over_a, _end_o = places([s_ for s_ in SPLIT if s_[0] in ("w1_2",)] + [("keys_parts", 2 * CH)], _end)
assert _end_o <= _end_a
_region_b, NSPLIT = places([s_ for s_ in SPLIT if s_[0] in ("wg1", "wu1", "wd1")], _end_a)
_over_b, _end_b = places([s_ for s_ in SPLIT if s_[0] in (
    "wq3", "wk3", "wv3", "wo3", "w1_3", "w2_3", "fw1", "fw2")], _end_a)
assert _end_b <= NSPLIT
SPLIT_AT = SPLIT_AT | _region_a | _over_a | _region_b | _over_b
EXACT_AT, NEXACT = places(EXACT)
RAW_AT, NRAW = places(RAW)

GROUPS = [
    ["gate0", "w1_0", "w3_0", "w2_0", "sel16"],
    ["wv1", "wproj", "gate1", "wg1", "wu1", "wd1"],
    ["wqkva", "gate2", "b2_2", "w1_2", "w2_2"],
    ["wq3", "wk3", "wv3", "wo3", "w1_3", "w2_3", "fw1", "fw2"],
]


def pieces():
    out, packed = [], {"split": 0, "exact": 0}
    for g, names in enumerate(GROUPS):
        for name in names:
            kind = "exact" if name in EXACT_AT else "split"
            at, n = (EXACT_AT if kind == "exact" else SPLIT_AT)[name]
            for k in range(0, n, PIECE):
                w = min(PIECE, n - k)
                last = out[-1] if out else None
                if last and last[0] == g and last[1] == kind and last[3] + last[5] == at + k and last[5] + w <= PIECE:
                    out[-1] = (g, kind, last[2] + [name], last[3], last[4], last[5] + w)
                else:
                    out.append((g, kind, [name], at + k, packed[kind], w))
                packed[kind] += w
    return out


PIECES = pieces()
READY_AT = {name: i + 1 for i, p in enumerate(PIECES) for name in p[2]}


class Ffn:
    def __init__(self, key, norm, tail, experts, blocks, up, gate, down, func, topk=0, spread=0,
                 spread_every=1, plain_block=None):
        self.key, self.norm, self.tail, self.experts, self.blocks = key, norm, tail, experts, blocks
        self.up, self.gate, self.down, self.func, self.topk = up, gate, down, func, topk
        self.spread, self.spread_every, self.plain_block = spread, spread_every, plain_block


FFN0 = Ffn("ffn0", 1, 1, 16, 8, "w1_0", "w3_0", "w2_0", ACT.Silu, 4, 8)
FFN1 = Ffn("ffn1", 3, 3, 16, 9, "wg1", "wu1", "wd1", ACT.Silu, 2, 8, 1, 8)
FFN2 = Ffn("ffn2", 5, 5, 8, 16, "w1_2", None, "w2_2", ACT.Relu, 2, 8, 2)
FFN3 = Ffn("ffn3", 7, 7, 0, 4, "w1_3", None, "w2_3", ACT.Relu)
FFN4 = Ffn("ffn4", 8, 8, 0, 4, "fw1", None, "fw2", ACT.Relu)
FFNS = [FFN0, FFN1, FFN2, FFN3, FFN4]
_blk = _sp = _rt = 0
for _f in FFNS:
    _f.block0, _f.spread0, _f.router0 = _blk, _sp, _rt
    _blk += NC * _f.blocks
    _sp += NC * _f.spread
    _rt += NC * (1 if _f.experts else 0)
    _f.dense = not _f.experts
    _f.lag = 2 if _f.dense else 3
ROUTED = {f.norm: f for f in FFNS if f.experts}


def build(nc, x_in, w_split, w_exact, w_raw, out):
    with ExitStack() as ctx:
        def sb(name, shape, dt=F32):
            return ctx.enter_context(nc.sbuf_tensor(name, shape, dt))

        def bank(name):
            return ctx.enter_context(nc.psum_tensor(name, [P, CH], F32))

        def sem(name):
            return ctx.enter_context(nc.semaphore(name))

        X = sb("X", [P, NC * TL, P])
        Z = sb("Z", [P, NC * TL, P])
        PAD = TAPS // 2
        XH = sb("XH", [P, T + 2 * PAD], F32R)
        XL = sb("XL", [P, T + 2 * PAD], F32R)
        WH = sb("WH", [P, NSPLIT], F32R)
        WL = sb("WL", [P, NSPLIT], F32R)
        WE = sb("WE", [P, NEXACT], F32R)
        WR = sb("WR", [P, NRAW])
        STG = sb("STG", [P, STAGES, PIECE])
        XN = sb("XN", [P, TL, P])
        X32 = sb("X32", [P, CH])
        YT = sb("YT", [P, CH])
        SCT = sb("SCT", [2 * NH, 2 * CH], F32R)
        S0 = sb("S0", [P, T])
        B = sb("B", [P, 12, CH])
        buf = [B[:, i, :] for i in range(12)]
        rbuf = [sb(f"rbuf{i}", [P, CH], F32R) for i in range(4)]
        VB = sb("VB", [P, TL, NH // 2, 2, 2, HD + 1])
        KVT = sb("KVT", [P, 2, 4, P])
        WM = sb("WM", [P, 4, P], F32R)
        small = sb("small", [P, 1024])
        IDX = sb("IDX", [P, TL, 8], U32)
        VEC = sb("VEC", [P, 32])

        G = [bank("gate_bank0"), bank("gate_bank1")]
        U = [bank("up_bank0"), bank("up_bank1")]
        SP = bank("spread_bank")
        Y = bank("y_bank")
        TN = bank("norm_bank")
        R = bank("route_bank")

        at = 0

        def cut(n):
            nonlocal at
            at += n
            assert at <= 1024
            return small[:, at - n:at]

        stats = cut(TL * 6).rearrange("p (a b) -> p a b", a=TL)
        mv = cut(TL * 2).rearrange("p (a b) -> p a b", a=TL)
        ve = cut(TL)
        rs = cut(TL)
        rr = cut(TL)
        ss = cut(TL)
        rmax = cut(TL)
        top = cut(TL * 8).rearrange("p (a b) -> p a b", a=TL)
        idxf = cut(TL * 8).rearrange("p (a b) -> p a b", a=TL)
        den = cut(TL)
        rec = cut(TL)
        RE = cut(TL * NH)
        RM = cut(TL * NH)
        RS_ = cut(TL * NH)
        EQ = cut(TL * NH * 4)
        SC2 = cut(TL * NH * 2)
        amax = cut(16)
        orec = cut(NH)
        wmean = cut(32)
        mhalf = VEC[:, 0:1]
        a_dec, one_minus_a, bias0 = VEC[:, 1:2], VEC[:, 2:3], VEC[:, 3:4]
        gam2 = VEC[:, 12:13]
        half_pi = VEC[:, 13:14]
        carry = VEC[:, 14:15]
        epsv = VEC[:, 15:16]
        zero = VEC[:, 16:17]

        def raw(name, a=0, n=None):
            o, w = RAW_AT[name]
            return WR[:, o + a:o + a + (w - a if n is None else n)]

        ident = raw("ident")

        x_loaded = [sem(f"x_loaded{c}") for c in range(NC)]
        raw_loaded = sem("raw_loaded")
        piece_loaded = [sem(f"piece_loaded{k}") for k in range(STAGES)]
        piece_ready = sem("piece_ready")
        consts_ready = sem("consts_ready")
        decay_ready = sem("decay_ready")
        made_ready = sem("made_ready")
        fills_ready = sem("fills_ready")
        out_stored = sem("out_stored")
        dve_chain = sem("dve_chain")
        act_chain = sem("act_chain")
        pool_chain = sem("pool_chain")
        stats_ready = sem("stats_ready")
        rstd_ready = sem("rstd_ready")
        xn_ready = sem("xn_ready")
        norm_turned = sem("norm_turned")
        x32_ready = sem("x32_ready")
        xh_ready = sem("xh_ready")
        xl_ready = sem("xl_ready")
        logits_t = sem("logits_t")
        logits_sb = sem("logits_sb")
        logits_tok = sem("logits_tok")
        shifted = sem("shifted")
        largest = sem("largest")
        chosen = sem("chosen")
        scored = sem("scored")
        weights_tok = sem("weights_tok")
        weights_t = sem("weights_t")
        weights_sb = sem("weights_sb")
        y_full = sem("y_full")
        yt_ready = sem("yt_ready")
        yt_turned = sem("yt_turned")
        res_done = sem("res_done")
        first_full = sem("first_full")
        second_full = sem("second_full")
        mul_done = sem("mul_done")
        spread_full = sem("spread_full")
        act_done = sem("act_done")
        h_ready = sem("h_ready")
        hh_ready = sem("hh_ready")
        hl_ready = sem("hl_ready")
        down_done = sem("down_done")
        s_high = sem("s_high")
        s_low = sem("s_low")
        qkv_full = sem("qkv_full")
        v_copied = sem("v_copied")
        v_turned = sem("v_turned")
        v_placed = sem("v_placed")
        var_full = sem("var_full")
        var_read = sem("var_read")
        rstd_qk = sem("rstd_qk")
        masked_dve, masked_pool, masked_act = sem("masked_dve"), sem("masked_pool"), sem("masked_act")
        rstd_full = sem("rstd_full")
        centred = sem("centred")
        qk_read = sem("qk_read")
        qk_ready = sem("qk_ready")
        s_full = sem("scores_full")
        s_read = sem("scores_read")
        p_ready = sem("probs_ready")
        p_turned = sem("probs_turned")
        pt_ready = sem("probs_t_ready")
        o_full = sem("o_full")
        o_read = sem("o_read")
        a_turned = sem("a_turned")
        a32_ready = sem("a32_ready")
        ah_ready = sem("ah_ready")
        al_ready = sem("al_ready")
        scan_in = sem("scan_in")
        sig_ready = sem("sig_ready")
        phase_weights = sem("phase_weights")
        proj_full = sem("proj_full")
        proj_sb = sem("proj_sb")
        ks_high = sem("ks_high")
        ks_ready = sem("ks_ready")
        vt_turned = sem("vt_turned")
        v4_ready = sem("v4_ready")
        t_full = sem("phase_full")
        m_ready = sem("rounded_ready")
        m_ready_dve = sem("rounded_ready_dve")
        r_ready = sem("rest_ready")
        ab_ready = sem("abs_ready")
        cos_ready = sem("cos_ready")
        sin_ready = sem("sin_ready")
        unit_used = sem("unit_used")
        kvf_ready = sem("kvf_ready")
        kv_turned = sem("kv_turned")
        kvt_cleared = sem("kvt_cleared")
        kv_ready = sem("kv_ready")
        oq_read = sem("oq_read")

        class Chain:

            def __init__(self, eng, s):
                self.eng, self.s, self.n = eng, s, 0

            def __call__(self, ins):
                self.n += 1
                ins.then_inc(self.s, 1)
                self.eng.wait_ge(self.s, self.n)

        def chunk(ap2, c, pad=0):
            return ap2[:, bass.ds(c * CH + pad, CH)]

        def tiles(a3, c):
            return a3[:, bass.ds(c * TL, TL), :]

        def bcast(ap, shape):
            return ap.broadcast_to(shape)

        def count(stage, c):
            return NC * stage + c

        def wh(name, a=0, n=P):
            o = SPLIT_AT[name][0] + a
            return WH[:, o:o + n], WL[:, o:o + n]

        turned = {"norms": 0, "tails": 0}

        def front_source(n):
            return Z if n == 7 else X

        def front_dve(v, chain, n, c, pos):
            m = count(n, c)
            src = front_source(n)

            def read_stats(t3, first):
                for j in range(TL):
                    i = nc.vector.bn_stats(stats[:, j, :], t3(j))
                chain(i)
                for j in range(TL):
                    i = nc.vector.bn_aggr(mv[:, j, :], stats[:, j, :])
                i.then_inc(stats_ready, 1)

            sbase = m + max(0, m - count(6, 0)) if n <= 6 else m + NC
            if pos == 0:
                if n == 0:
                    v.wait_ge(x_loaded[c], 16)
                else:
                    v.wait_ge(res_done, count(n - 1, c) + 1)
                read_stats(lambda j: src[:, c * TL + j, :], True)
            if pos == 1:
                v.wait_ge(rstd_ready, sbase + 1)
                if m:
                    v.wait_ge(norm_turned, m)
                dst = (lambda j: Z[:, c * TL + j, :]) if n == 6 else (lambda j: XN[:, j, :])
                for j in range(TL):
                    i = nc.vector.tensor_scalar(dst(j), src[:, c * TL + j, :], mv[:, j, 0:1],
                                                rs[:, j:j + 1], ALU.subtract, ALU.mult)
                if n == 6:
                    chain(i)
                    read_stats(lambda j: Z[:, c * TL + j, :], False)
                else:
                    i.then_inc(xn_ready, 1)
            if pos == 11 and n == 6:
                v.wait_ge(rstd_ready, sbase + 2)
                for j in range(TL):
                    i = nc.vector.tensor_scalar(XN[:, j, :], Z[:, c * TL + j, :], mv[:, j, 0:1],
                                                rs[:, j:j + 1], ALU.subtract, ALU.mult)
                i.then_inc(xn_ready, 1)
            if pos == 3:
                v.wait_ge(x32_ready, m + 1)
                nc.vector.tensor_copy(chunk(XH, c, PAD), X32[:, :]).then_inc(xh_ready, 1)
                v.wait_ge(xh_ready, m + 1)
                nc.vector.tensor_tensor(chunk(XL, c, PAD), X32[:, :], chunk(XH, c, PAD).bitcast(F32),
                                        ALU.subtract).then_inc(xl_ready, 1)
            f = ROUTED.get(n)
            if not f:
                return
            E, K = f.experts, f.topk
            r = f.router0 + c
            Rv = R[:, 0:TL * E].rearrange("p (t e) -> p t e", t=TL)
            re = RE[:, 0:TL * E].rearrange("p (t e) -> p t e", t=TL)
            rm = RM[:, 0:TL * E].rearrange("p (t e) -> p t e", t=TL)
            rw = RS_[:, 0:TL * E].rearrange("p (t e) -> p t e", t=TL)
            eq = EQ[:, 0:TL * E * K].rearrange("p (t e k) -> p t e k", t=TL, k=K)
            D_ = NH // E
            sc2 = SC2[:, :].rearrange("p (t s e d) -> p t s e d", t=TL, s=2, d=D_)
            rwd = bcast(rw.unsqueeze(3), [P, TL, E, D_])
            if pos == 5 and n != 3:
                v.wait_ge(logits_tok, r + 1)
                chain(nc.vector.tensor_reduce(rmax[:, :], Rv, AX.X, ALU.max))
                nc.vector.tensor_tensor(re, Rv, bcast(rmax[:, :].unsqueeze(2), [P, TL, E]),
                                        ALU.subtract).then_inc(shifted, 1)
            if pos == 7:
                v.wait_ge(scored, r + 1)
                for j in range(TL):
                    i = nc.vector.max(top[:, j, :], re[:, j, :])
                chain(i)
                for j in range(TL):
                    i = nc.vector.max_index(IDX[:, j, :], top[:, j, :], re[:, j, :])
                chain(i)
                nc.vector.tensor_copy(idxf, IDX[:, :, :]).then_inc(largest, 1)
            if pos == 8:
                v.wait_ge(largest, r + 1)
                for j in range(TL):
                    i = nc.vector.tensor_tensor(
                        eq[:, j, :, :], bcast(raw("iota", 0, E).unsqueeze(2), [P, E, K]),
                        bcast(idxf[:, j, 0:K].unsqueeze(1), [P, E, K]), ALU.is_equal)
                chain(i)
                nc.vector.tensor_reduce(RM[:, 0:TL * E], EQ[:, 0:TL * E * K].rearrange(
                    "p (a k) -> p a k", k=K), AX.X, ALU.add).then_inc(chosen, 1)
            if pos == 9:
                v.wait_ge(chosen, r + 1)
                chain(nc.vector.tensor_reduce(den[:, :], top[:, :, 0:K], AX.X, ALU.add))
                if n == 3:
                    chain(nc.vector.tensor_scalar(den[:, :], den[:, :], 1e-20, None, ALU.add))
                chain(nc.vector.reciprocal(rec[:, :], den[:, :]))
                if n == 3:
                    chain(nc.vector.tensor_scalar(rec[:, :], rec[:, :], 2.5, None, ALU.mult))
                chain(nc.vector.tensor_tensor(rw, re, rm, ALU.mult))
                chain(nc.vector.tensor_tensor(rw, rw, bcast(rec[:, :].unsqueeze(2), [P, TL, E]), ALU.mult))
                parts = [slice(0, TL)] if D_ == 1 else [slice(k, k + 1) for k in range(TL)]
                cut_ = (lambda t5, k, h_: t5[:, k, h_, :, 0]) if D_ == 1 else (lambda t5, k, h_: t5[:, k.start, h_, :, :])
                src_ = (lambda k: rw) if D_ == 1 else (lambda k: rwd[:, k.start, :, :])
                for k in parts:
                    i = nc.vector.tensor_copy(cut_(sc2, k, 0).bitcast(F32R), src_(k))
                chain(i)
                for k in parts:
                    i = nc.vector.tensor_tensor(cut_(sc2, k, 1), src_(k), cut_(sc2, k, 0), ALU.subtract)
                i.then_inc(weights_tok, 1)

        def front_pool(g, chain, n, c, pos):
            m = count(n, c)
            sbase = m + max(0, m - count(6, 0)) if n <= 6 else m + NC
            if pos == 0 or pos == 1 and n == 6:
                g.wait_ge(stats_ready, sbase + pos + 1)
                chain(nc.gpsimd.tensor_scalar(ve[:, :], mv[:, :, 1], 1.0, EPS, ALU.mult, ALU.add))
                i = nc.gpsimd.tensor_tensor(rs[:, :], ve[:, :], bcast(mhalf, [P, TL]), ALU.pow)
                if n == 4:
                    chain(i)
                    chain(nc.gpsimd.tensor_tensor(ss[:, :], rs[:, :], rs[:, :], ALU.mult))
                    chain(nc.gpsimd.tensor_tensor(ss[:, :], ss[:, :], mv[:, :, 1], ALU.mult))
                    chain(nc.gpsimd.tensor_scalar(ss[:, :], ss[:, :], float(P), 1e-24, ALU.mult, ALU.max))
                    chain(nc.gpsimd.tensor_tensor(rr[:, :], ss[:, :], bcast(mhalf, [P, TL]), ALU.pow))
                    i = nc.gpsimd.tensor_tensor(rs[:, :], rs[:, :], rr[:, :], ALU.mult)
                i.then_inc(rstd_ready, 1)

        def front_act(a, chain, n, c, pos):
            m = count(n, c)
            if pos == 2:
                a.wait_ge(norm_turned, m + 1)
                if m:
                    a.wait_ge(xl_ready, m)
                if n == 4:
                    nc.scalar.activation(X32[:, :], TN[:, :], ACT.Copy, scale=gam2).then_inc(x32_ready, 1)
                elif n in (6, 7):
                    g_, b_ = ("g1_3", "e1_3") if n == 6 else ("g2_3", "e2_3")
                    nc.scalar.activation(X32[:, :], TN[:, :], ACT.Identity, scale=raw(g_), bias=raw(b_))\
                        .then_inc(x32_ready, 1)
                else:
                    nc.scalar.activation(X32[:, :], TN[:, :], ACT.Copy).then_inc(x32_ready, 1)
            f = ROUTED.get(n)
            if not f:
                return
            E = f.experts
            r = f.router0 + c
            if pos == 4:
                a.wait_ge(logits_t, r + 1)
                bias = raw("bg2")[0:E, :] if n == 5 else zero[0:E, :]
                nc.scalar.activation(YL[0:E, :], R[0:E, :], ACT.Identity, bias=bias).then_inc(logits_sb, 1)
            if pos == 6:
                Rv = R[:, 0:TL * E].rearrange("p (t e) -> p t e", t=TL)
                re = RE[:, 0:TL * E].rearrange("p (t e) -> p t e", t=TL)
                if n == 3:
                    a.wait_ge(logits_tok, r + 1)
                    nc.scalar.activation(re, Rv, ACT.Sigmoid).then_inc(scored, 1)
                else:
                    a.wait_ge(shifted, shift_count(n, c) + 1)
                    nc.scalar.activation(re, re, ACT.Exp).then_inc(scored, 1)
            if pos == 10:
                a.wait_ge(weights_t, r + 1)
                nc.scalar.activation(SCT[0:2 * NH, bass.ds(c % 2 * CH, CH)], R[0:2 * NH, :], ACT.Copy)\
                    .then_inc(weights_sb, 1)

        YL = sb("YL", [NH, CH])

        mv0 = EQ[:, 0:2 * NC * TL].rearrange("p (a b) -> p a b", b=2)
        ve0, rs0 = EQ[:, 32:48], EQ[:, 48:64]
        stats0 = EQ[:, 64:64 + 6 * NC * TL].rearrange("p (a b) -> p a b", b=6)
        TN0 = [TN, G[0], G[1], U[0]]
        XF0 = [buf[4 + c] for c in range(NC)]

        def first_stats(v, chain, c):
            v.wait_ge(x_loaded[c], 16)
            for j in range(TL):
                i = nc.vector.bn_stats(stats0[:, c * TL + j, :], X[:, c * TL + j, :])
            chain(i)
            for j in range(TL):
                i = nc.vector.bn_aggr(mv0[:, c * TL + j, :], stats0[:, c * TL + j, :])
            i.then_inc(stats_ready, 1)

        def first_rstd(g, chain, c):
            g.wait_ge(stats_ready, c + 1)
            w = slice(c * TL, c * TL + TL)
            chain(nc.gpsimd.tensor_scalar(ve0[:, w], mv0[:, w, 1], 1.0, EPS, ALU.mult, ALU.add))
            nc.gpsimd.tensor_tensor(rs0[:, w], ve0[:, w], bcast(mhalf, [P, TL]), ALU.pow).then_inc(rstd_ready, 1)

        def first_normalise(v, c):
            v.wait_ge(rstd_ready, c + 1)
            for j in range(c * TL, c * TL + TL):
                i = nc.vector.tensor_scalar(Z[:, j, :], X[:, j, :], mv0[:, j, 0:1], rs0[:, j:j + 1],
                                            ALU.subtract, ALU.mult)
            i.then_inc(xn_ready, 1)

        def first_turn(pe, c):
            pe.wait_ge(xn_ready, c + 1)
            for j in range(TL):
                i = nc.tensor.transpose(TN0[c][:, j * P:(j + 1) * P], Z[:, c * TL + j, :], ident)
            i.then_inc(norm_turned, 1)
            turned["norms"] += 1

        def first_copy(a, c):
            a.wait_ge(norm_turned, c + 1)
            nc.scalar.activation(XF0[c], TN0[c][:, :], ACT.Copy).then_inc(x32_ready, 1)

        def first_split(v, chain, c):
            v.wait_ge(x32_ready, c + 1)
            nc.vector.tensor_copy(chunk(XH, c, PAD), XF0[c]).then_inc(xh_ready, 1)
            chain(nc.vector.tensor_tensor_scan(S0[:, c * CH:(c + 1) * CH], bcast(a_dec, [P, CH]), XF0[c],
                                               0.0 if c == 0 else S0[:, c * CH - 1:c * CH], ALU.mult, ALU.add))
            v.wait_ge(xh_ready, c + 1)
            nc.vector.tensor_tensor(chunk(XL, c, PAD), XF0[c], chunk(XH, c, PAD).bitcast(F32),
                                    ALU.subtract).then_inc(xl_ready, 1)

        def shift_count(n, c):
            return {1: 0, 5: NC}[n] + c

        def front_pe(pe, n, c, pos):
            m = count(n, c)
            if pos == 2:
                pe.wait_ge(xn_ready, m + 1)
                if m:
                    pe.wait_ge(x32_ready, m)
                if turned["tails"]:
                    pe.wait_ge(res_done, turned["tails"])
                turned["norms"] += 1
                for j in range(TL):
                    i = nc.tensor.transpose(TN[:, j * P:(j + 1) * P], XN[:, j, :], ident)
                i.then_inc(norm_turned, 1)
            f = ROUTED.get(n)
            if not f:
                return
            E = f.experts
            r = f.router0 + c
            if pos == 4:
                pe.wait_ge(xl_ready, m + 1)
                if n == 3 and c == 0:
                    pe.wait_ge(v_placed, 2 * NC)
                pe.wait_ge(piece_ready, READY_AT[f"gate{(n - 1) // 2}"])
                if r:
                    pe.wait_ge(weights_sb, r)
                mm3(R[:, :], wh(f"gate{(n - 1) // 2}"), (chunk(XH, c, PAD), chunk(XL, c, PAD)), True, True)\
                    .then_inc(logits_t, 1)
            if pos == 5:
                pe.wait_ge(logits_sb, r + 1)
                for j in range(TL):
                    i = nc.tensor.transpose(R[:, j * E:(j + 1) * E], YL[0:E, j * P:(j + 1) * P],
                                            ident[0:E, 0:E])
                i.then_inc(logits_tok, 1)
            if pos == 10:
                pe.wait_ge(weights_tok, r + 1)
                for j in range(TL):
                    i = nc.tensor.transpose(R[0:2 * NH, j * P:(j + 1) * P],
                                            SC2[:, j * 2 * NH:(j + 1) * 2 * NH], ident)
                i.then_inc(weights_t, 1)

        def mm3(dst, w, x, start, stop):
            nc.tensor.matmul(dst, w[0], x[0], start=start, stop=False)
            nc.tensor.matmul(dst, w[0], x[1], start=False, stop=False)
            return nc.tensor.matmul(dst, w[1], x[0], start=False, stop=stop)

        def tail_pe(pe, t, c):
            n = count(t, c)
            pe.wait_ge(yt_ready, n + 1)
            if turned["norms"]:
                pe.wait_ge(x32_ready, turned["norms"])
            if n:
                pe.wait_ge(res_done, n)
            turned["tails"] += 1
            for j in range(TL):
                i = nc.tensor.transpose(TN[:, j * P:(j + 1) * P], YT[:, j * P:(j + 1) * P], ident)
            i.then_inc(yt_turned, 1)

        def tail_dve(v, chain, t, c):
            n = count(t, c)
            v.wait_ge(yt_turned, n + 1)
            Yv = TN[:, :].rearrange("p (t d) -> p t d", t=TL)
            if t == 6:
                nc.vector.tensor_tensor(tiles(Z, c), tiles(Z, c), Yv, ALU.add).then_inc(res_done, 1)
            elif t == 7:
                chain(nc.vector.tensor_tensor(tiles(Z, c), tiles(Z, c), Yv, ALU.add))
                nc.vector.tensor_tensor(tiles(X, c), tiles(X, c), tiles(Z, c), ALU.add).then_inc(res_done, 1)
            else:
                nc.vector.tensor_tensor(tiles(X, c), tiles(X, c), Yv, ALU.add).then_inc(res_done, 1)

        def y_bank_free(pe, t, c):
            if count(t, c):
                pe.wait_ge(yt_ready, count(t, c))

        def yt_free(eng, t, c):
            if count(t, c):
                eng.wait_ge(yt_turned, count(t, c))

        def block_no(f, c, b):
            return f.block0 + f.blocks * c + b

        AO = [buf[0], buf[1]]
        MO = [buf[2], buf[3]]
        HO = [buf[4], buf[5], buf[6]]

        def body_start(eng, t, c):
            if count(t, c):
                eng.wait_ge(yt_ready, count(t, c))

        def count_y(t, c):
            return {0: 0, 2: NC, 6: 2 * NC}[t] + c

        def lagged(f, c, b, lag):
            k = c * f.blocks + b
            last = k == NC * f.blocks - 1
            return [divmod(i, f.blocks) for i in range(k - lag, k + (1 if last else -lag + 1)) if i >= 0]

        def in_stage(f, c, b, depth):
            return c * f.blocks + b >= depth

        STEPS_AT = {
            4: {0: (2, 3), 1: (0,), 3: (1, 11)},
            8: {0: (0, 4), 1: (1, 5), 2: (11, 2), 3: (6, 3, 7), 4: (8,), 6: (9,), 7: (10,)},
            9: {0: (0, 4), 1: (5,), 2: (1,), 3: (6,), 5: (7, 11, 2, 8), 6: (9,), 7: (3, 10)},
            16: {0: (0,), 1: (4,), 2: (1,), 3: (5,), 4: (11,), 5: (6,), 7: (2, 7), 8: (3,), 9: (8,), 11: (9,), 13: (10,)},
        }
        EARLY = 20
        ALL_STEPS = (0, 1, 11, 2, 3, 4, 5, 6, 7, 8, 9, 10)
        NORM_STEPS = (0, 1, 11, 2, 3)
        LATE_NORM, LATE_ROUTE = 12, 13

        def late_start(f, c, b):
            return f in (FFN0, FFN2) and (c, b) == (0, 0)


        def hooks(f, c, b, hook, tail_late):
            if late_start(f, c, b):
                hook(LATE_NORM)
            for pos in STEPS_AT[f.blocks].get(b, ()):
                hook(pos)
            if b == (min(f.lag + tail_late, f.blocks - 1) if c else tail_late):
                hook(-1)
            if c == NC - 1:
                hook(EARLY + b)

        def ffn_pe(pe, f, c, hook):
            if c == 0:
                body_start(pe, f.tail, 0)
                for name in [f.up, f.gate, f.down]:
                    if name:
                        pe.wait_ge(piece_ready, READY_AT[name])
                if f.experts:
                    pe.wait_ge(piece_ready, READY_AT["sel16"])
                if f.experts == 8:
                    pe.wait_ge(piece_ready, READY_AT["b2_2"])
            pe.wait_ge(xl_ready, count(f.norm, c) + 1)

            def up(c, b):
                n = block_no(f, c, b)
                xs = (chunk(XH, c, PAD), chunk(XL, c, PAD))
                if in_stage(f, c, b, 2):
                    pe.wait_ge(act_done, n - 1)
                mm3(G[n % 2][:, :], wh(f.up, b * P), xs, True, True).then_inc(first_full, 1)
                if f.gate:
                    if in_stage(f, c, b, 2):
                        pe.wait_ge(mul_done, n - 1)
                    mm3(U[n % 2][:, :], wh(f.gate, b * P), xs, True, True).then_inc(second_full, 1)

            def spread(c, b):
                if f.dense or b == f.plain_block or b % f.spread_every:
                    return
                n = block_no(f, c, b)
                if b == 0:
                    pe.wait_ge(weights_sb, f.router0 + c + 1)
                if in_stage(f, c, b, 1):
                    pe.wait_ge(h_ready, n)
                o = EXACT_AT["sel16"][0] + b // f.spread_every * P
                nc.tensor.matmul(SP[:, :], WE[0:2 * NH, o:o + P], SCT[0:2 * NH, bass.ds(c % 2 * CH, CH)],
                                 start=True, stop=True).then_inc(spread_full, 1)

            def down(c, b):
                n = block_no(f, c, b)
                if b == 0:
                    y_bank_free(pe, f.tail, c)
                    if f.experts == 8:
                        s = SCT[0:2 * NH, bass.ds(c % 2 * CH, CH)]
                        bh, bl = wh("b2_2")
                        nc.tensor.matmul(Y[:, :], bh[0:2 * NH, :], s, start=True, stop=False)
                        nc.tensor.matmul(Y[:, :], bl[0:2 * NH, :], s, start=False, stop=False)
                pe.wait_ge(hl_ready, n + 1)
                mm3(Y[:, :], wh(f.down, b * P), (rbuf[n % 2][:, :], rbuf[2 + n % 2][:, :]),
                    b == 0 and f.experts != 8, b == f.blocks - 1).then_inc(down_done, 1)

            for b in range(f.blocks):
                up(c, b)
                if late_start(f, c, b):
                    hook(LATE_ROUTE)
                for at_ in lagged(f, c, b, 1 if f.gate else 0):
                    spread(*at_)
                for at_ in lagged(f, c, b, f.lag):
                    down(*at_)
                hooks(f, c, b, hook, 0)

        def ffn_act(a, chain, f, c, hook):
            if c == 0:
                body_start(a, f.tail, 0)

            def act(c, b):
                n = block_no(f, c, b)
                a.wait_ge(first_full, n + 1)
                if in_stage(f, c, b, 2):
                    a.wait_ge(hl_ready if f.dense else mul_done if f.gate else h_ready, n - 1)
                if f.gate:
                    nc.scalar.activation(AO[n % 2], G[n % 2][:, :], ACT.Silu).then_inc(act_done, 1)
                else:
                    bias = {"ffn2": "b1_2", "ffn3": "b1_3", "ffn4": "fb1"}[f.key]
                    nc.scalar.activation(AO[n % 2], G[n % 2][:, :], ACT.Relu, bias=raw(bias, b, 1))\
                        .then_inc(act_done, 1)

            def high(c, b):
                n = block_no(f, c, b)
                a.wait_ge(h_ready, n + 1)
                if in_stage(f, c, b, 2):
                    a.wait_ge(down_done, n - 1)
                nc.scalar.activation(rbuf[n % 2][:, :], HO[n % 3], ACT.Copy).then_inc(hh_ready, 1)

            def result(c):
                yt_free(a, f.tail, c)
                a.wait_ge(down_done, block_no(f, c, f.blocks - 1) + 1)
                bias = {"ffn3": raw("b2_3"), "ffn4": raw("fb2")}.get(f.key, zero)
                nc.scalar.activation(YT[:, :], Y[:, :], ACT.Identity, bias=bias).then_inc(yt_ready, 1)

            for b in range(f.blocks):
                act(c, b)
                if late_start(f, c, b):
                    hook(LATE_ROUTE)
                if not f.dense:
                    for at_ in lagged(f, c, b, 2 if f.gate else 1):
                        high(*at_)
                if c and b == f.lag - 1:
                    result(c - 1)
                hooks(f, c, b, hook, 0)
            if c == NC - 1:
                result(c)

        def ffn_dve(v, chain, f, c, hook):
            if c == 0:
                body_start(v, f.tail, 0)

            def gate(c, b):
                n = block_no(f, c, b)
                v.wait_ge(act_done, n + 1)
                v.wait_ge(second_full, n + 1)
                if in_stage(f, c, b, 2):
                    v.wait_ge(h_ready, n - 1)
                nc.vector.tensor_tensor(MO[n % 2], AO[n % 2], U[n % 2][:, :], ALU.mult).then_inc(mul_done, 1)

            def weigh(c, b):
                n = block_no(f, c, b)
                v.wait_ge(mul_done if f.gate else act_done, n + 1)
                if in_stage(f, c, b, 3):
                    v.wait_ge(hl_ready, n - 2)
                src = MO[n % 2] if f.gate else AO[n % 2]
                if b == f.plain_block:
                    nc.vector.tensor_copy(HO[n % 3], src).then_inc(h_ready, 1)
                else:
                    v.wait_ge(spread_full, f.spread0 + f.spread * c + b // f.spread_every + 1)
                    nc.vector.tensor_tensor(HO[n % 3], src, SP[:, :], ALU.mult).then_inc(h_ready, 1)

            def split(c, b):
                n = block_no(f, c, b)
                v.wait_ge(act_done, n + 1)
                if in_stage(f, c, b, 2):
                    v.wait_ge(down_done, n - 1)
                nc.vector.tensor_copy(rbuf[n % 2][:, :], AO[n % 2]).then_inc(hh_ready, 1)
                if not low_on_pool(f, c, b):
                    low(nc.vector, v, f, n)

            for b in range(f.blocks):
                if f.gate:
                    gate(c, b)
                    for at_ in lagged(f, c, b, 1):
                        weigh(*at_)
                elif f.dense:
                    split(c, b)
                else:
                    weigh(c, b)
                if not f.dense and (c, b) == (NC - 1, f.blocks - 1):
                    for k in (2, 1):
                        low(nc.vector, v, f, block_no(f, c, f.blocks - k))
                hooks(f, c, b, hook, 1)

        def low(e_, eng, f, n):
            eng.wait_ge(hh_ready, n + 1)
            if e_ is nc.vector and n:
                eng.wait_ge(hl_ready, n)
            e_.tensor_tensor(rbuf[2 + n % 2][:, :], AO[n % 2] if f.dense else HO[n % 3],
                             rbuf[n % 2][:, :].bitcast(F32), ALU.subtract).then_inc(hl_ready, 1)

        def low_on_pool(f, c, b):
            return c * f.blocks + b < NC * f.blocks - 2

        def ffn_pool(g, chain, f, c, hook, work):
            for b in range(f.blocks):
                for at_ in lagged(f, c, b, 0 if f.dense else 2):
                    if low_on_pool(f, *at_):
                        low(nc.gpsimd, g, f, block_no(f, *at_))
                hooks(f, c, b, hook, 0)
                if b % 3 == 2:
                    work()

        def stage0_pe(pe, c, hook):
            if c == 0:
                pe.wait_ge(made_ready, 1)
                pe.wait_ge(x32_ready, NC)
            pe.wait_ge(xl_ready, min(c + 2, NC))
            bank_, e = (Y, SP)[c % 2][:, :], c % 2
            if c >= 2:
                pe.wait_ge(yt_ready, c - 1)
            for k in range(TAPS):
                mm3(bank_, wh("taps", k * P), (chunk(XH, c, k), chunk(XL, c, k)), k == 0, False)
            pe.wait_ge(s_low, c + 1)
            mm3(bank_, wh("wt0s"), (rbuf[e][:, :], rbuf[2 + e][:, :]), False, True).then_inc(y_full, 1)

        def stage0_act(a, chain, c, hook):
            yt_free(a, 0, c)
            a.wait_ge(y_full, c + 1)
            nc.scalar.activation(YT[:, :], (Y, SP)[c % 2][:, :], ACT.Identity, bias=bias0).then_inc(yt_ready, 1)

        def stage0_dve(v, chain, c, hook):
            e = c % 2
            if hook and c < 2:
                return
            if c >= 2:
                v.wait_ge(y_full, c - 1)
            nc.vector.tensor_copy(rbuf[e][:, :], chunk(S0, c)).then_inc(s_high, 1)
            v.wait_ge(s_high, c + 1)
            nc.vector.tensor_tensor(rbuf[2 + e][:, :], chunk(S0, c), rbuf[e][:, :].bitcast(F32), ALU.subtract)\
                .then_inc(s_low, 1)

        UN = 2 * TL
        NU = NC * UN
        HU = NH // 2
        GR = 2 * NH
        QN = [S0[:, 0:CH], S0[:, CH:2 * CH]]
        KN = [S0[:, 2 * CH:3 * CH], S0[:, 3 * CH:4 * CH]]
        Zf = Z[:, :, :].rearrange("p a b -> p (a b)")
        AT = [Zf[:, 0:CH], Zf[:, CH:2 * CH]]
        qc, kc = Zf[:, 2 * CH:3 * CH], Zf[:, 3 * CH:4 * CH]
        KM = [B[:, 4 * k_:4 * k_ + 4, :].rearrange("p a b -> p (a b)").rearrange("p (h t) -> p h t", h=NH)
              for k_ in range(2)]
        PRB = [buf[8], buf[9]]
        PT = [buf[10], buf[11]]
        WK = sb("WK", [P, 3, CH])
        sqq, sqk = WK[:, 0, :], WK[:, 1, :]
        sdev, rstd = WK[0:GR, 2, :], WK[0:GR, 0, :]
        A32w = WK[:, 1, :]
        VTD = KVT[:, :, :, :].rearrange("p s j m -> p (s j m)").rearrange("p (w s t) -> p w s t", s=2, t=WIN)

        def VQ(c):
            return Y if c else R

        PREPARE_AT = {1: 0, 2: 1, 3: 2, 5: 3}

        def attn_early_pe(pe, b):
            if b == 0:
                pe.wait_ge(made_ready, 2)
                pe.wait_ge(piece_ready, READY_AT["wv1"])
            if b != 4:
                if b < 7:
                    attn_prepare_pe(pe, 0, b if b < 4 else b - 1)
                else:
                    attn_values_pe(pe, 0, 0)

        def attn_early_act(a, b):
            if b < 4:
                attn_prepare_act(a, 0, b)
            if b == 7:
                attn_values_act(a, 0, 0)

        def attn_early_dve(v, b):
            if b == 2:
                attn_prepare_dve(v, 0, 2)
            if b == 6:
                attn_prepare_dve(v, 0, 4)

        def attn_prepare_pe(pe, c, step):
            xs = (chunk(XH, c, PAD), chunk(XL, c, PAD))
            if step == 0:
                pe.wait_ge(xl_ready, count(2, c) + 1)
                if c:
                    pe.wait_ge(qk_read, 2 * c)
                else:
                    pe.wait_ge(weights_sb, FFN0.router0 + NC)
                mm3(VQ(c)[:, :], wh("wqk1c", 0), xs, True, True).then_inc(qkv_full, 1)
            if step == 1:
                pe.wait_ge(centred, 2 * c + 1)
                if c:
                    pe.wait_ge(v_placed, 2 * c)
                mm3(R[:, :], wh("wqk1c", P), xs, True, True).then_inc(qkv_full, 1)
            if step == 2:
                pe.wait_ge(centred, 2 * c + 2)
                nc.tensor.matmul(R[0:GR, :], raw("mean_k"), sqk, start=True, stop=False)
                nc.tensor.matmul(R[0:GR, :], raw("mean_q"), sqq, start=False, stop=True).then_inc(var_full, 1)
            if step == 3:
                if c:
                    y_bank_free(pe, 2, c - 1)
                else:
                    pe.wait_ge(var_read, 1)
                mm3(VQ(c)[:, :], wh("wv1"), xs, True, True).then_inc(qkv_full, 1)
            if step == 4:
                if not c:
                    pe.wait_ge(v_copied, 1)
                pe.wait_ge(rstd_qk, c + 1)
                nc.tensor.matmul(R[:, :], raw("spread_k")[0:GR, :], rstd, start=True, stop=True).then_inc(rstd_full, 1)
            if step == (4 if c else 5):
                if c:
                    pe.wait_ge(v_copied, c + 1)
                else:
                    pe.wait_ge(qk_read, 1)
                nc.tensor.matmul(VQ(c)[:, :], raw("spread_q")[0:GR, :], rstd, start=True, stop=True).then_inc(rstd_full, 1)

        def attn_values_pe(pe, c, half):
            pe.wait_ge(v_copied, c + 1)
            if half == 0:
                pe.wait_ge(qk_read, 2 * c + 2)
            else:
                pe.wait_ge(v_placed, 2 * c + 1)
            for w in range(4):
                i = nc.tensor.transpose(R[:, w * P:(w + 1) * P],
                                        VTD[:, 4 * half + w, :, :].rearrange("p s t -> p (s t)"), ident)
            i.then_inc(v_turned, 1)

        def attn_prepare_act(a, c, step):
            if step in (0, 1):
                src, sq, dst = ((VQ(c), sqq, qc), (R, sqk, kc))[step]
                a.wait_ge(qkv_full, 3 * c + 1 + step)
                if c and step == 0:
                    a.wait_ge(qk_ready, 2 * c)
                nc.scalar.activation(sq, src[:, :], ACT.Square)
                nc.scalar.activation(dst, src[:, :], ACT.Copy).then_inc(centred, 1)
            if step == 2:
                a.wait_ge(var_full, c + 1)
                nc.scalar.activation(sdev, R[0:GR, :], ACT.Sqrt, bias=epsv[0:GR, :]).then_inc(var_read, 1)
            if step == 3:
                a.wait_ge(qkv_full, 3 * c + 3)
                if c:
                    a.wait_ge(v_turned, 2 * c)
                for s_ in range(2):
                    i = nc.scalar.activation(VTD[:, :, s_, :], VQ(c)[:, :].rearrange("p (w t) -> p w t", t=WIN), ACT.Copy)
                i.then_inc(v_copied, 1)

        def attn_values_act(a, c, half):
            a.wait_ge(v_turned, 2 * c + half + 1)
            if c:
                a.wait_ge(o_full, UN * (c - 1) + 4 * half + 4)
            src = R[:, :].rearrange("p (i w q h d) -> p i w q h d", i=2, w=2, q=HU, h=2)
            for s_ in range(2):
                rows = slice(64 * s_, 64 * s_ + 64)
                for i_ in range(2):
                    for w in range(2):
                        i = nc.scalar.activation(VB[rows, 2 * half + i_, :, w, s_, 0:HD],
                                                 src[rows, i_, w, :, s_, :], ACT.Copy)
            i.then_inc(v_placed, 1)

        def attn_prepare_dve(v, c, step):
            if step == 2:
                v.wait_ge(var_read, c + 1)
                nc.vector.reciprocal(rstd, sdev).then_inc(rstd_qk, 1)
            if step == 4:
                for k, (bank_, x, dst) in enumerate(((R, kc, KN), (VQ(c), qc, QN))):
                    v.wait_ge(rstd_full, 2 * c + k + 1)
                    v.wait_ge(centred, 2 * c + 2)
                    nc.vector.tensor_tensor(x, x, bank_[:, :], ALU.mult).then_inc(qk_read, 1)
                    v.wait_ge(qk_read, 2 * c + k + 1)
                    if c >= 2:
                        v.wait_ge(s_full, UN * (c - 1))
                    nc.vector.tensor_scalar(dst[c % 2], x, raw("ln_g1"), raw("ln_b1"), ALU.mult, ALU.add)\
                        .then_inc(qk_ready, 1)

        def attn_mask(eng, tile):
            c, i_ = tile // TL, tile % TL
            if tile >= NC * TL:
                return
            heads, done = {nc.vector: (range(0, 8), masked_dve), nc.gpsimd: (range(8, 12), masked_pool),
                           nc.scalar: (range(12, 16), masked_act)}[eng]
            eng.wait_ge(qk_ready, 2 * c + 1)
            if tile >= 2:
                eng.wait_ge(s_full, 2 * (tile - 2) + (1 if eng is nc.vector else 2))
            for h in heads:
                dst, src = KM[tile % 2][:, h, :], KN[c % 2][:, i_ * P:(i_ + 1) * P]
                if eng is nc.scalar:
                    i = eng.activation(dst, src, ACT.Copy, scale=raw("head_mask", h, 1))
                else:
                    i = eng.tensor_scalar(dst, src, raw("head_mask", h, 1), None, ALU.mult)
            i.then_inc(done, 1)

        def attn_pe(pe, c, hook):
            def scores(N):
                if N >= NU:
                    return
                tile, u = N // 2, N % 2
                c_, i_ = tile // TL, tile % TL
                for done in ((masked_pool, masked_act) if u else (masked_dve,)):
                    pe.wait_ge(done, tile + 1)
                if N % UN == 0:
                    pe.wait_ge(qk_ready, 2 * c_ + 2)
                if N >= 2:
                    pe.wait_ge(s_read, N - 1)
                for w in range(2):
                    tok = slice(i_ * P + w * WIN, i_ * P + (w + 1) * WIN)
                    i = nc.tensor.matmul(G[u][w * WIN:(w + 1) * WIN, :], QN[c_ % 2][:, tok],
                                         KM[tile % 2][:, HU * u:HU * u + HU, w * WIN:(w + 1) * WIN],
                                         start=True, stop=True)
                i.then_inc(s_full, 1)

            def turn(N):
                u = N % 2
                pe.wait_ge(p_ready, N + 1)
                if N >= 2:
                    pe.wait_ge(pt_ready, N - 1)
                for q in range(4):
                    i = nc.tensor.transpose(U[u][:, q * P:(q + 1) * P], PRB[u][:, q * P:(q + 1) * P], ident)
                i.then_inc(p_turned, 1)

            def weigh(N):
                tile, u = N // 2, N % 2
                pe.wait_ge(pt_ready, N + 1)
                if N % (UN // 2) == 0:
                    pe.wait_ge(v_placed, N // (UN // 2) + 1)
                if u == 0 and tile:
                    pe.wait_ge(o_read, tile)
                for q in range(4):
                    pr = 4 * u + q
                    i = nc.tensor.matmul(SP[:, pr * 36:(pr + 1) * 36], PT[u][:, q * P:(q + 1) * P],
                                         VB[:, tile % TL, pr, :, :, :].rearrange("p a b d -> p (a b d)"),
                                         start=True, stop=True)
                i.then_inc(o_full, 1)

            nxt = c + 1 < NC
            if c == 0:
                body_start(pe, 2, 0)
                scores(0)
            for n in range(UN):
                N = c * UN + n
                if n == 6 and nxt:
                    attn_prepare_pe(pe, c + 1, 4)
                if N:
                    turn(N - 1)
                scores(N + 1)
                if N >= 2:
                    weigh(N - 2)
                if n == 0:
                    attn_values_pe(pe, c, 1)
                    if c == 0:
                        hook(-1)
                if n == 3 and c:
                    attn_turn_pe(pe, c - 1)
                if n == 4 and c:
                    attn_project_pe(pe, c - 1)
                attn_hooks(n, c, hook, 4)
                if n in PREPARE_AT and nxt:
                    attn_prepare_pe(pe, c + 1, PREPARE_AT[n])
                if n == 7 and nxt:
                    attn_values_pe(pe, c + 1, 0)
            if not nxt:
                turn(NU - 1)
                weigh(NU - 2)
                weigh(NU - 1)
                attn_turn_pe(pe, c)
                hook(10)
                attn_project_pe(pe, c)

        def attn_hooks(n, c, hook, tail_at):
            if n == tail_at and c:
                hook(-1)
            for pos in {0: (0,), 1: (4,), 2: (1, 5), 3: (11, 2, 6), 4: (3, 7), 5: (8,), 6: (9,)}.get(n, ()):
                hook(pos)

        def attn_turn_pe(pe, c):
            pe.wait_ge(o_read, (c + 1) * TL)
            if c + 1 < NC:
                pe.wait_ge(qk_read, 2 * c + 4)
            for j in range(TL):
                i = nc.tensor.transpose(Y[:, j * P:(j + 1) * P], AT[c % 2][:, j * P:(j + 1) * P], ident)
            i.then_inc(a_turned, 1)

        def attn_project_pe(pe, c):
            pe.wait_ge(piece_ready, READY_AT["wproj"])
            pe.wait_ge(al_ready, c + 1)
            mm3(Y[:, :], wh("wproj"), (rbuf[0][:, :], rbuf[1][:, :]), True, True).then_inc(y_full, 1)

        def attn_out_act(a, c):
            a.wait_ge(a_turned, c + 1)
            if c:
                a.wait_ge(al_ready, c)
            nc.scalar.activation(A32w, Y[:, :], ACT.Copy).then_inc(a32_ready, 1)

        def attn_project_act(a, c):
            yt_free(a, 2, c)
            a.wait_ge(y_full, count_y(2, c) + 1)
            nc.scalar.activation(YT[:, :], Y[:, :], ACT.Identity, bias=raw("bproj")).then_inc(yt_ready, 1)

        def attn_project_dve(v, c):
            v.wait_ge(a32_ready, c + 1)
            if c:
                v.wait_ge(y_full, count_y(2, c))
            nc.vector.tensor_copy(rbuf[0][:, :], A32w).then_inc(ah_ready, 1)
            v.wait_ge(ah_ready, c + 1)
            nc.vector.tensor_tensor(rbuf[1][:, :], A32w, rbuf[0][:, :].bitcast(F32), ALU.subtract)\
                .then_inc(al_ready, 1)

        def attn_act(a, chain, c, hook):
            nxt = c + 1 < NC

            def probs(N):
                a.wait_ge(s_read, N + 1)
                nc.scalar.activation(PRB[N % 2], PRB[N % 2], ACT.Exp).then_inc(p_ready, 1)

            def evac(N):
                a.wait_ge(p_turned, N + 1)
                if N >= 2:
                    a.wait_ge(o_full, N - 1)
                nc.scalar.activation(PT[N % 2], U[N % 2][:, :], ACT.Copy).then_inc(pt_ready, 1)

            if c == 0:
                body_start(a, 2, 0)
                attn_mask(nc.scalar, 0)
            for n in range(UN):
                N = c * UN + n
                probs(N)
                if N:
                    evac(N - 1)
                if n == 1:
                    attn_values_act(a, c, 1)
                if n == 4 and c:
                    attn_project_act(a, c - 1)
                attn_hooks(n, c, hook, 5)
                if n in PREPARE_AT and nxt:
                    attn_prepare_act(a, c + 1, PREPARE_AT[n])
                if n == 3 and c:
                    attn_out_act(a, c - 1)
                if n % 2 == 0:
                    attn_mask(nc.scalar, c * TL + n // 2 + 1)
            if nxt:
                attn_values_act(a, c + 1, 0)
            else:
                evac(NU - 1)
                attn_out_act(a, c)
                hook(10)
                attn_project_act(a, c)

        def attn_dve(v, chain, c, hook):
            nxt = c + 1 < NC

            def finish(tile):
                v.wait_ge(o_full, 2 * tile + 2)
                c_, i_ = tile // TL, tile % TL
                O = SP[:, 0:HU * 36].rearrange("p (q w h d) -> p q w h d", q=HU, w=2, h=2)
                for w in range(2):
                    rows = slice(64 * w, 64 * w + 64)
                    i = nc.vector.reciprocal(orec[rows, :].rearrange("p (q h) -> p q h", h=2),
                                             O[rows, :, w, :, HD])
                chain(i)
                for w in range(2):
                    rows = slice(64 * w, 64 * w + 64)
                    for h2 in range(2):
                        i = nc.vector.tensor_tensor(
                            AT[c_ % 2][rows, i_ * P:(i_ + 1) * P].rearrange("p (q h d) -> p q h d", h=2, d=HD)[:, :, h2, :],
                            O[rows, :, w, h2, 0:HD],
                            bcast(orec[rows, :].rearrange("p (q h) -> p q h", h=2)[:, :, h2].unsqueeze(2),
                                  [64, HU, HD]), ALU.mult)
                i.then_inc(o_read, 1)

            if c == 0:
                body_start(v, 2, 0)
                attn_mask(nc.vector, 0)
            for n in range(UN):
                N = c * UN + n
                u = n % 2
                v.wait_ge(s_full, N + 1)
                Sv = G[u][:, :].rearrange("p (h k) -> p h k", k=WIN)
                chain(nc.vector.tensor_reduce(amax[:, HU * u:HU * u + HU], Sv, AX.X, ALU.max))
                if N >= 2:
                    v.wait_ge(p_turned, N - 1)
                nc.vector.tensor_tensor(PRB[u].rearrange("p (h k) -> p h k", k=WIN), Sv,
                                        bcast(amax[:, HU * u:HU * u + HU].unsqueeze(2), [P, HU, WIN]), ALU.subtract)\
                    .then_inc(s_read, 1)
                if n == 6 and nxt:
                    attn_prepare_dve(v, c + 1, 4)
                if u == 0:
                    if N >= 4:
                        finish(N // 2 - 2)
                    attn_mask(nc.vector, N // 2 + 1)
                if n == 4 and c:
                    attn_project_dve(v, c - 1)
                if n == 0 and c == 0:
                    hook(-1)
                attn_hooks(n, c, hook, 7)
                if n == 5 and nxt:
                    attn_prepare_dve(v, c + 1, 2)
            if not nxt:
                finish(NU // 2 - 2)
                finish(NU // 2 - 1)
                attn_project_dve(v, c)

        def attn_pool(g, chain, c, hook, work):
            if c == 0:
                body_start(g, 2, 0)
                attn_mask(nc.gpsimd, 0)
            for n in range(UN):
                if n % 2 == 0:
                    attn_mask(nc.gpsimd, c * TL + n // 2 + 1)
                attn_hooks(n, c, hook, 4)
                if n % 2 and n > 1:
                    work()

        SB = [(U[0], G[1], G[0]), (U[1], SP, Y)]

        def scan_start(eng, c):
            if c == 0:
                body_start(eng, 4, 0)
            elif c >= 2:
                eng.wait_ge(yt_ready, count(4, c - 1))

        def scan_pe(pe, c, hook):
            scan_start(pe, c)
            xs = (chunk(XH, c, PAD), chunk(XL, c, PAD))
            pe.wait_ge(piece_ready, READY_AT["wqkva"])
            pe.wait_ge(xl_ready, count(4, c) + 1)
            for k in range(3):
                mm3(SB[c % 2][k][:, :], wh("wqkva", (2 - k) * P), xs, True, True).then_inc(scan_in, 1)

        def scan_act(a, chain, c, hook):
            scan_start(a, c)
            a.wait_ge(scan_in, 3 * c + 1)
            nc.scalar.activation(buf[c % 2], SB[c % 2][0][:, :], ACT.Sigmoid).then_inc(sig_ready, 1)

        def scan_dve(v, chain, c, hook):
            scan_start(v, c)
            v.wait_ge(sig_ready, c + 1)
            v.wait_ge(scan_in, 3 * c + 2)
            chain(nc.vector.tensor_tensor_scan(buf[2], buf[c % 2], SB[c % 2][1][:, :], 0.0 if c == 0 else carry,
                                               ALU.mult, ALU.add))
            chain(nc.vector.tensor_copy(carry, buf[2][:, CH - 1:CH]))
            v.wait_ge(scan_in, 3 * c + 3)
            yt_free(v, 4, c)
            nc.vector.tensor_tensor(YT[:, :], buf[2], SB[c % 2][2][:, :], ALU.mult).then_inc(yt_ready, 1)

        UL = 16
        UALL = 2 * NC * UL
        TB = [G[0], G[1], U[0]]
        AHEAD = len(TB)
        def PB(cp):
            return U[1] if cp else R

        TURNED = [U[1], TN]
        KVB = [SP, R]
        OB = [SP, R]
        MB = [buf[0], buf[1]]
        RB = [buf[2], buf[3]]
        AB = [buf[4], buf[5]]
        SN = [buf[6], buf[7]]
        CS = [buf[8], buf[9]]
        P32 = [buf[10], buf[11]]
        FH, FL = wh("w1_2", 0, 4 * CH)
        V4 = STG[:, 0:2, :]
        A32 = VT3 = STG[:, 2, :]
        KS = [[t_[:, k:k + CH] for t_ in wh("keys_parts", 0, 2 * CH) for k in (0, CH)],
              [FH[:, k * CH:(k + 1) * CH] for k in range(4)]]
        TURN = 2.0 * float(np.pi)
        VSTEP = 4

        def proj_no(cp, s_):
            return min(cp, NC) * 5 + max(0, cp - NC) * 4 + s_

        def lin_proj_pe(pe, cp, s_):
            c = cp % NC
            xs = (chunk(XH, c, PAD), chunk(XL, c, PAD))
            k = proj_no(cp, s_)
            if s_ == 0:
                pe.wait_ge(xl_ready, count(6, c) + 1)
            if k:
                pe.wait_ge(proj_sb, k)
            else:
                pe.wait_ge(weights_sb, FFN2.router0 + NC)
            if cp and s_ == 0:
                pe.wait_ge(v4_ready, min(cp, NC))
            if s_ == VSTEP:
                mm3(PB(cp)[:, :], wh("wv3"), xs, True, True).then_inc(proj_full, 1)
            else:
                mm3(PB(cp)[:, :], wh("wk3" if cp < NC else "wq3", s_ * P), xs, True, True).then_inc(proj_full, 1)

        def lin_turn_pe(pe, cp):
            k = proj_no(cp, VSTEP)
            pe.wait_ge(proj_sb, k + 1)
            for j in range(TL):
                i = nc.tensor.transpose(PB(cp)[:, j * P:(j + 1) * P], VT3[:, j * P:(j + 1) * P], ident)
            i.then_inc(vt_turned, 1)

        def lin_turn_act(a, cp):
            k = proj_no(cp, VSTEP)
            a.wait_ge(vt_turned, cp + 1)
            if cp >= 2:
                a.wait_ge(unit_used, UL * (cp - 1))
            nc.scalar.activation(V4[:, cp % 2, :], PB(cp)[:, :], ACT.Copy).then_inc(v4_ready, 1)

        def lin_proj_act(a, cp, s_):
            k = proj_no(cp, s_)
            a.wait_ge(proj_full, k + 1)
            if s_ == VSTEP:
                if cp >= 1:
                    a.wait_ge(vt_turned, cp)
                nc.scalar.activation(VT3[:, :], PB(cp)[:, :], ACT.Identity, bias=raw("bv")).then_inc(proj_sb, 1)
                return
            if 4 * cp + s_ >= 2:
                a.wait_ge(ks_ready, 4 * cp + s_ - 1)
            nc.scalar.activation(P32[s_ % 2], PB(cp)[:, :], ACT.Identity,
                                 bias=raw("bk4" if cp < NC else "bq4", s_, 1)).then_inc(proj_sb, 1)

        def lin_split(e_, g, cp, s_):
            if s_ == VSTEP:
                return
            g.wait_ge(proj_sb, proj_no(cp, s_) + 1)
            if cp >= 2 and s_ == 0:
                g.wait_ge(t_full, UL * (cp - 1))
            dst, lo = KS[cp % 2][s_], slice(P // 2, P)
            if cp:
                nc.gpsimd.tensor_scalar(dst, P32[s_ % 2], 1.0, 0.0, ALU.mult, ALU.add).then_inc(ks_high, 1)
            else:
                nc.vector.tensor_copy(dst, P32[s_ % 2]).then_inc(ks_high, 1)
            g.wait_ge(ks_high, 4 * cp + s_ + 1)
            e_.tensor_tensor(dst[lo, :], P32[s_ % 2][lo, :], dst[lo, :].bitcast(F32), ALU.subtract)\
                .then_inc(ks_ready, 1)
            g.wait_ge(ks_ready, 4 * cp + s_ + 1)

        def lin_phases(pe, q):
            cp, n = q // UL, q % UL
            if q >= UALL:
                return
            pe.wait_ge(ks_ready, 4 * cp + (4 if n else 1) if cp >= NC or n == 0 else 4 * cp + 4)
            if q >= AHEAD:
                pe.wait_ge(r_ready, q - AHEAD + 1)
            if cp < NC:
                i_, g_ = n // 4, n % 4
                nc.tensor.matmul(TB[q % AHEAD][:, :], KS[cp % 2][g_][:, i_ * P:(i_ + 1) * P],
                                 WM[:, :, :].rearrange("p j m -> p (j m)"),
                                 start=True, stop=True).then_inc(t_full, 1)
            else:
                g_, j = n // 4, n % 4
                nc.tensor.matmul(TB[q % AHEAD][:, :], WM[:, j, :], KS[cp % 2][g_],
                                 start=True, stop=True).then_inc(t_full, 1)

        def lin_use(pe, q):
            cp, n = q // UL, q % UL
            if cp < NC:
                i_, g_ = n // 4, n % 4
                rows = slice(32 * g_, 32 * g_ + 32)
                if n == 0:
                    pe.wait_ge(v4_ready, cp + 1)
                for s_, src in enumerate((CS, SN)):
                    if s_ == 0:
                        pe.wait_ge(cos_ready, q + 1)
                    else:
                        pe.wait_ge(sin_ready, q + 1)
                    i = nc.tensor.matmul(KVB[s_][rows, :], V4[:, cp % 2, i_ * P + 32 * g_:i_ * P + 32 * g_ + 32],
                                         src[q % 2], start=q < 4, stop=q >= NC * UL - 4)
                i.then_inc(unit_used, 1)
            else:
                c, g_, j = cp - NC, n // 4, n % 4
                rows = slice(32 * g_, 32 * g_ + 32)
                if n == 0:
                    if c == 0:
                        pe.wait_ge(kv_ready, 1)
                    if c >= 2:
                        pe.wait_ge(oq_read, c - 1)
                for s_, src in enumerate((CS, SN)):
                    if s_ == 0:
                        pe.wait_ge(cos_ready, q + 1)
                    else:
                        pe.wait_ge(sin_ready, q + 1)
                    i = nc.tensor.matmul(OB[c % 2][rows, :], KVT[:, s_, j, rows], src[q % 2],
                                         start=j == 0 and s_ == 0, stop=j == 3 and s_ == 1)
                i.then_inc(unit_used, 1)

        def rounds_on_act(q):
            return q % 2 == 0

        def lin_round_act(a, q):
            if q < UALL and rounds_on_act(q):
                a.wait_ge(t_full, q + 1)
                if q >= 2:
                    a.wait_ge(r_ready, q - 1)
                nc.scalar.activation(MB[q % 2], TB[q % AHEAD][:, :], ACT.Identity, bias=roundv).then_inc(m_ready, 1)

        def lin_round_dve(v, q):
            if q < UALL and not rounds_on_act(q):
                v.wait_ge(t_full, q + 1)
                if q >= 2:
                    v.wait_ge(r_ready, q - 1)
                nc.vector.tensor_scalar(MB[q % 2], TB[q % AHEAD][:, :], ROUND, None, ALU.add).then_inc(m_ready_dve, 1)

        def rounded(v, q):
            acts = (q + 2) // 2
            if rounds_on_act(q):
                v.wait_ge(m_ready, acts)
            else:
                v.wait_ge(m_ready_dve, q + 1 - acts)

        def lin_abs(v, q):
            v.wait_ge(r_ready, q + 1)
            if q >= 2:
                v.wait_ge(cos_ready, q - 1)
            nc.vector.tensor_scalar(AB[q % 2].bitcast(U32), RB[q % 2].bitcast(U32), 0x7fffffff, None,
                                    ALU.bitwise_and).then_inc(ab_ready, 1)

        def lin_pool(g, cp, hook):
            if cp == 0:
                body_start(g, 6, 0)
            for n in range(UL):
                if n - 2 in PROJ_AT and PROJ_AT[n - 2] in lin_projects(cp + 1):
                    lin_split(nc.gpsimd, g, cp + 1, PROJ_AT[n - 2])
                lin_hooks(n, hook, 2, {0: (0,), 2: (1,)})

        def lin_trig(a, q):
            a.wait_ge(ab_ready, q + 1)
            if q >= 2:
                a.wait_ge(unit_used, q - 1)
            nc.scalar.activation(CS[q % 2], AB[q % 2], ACT.Sin, scale=-TURN, bias=half_pi).then_inc(cos_ready, 1)
            nc.scalar.activation(SN[q % 2], RB[q % 2], ACT.Sin, scale=-TURN).then_inc(sin_ready, 1)

        def lin_rest(v, chain, q):
            rounded(v, q)
            if q >= 2:
                v.wait_ge(sin_ready, q - 1)
            nc.vector.scalar_tensor_tensor(RB[q % 2], MB[q % 2], ROUND, TB[q % AHEAD][:, :],
                                           ALU.subtract, ALU.subtract).then_inc(r_ready, 1)
            lin_round_dve(v, q + 1)
            lin_abs(v, q)

        PROJ_AT = {6 + s_: s_ for s_ in range(5)}

        def lin_projects(cp):
            return range(5 if cp < NC else 4) if cp < 2 * NC else range(0)

        def lin_early_pe(pe, b):
            if b == 0:
                pe.wait_ge(piece_ready, READY_AT["wo3"])
            if b % 2 == 0 and 2 <= b <= 10:
                lin_proj_pe(pe, 0, b // 2 - 1)
            if b == 12:
                lin_turn_pe(pe, 0)

        def lin_early_act(a, b):
            if b == 2:
                a.wait_ge(piece_ready, len(PIECES))
            if b % 2 == 0 and 2 <= b <= 10:
                lin_proj_act(a, 0, b // 2 - 1)
            if b == 12:
                lin_turn_act(a, 0)

        def lin_early_dve(v, b):
            if b % 2 == 1 and 3 <= b <= 9:
                lin_split(nc.vector, v, 0, (b - 3) // 2)

        def lin_hooks(n, hook, tail_at, steps):
            if n == tail_at:
                hook(-1)
            for pos in steps.get(n, ()):
                hook(pos)

        def lin_pe(pe, cp, hook):
            if cp == 0:
                body_start(pe, 6, 0)
                pe.wait_ge(phase_weights, 1)
                for q in range(AHEAD):
                    lin_phases(pe, q)
            for n in range(UL):
                q = UL * cp + n
                if cp == NC and n == 0:
                    pe.wait_ge(kvf_ready, 1)
                    pe.wait_ge(proj_sb, proj_no(NC, 4))
                    pe.wait_ge(x32_ready, turned["norms"])
                    pe.wait_ge(res_done, turned["tails"])
                    for s_ in range(2):
                        for j in range(4):
                            i = nc.tensor.transpose(TURNED[s_][:, j * P:(j + 1) * P], V4[:, s_, j * P:(j + 1) * P], ident)
                    i.then_inc(kv_turned, 1)
                lin_phases(pe, q + AHEAD)
                lin_use(pe, q)
                if n in PROJ_AT and PROJ_AT[n] in lin_projects(cp + 1):
                    if cp == NC and n == 8:
                        pe.wait_ge(kv_ready, 1)
                    lin_proj_pe(pe, cp + 1, PROJ_AT[n])
                if n == 14 and cp + 1 < NC:
                    lin_turn_pe(pe, cp + 1)
                if n == 2 and cp > NC:
                    project_pe(pe, cp - NC - 1)
                lin_hooks(n, hook, 3 if cp in (0, NC) else 6, {5: (2,)})
            if cp == 2 * NC - 1:
                project_pe(pe, NC - 1)

        def lin_act(a, cp, hook):
            if cp == 0:
                body_start(a, 6, 0)
                for q in range(2):
                    lin_round_act(a, q)
            if cp == NC:
                a.wait_ge(unit_used, NC * UL)
                for s_ in range(2):
                    i = nc.scalar.activation(V4[:, s_, :], KVB[s_][:, :], ACT.Copy, scale=1.0 / P)
                i.then_inc(kvf_ready, 1)
            for n in range(UL):
                q = UL * cp + n
                lin_round_act(a, q + 2)
                lin_trig(a, q)
                if n - 1 in PROJ_AT and PROJ_AT[n - 1] in lin_projects(cp + 1):
                    lin_proj_act(a, cp + 1, PROJ_AT[n - 1])
                if n == 15 and cp + 1 < NC:
                    lin_turn_act(a, cp + 1)
                if n == 1 and cp > NC:
                    output_act(a, cp - NC - 1)
                if n == 4 and cp > NC:
                    project_act(a, cp - NC - 1)
                lin_hooks(n, hook, 6, {6: (2,)})
            if cp == 2 * NC - 1:
                output_act(a, NC - 1)
                project_act(a, NC - 1)

        def lin_dve(v, chain, cp, hook):
            if cp == 0:
                body_start(v, 6, 0)
                nc.vector.memset(KVT[:, :, :, :].rearrange("p s j m -> p (s j m)"), 0.0).then_inc(kvt_cleared, 1)
            for n in range(UL):
                q = UL * cp + n
                if q == 0:
                    lin_round_dve(v, 0)
                lin_rest(v, chain, q)
                if cp == NC and n == 1:
                    v.wait_ge(kv_turned, 1)
                    v.wait_ge(kvt_cleared, 1)
                    for s_ in range(2):
                        for j in range(4):
                            at_ = lambda ap2: ap2.rearrange("p (g k d) -> p g k d", g=4, d=HD)[:, :, j, :]
                            i = nc.vector.tensor_copy(at_(KVT[:, s_, j, :]), at_(TURNED[s_][:, j * P:(j + 1) * P]))
                    i.then_inc(kv_ready, 1)
                if n == 2 and cp > NC:
                    project_dve(v, cp - NC - 1)
                lin_hooks(n, hook, 4 if cp in (0, NC) else 9, {0: (0,), 3: (1,), 4: (11,), 8: (3,)})
            if cp == 2 * NC - 1:
                project_dve(v, NC - 1)

        def output_act(a, c):
            a.wait_ge(unit_used, UL * (NC + c + 1))
            if c == 0:
                a.wait_ge(vt_turned, NC)
            else:
                a.wait_ge(al_ready, NC + c)
            nc.scalar.activation(A32[:, :], OB[c % 2][:, :], ACT.Copy).then_inc(oq_read, 1)

        def project_pe(pe, c):
            y_bank_free(pe, 6, c)
            pe.wait_ge(al_ready, NC + c + 1)
            mm3(Y[:, :], wh("wo3"), (rbuf[0][:, :], rbuf[1][:, :]), True, True).then_inc(y_full, 1)

        def project_act(a, c):
            yt_free(a, 6, c)
            a.wait_ge(y_full, count_y(6, c) + 1)
            nc.scalar.activation(YT[:, :], Y[:, :], ACT.Identity, bias=raw("bo")).then_inc(yt_ready, 1)

        def project_dve(v, c):
            v.wait_ge(oq_read, c + 1)
            if c:
                v.wait_ge(y_full, count_y(6, c))
            nc.vector.tensor_copy(rbuf[0][:, :], A32[:, :]).then_inc(ah_ready, 1)
            v.wait_ge(ah_ready, NC + c + 1)
            nc.vector.tensor_tensor(rbuf[1][:, :], A32[:, :], rbuf[0][:, :].bitcast(F32), ALU.subtract)\
                .then_inc(al_ready, 1)

        roundv = VEC[:, 17:18]

        STAGES_ = [
            ("stage0", 0, 0), (FFN0, 1, 1), ("attn", 2, 2), (FFN1, 3, 3), ("scan", 4, 4), (FFN2, 5, 5),
            ("keys", None, 6), ("queries", 6, None), (FFN3, 7, 7), (FFN4, 8, 8),
        ]

        def slots():
            bodies = [(body, t, n, c) for body, t, n in STAGES_ for c in range(NC)]
            fronts = [(n, c) if n else None for _, _, n, c in bodies] + [None, None]
            tails = []
            for k, (body, t, n, c) in enumerate(bodies):
                tail = tails.pop() if tails else None
                if t is not None:
                    tails.append((t, c))
                yield body, c, tail, fronts[k + 2], fronts[k + 1]

        BODY = {
            "stage0": (stage0_pe, stage0_act, stage0_dve), "attn": (attn_pe, attn_act, attn_dve),
            "scan": (scan_pe, scan_act, scan_dve),
            "keys": (lin_pe, lin_act, lin_dve),
            "queries": tuple((lambda *args, f_=f_: f_(*args[:-2], NC + args[-2], args[-1]))
                             for f_ in (lin_pe, lin_act, lin_dve)),
        }
        HOOKED = ("attn", "keys", "queries")

        def walk(which, eng, chain, do_front, do_tail):
            late = False
            for body, c, tail, norm, route in slots():
                was_late, late = late, body in ("stage0", "scan") or isinstance(body, Ffn) and body.dense
                late_norm = norm if not late else route if was_late else None
                def hook(pos):
                    if pos == -1:
                        if tail:
                            do_tail(*tail)
                    elif pos >= EARLY:
                        if body in (FFN0, FFN2):
                            early = (attn_early_pe, attn_early_act, attn_early_dve) if body is FFN0 else \
                                (lin_early_pe, lin_early_act, lin_early_dve)
                            early[which](eng, pos - EARLY)
                    elif pos == LATE_NORM:
                        do_front(body.norm, 1, 2)
                        do_front(body.norm, 1, 3)
                    elif pos == LATE_ROUTE:
                        do_front(body.norm, 0, 10)
                    else:
                        front = late_norm if pos in (2, 3) else norm if pos in NORM_STEPS else route
                        if front:
                            do_front(*front, pos)
                if isinstance(body, Ffn):
                    (ffn_pe, ffn_act, ffn_dve)[which](*([eng] + ([chain] if which else []) + [body, c, hook]))
                else:
                    first = () if body != "scan" else (3, 0) if which == 2 else (2,)
                    for pos in first:
                        hook(pos)
                    args = [c, hook]
                    BODY[body][which](*([eng] + ([chain] if which == 2 or which == 1 and body not in ("keys", "queries") else []) + args))
                    if body not in HOOKED:
                        if body == "stage0":
                            first = (0,)
                            hook(0)
                        hook(-1)
                        for pos in ALL_STEPS:
                            if pos not in first and (c, pos) != (NC - 1, 10):
                                hook(pos)

        block = ctx.enter_context(nc.Block())

        @block.sync
        def _(sp):
            for c in range(NC):
                sp.dma_start(tiles(X, c), x_in[bass.ts(c, CH), :].rearrange("(t p) d -> p t d", p=P))\
                    .then_inc(x_loaded[c], 16)
                if c == 0:
                    sp.dma_start(WR[:, :], w_raw).then_inc(raw_loaded, 16)
            for i, (_, kind, _, _, col, n) in enumerate(PIECES):
                if i >= STAGES:
                    sp.wait_ge(piece_ready, i - STAGES + 1)
                src = w_split if kind == "split" else w_exact
                sp.dma_start(STG[:, i % STAGES, 0:n], src[:, col:col + n]).then_inc(piece_loaded[i % STAGES], 16)
            for c in range(NC):
                sp.wait_ge(res_done, count(8, c) + 1)
                sp.dma_start(out[bass.ts(c, CH), :].rearrange("(t p) d -> p t d", p=P), tiles(X, c))\
                    .then_inc(out_stored, 16)
            sp.wait_ge(out_stored, 16 * NC)

        @block.gpsimd
        def _(g):
            chain = Chain(g, pool_chain)
            state = [0]

            def work(limit):
                i = state[0]
                if i >= len(PIECES) or PIECES[i][0] > limit:
                    return
                state[0] += 1
                _, kind, _, at_, _, n = PIECES[i]
                g.wait_ge(piece_loaded[i % STAGES], 16 * (i // STAGES + 1))
                if PIECES[i][0] == 2:
                    g.wait_ge(yt_ready, count(1, 3) + 1)
                if PIECES[i][0] == 3:
                    g.wait_ge(yt_ready, count(3, 3) + 1)
                s_ = STG[:, i % STAGES, 0:n]
                if kind == "exact":
                    nc.gpsimd.tensor_scalar(WE[:, at_:at_ + n], s_, 1.0, 0.0, ALU.mult, ALU.add)\
                        .then_inc(piece_ready, 1)
                else:
                    hi = WH[:, at_:at_ + n]
                    chain(nc.gpsimd.tensor_scalar(hi, s_, 1.0, 0.0, ALU.mult, ALU.add))
                    nc.gpsimd.tensor_tensor(WL[:, at_:at_ + n], s_, hi.bitcast(F32), ALU.subtract)\
                        .then_inc(piece_ready, 1)

            g.wait_ge(fills_ready, 1)
            for c in range(NC):
                first_rstd(g, chain, c)
            while state[0] < len(PIECES) and PIECES[state[0]][0] == 0:
                work(0)
            for body, c, tail, norm, route in slots():
                def hook(pos):
                    if pos in NORM_STEPS and norm:
                        front_pool(g, chain, *norm, pos)
                limit = {"stage0": 0, FFN0: 1, "attn": 2, FFN1: 2, "scan": 3, FFN2: 3}.get(body, 3)
                if isinstance(body, Ffn):
                    ffn_pool(g, chain, body, c, hook, lambda: work(limit))
                elif body in ("keys", "queries"):
                    lin_pool(g, c + (NC if body == "queries" else 0), hook)
                elif body == "attn":
                    attn_pool(g, chain, c, hook, lambda: work(limit))
                else:
                    for pos in range(4):
                        hook(pos)
                        work(limit)
                if c == NC - 1:
                    while state[0] < len(PIECES) and PIECES[state[0]][0] <= limit:
                        work(limit)

        @block.scalar
        def _(a):
            chain = Chain(a, act_chain)
            a.wait_ge(raw_loaded, 16)
            nc.scalar.activation(a_dec, raw("decay"), ACT.Sigmoid).then_inc(decay_ready, 1)
            for c in range(NC):
                first_copy(a, c)
            a.wait_ge(consts_ready, 1)
            walk(1, a, chain, lambda n, c, pos: front_act(a, chain, n, c, pos), lambda t, c: None)

        @block.vector
        def _(v):
            chain = Chain(v, dve_chain)
            for ap, value in ((mhalf, -0.5), (half_pi, float(np.pi / 2)), (epsv, EPS), (roundv, ROUND)):
                nc.vector.memset(ap, value)
            WM32 = buf[11]
            nc.vector.memset(zero, 0.0).then_inc(fills_ready, 1)
            for c in range(NC):
                first_stats(v, chain, c)
            for c in range(NC):
                first_normalise(v, c)
            for t_ in (XH, XL):
                nc.vector.memset(t_[:, 0:PAD].bitcast(F32), 0.0)
                chain(nc.vector.memset(t_[:, T + PAD:T + 2 * PAD].bitcast(F32), 0.0))
            v.wait_ge(raw_loaded, 16)
            v.wait_ge(decay_ready, 1)
            for c in range(2):
                first_split(v, chain, c)
            nc.vector.tensor_scalar(gam2, raw("gamma2"), float(np.sqrt(P)), None, ALU.mult)
            nc.vector.tensor_tensor(bias0, raw("b0"), raw("convb"), ALU.add).then_inc(consts_ready, 1)
            made = B[:, 0:2, :].rearrange("p a b -> p (a b)")
            for k in range(TAPS):
                nc.vector.tensor_scalar(made[:, P * (1 + k):P * (2 + k)], ident, raw("convw", k, 1), None, ALU.mult)
            chain(nc.vector.tensor_scalar(one_minus_a, a_dec, -1.0, 1.0, ALU.mult, ALU.add))
            chain(nc.vector.tensor_scalar(made[:, 0:P], raw("wt0"), one_minus_a, None, ALU.mult))

            def split_made(at_, n):
                o = SPLIT_AT["wt0s"][0] + at_
                chain(nc.vector.tensor_copy(WH[:, o:o + n], made[:, at_:at_ + n]))
                nc.vector.tensor_tensor(WL[:, o:o + n], made[:, at_:at_ + n], WH[:, o:o + n].bitcast(F32),
                                        ALU.subtract).then_inc(made_ready, 1)

            split_made(0, 6 * P)
            for c in range(2, NC):
                first_split(v, chain, c)
            stage0_dve(v, chain, 0, None)
            stage0_dve(v, chain, 1, None)
            w3 = raw("wqk1").rearrange("p (g d) -> p g d", d=HD)
            chain(nc.vector.tensor_reduce(wmean[:, :], w3, AX.X, ALU.add))
            chain(nc.vector.tensor_scalar(wmean[:, :], wmean[:, :], 1.0 / HD, None, ALU.mult))
            chain(nc.vector.tensor_tensor(made[:, P * 6:P * 8].rearrange("p (g d) -> p g d", d=HD), w3,
                                          bcast(wmean[:, :].unsqueeze(2), [P, 32, HD]), ALU.subtract))
            split_made(6 * P, 2 * P)
            for j in range(4):
                mask = raw("head_of_4", j, 1)
                i = nc.vector.tensor_scalar(WM32[:, j * P:(j + 1) * P], raw("proj"), mask,
                                            1.0 / (float(np.sqrt(HD)) * 2.0 * float(np.pi)), ALU.mult, ALU.mult)
            chain(i)
            wm = WM[:, :, :].rearrange("p j m -> p (j m)")
            chain(nc.vector.tensor_copy(wm, WM32))
            for r_ in (32, 96):
                i = nc.vector.tensor_tensor(wm[r_:r_ + 32, :], WM32[r_:r_ + 32, :], wm[r_:r_ + 32, :].bitcast(F32),
                                            ALU.subtract)
            i.then_inc(phase_weights, 1)
            chain(nc.vector.memset(VB[:, :, :, :, :, :].rearrange("p i q w h d -> p (i q w h d)"), 0.0))
            for s_ in range(2):
                nc.vector.memset(VB[64 * s_:64 * s_ + 64, :, :, :, s_, HD].rearrange("p i q w -> p (i q) w"), 1.0)
            walk(2, v, chain, lambda n, c, pos: front_dve(v, chain, n, c, pos),
                 lambda t, c: tail_dve(v, chain, t, c))
            tail_dve(v, chain, 8, NC - 1)

        @block.tensor
        def _(pe):
            pe.wait_ge(raw_loaded, 16)
            for c in range(NC):
                first_turn(pe, c)
            walk(0, pe, None, lambda n, c, pos: front_pe(pe, n, c, pos), lambda t, c: tail_pe(pe, t, c))
            tail_pe(pe, 8, NC - 1)


def kernel(**inputs):
    import concourse.bacc as _bacc
    from concourse.bass_utils import run_bass_kernel_spmd as _run

    f = {k: np.asarray(v) for k, v in inputs.items()}

    def rows(a):
        a = a.reshape(a.shape[0], -1)
        return np.concatenate([a, np.zeros((P - a.shape[0], a.shape[1]), a.dtype)]) if a.shape[0] < P else a

    def wide(a):
        return np.concatenate([a, np.zeros((a.shape[0], P - a.shape[1]), a.dtype)], axis=1)

    def experts(a):
        return a.transpose(1, 0, 2).reshape(a.shape[1], -1)

    def blocks(a):
        return a.reshape(-1, P, a.shape[-1]).transpose(1, 0, 2).reshape(P, -1)

    def cols(a):
        return a.reshape(-1, P).T

    def four_times(a):
        return np.tile(a.reshape(-1, 4, 1, P // 4), (1, 1, 4, 1)).reshape(-1, 4 * P)

    qkv = f["L1_attn_W_qkv"]
    z64 = np.zeros((P, 64), np.float32)
    w = {
        "gate0": wide(f["L0_ffn_gate_w"].T), "w1_0": experts(f["L0_ffn_w1"]), "w3_0": experts(f["L0_ffn_w3"]),
        "w2_0": blocks(f["L0_ffn_w2"].reshape(-1, P)),
        "wqk1": qkv[:, 0:2 * P], "wv1": qkv[:, 2 * P:], "wproj": f["L1_attn_W_proj"],
        "gate1": wide(f["L1_ffn_gate_w"].T),
        "wg1": np.concatenate([experts(f["L1_ffn_w_gate"]), f["L1_ffn_ws_gate"], z64], axis=1),
        "wu1": np.concatenate([experts(f["L1_ffn_w_up"]), f["L1_ffn_ws_up"], z64], axis=1),
        "wd1": blocks(np.concatenate([f["L1_ffn_w_down"].reshape(-1, P), f["L1_ffn_ws_down"], z64.T], axis=0)),
        "wqkva": f["L2_attn_W_qkva"].T, "gate2": wide(f["L2_ffn_Wg"]), "w1_2": experts(f["L2_ffn_W1"]),
        "w2_2": blocks(f["L2_ffn_W2"].reshape(-1, P)),
        "b2_2": rows(np.tile(np.stack([f["L2_ffn_b2"], np.zeros_like(f["L2_ffn_b2"])], axis=1).reshape(NH, P), (2, 1))),
        "wq3": four_times(f["L3_attn_wq"]), "wk3": four_times(f["L3_attn_wk"]), "wv3": f["L3_attn_wv"], "wo3": f["L3_attn_wo"],
        "w1_3": f["L3_attn_w1"], "w2_3": blocks(f["L3_attn_w2"]), "fw1": f["L3_ffn_W1"], "fw2": blocks(f["L3_ffn_W2"]),
        "wt0": f["L0_attn_W"].T, "proj": np.tile(f["L3_attn_proj_mat"], (NH, 1)),
        "decay": cols(f["L0_attn_decay_logit"]), "convw": f["L0_attn_conv_w"].reshape(P, TAPS),
        "b0": cols(f["L0_attn_b"]), "convb": cols(f["L0_attn_conv_b"]),
        "ln_g1": cols(np.tile(f["L1_attn_ln_gamma"], NH)), "ln_b1": cols(np.tile(f["L1_attn_ln_beta"], NH)),
        "bproj": cols(f["L1_attn_b_proj"]), "gamma2": cols(f["L2_attn_gamma"]),
        "bg2": rows(f["L2_ffn_bg"].reshape(-1, 1)), "b1_2": cols(f["L2_ffn_b1"].reshape(-1)),
        "bq4": four_times(f["L3_attn_bq"].reshape(1, P)).reshape(4, P).T,
        "bk4": four_times(f["L3_attn_bk"].reshape(1, P)).reshape(4, P).T, "bv": cols(f["L3_attn_bv"]),
        "bo": cols(f["L3_attn_bo"]), "g1_3": cols(f["L3_attn_ln1_g"]), "e1_3": cols(f["L3_attn_ln1_b"]),
        "g2_3": cols(f["L3_attn_ln2_g"]), "e2_3": cols(f["L3_attn_ln2_b"]), "b1_3": cols(f["L3_attn_b1"]),
        "b2_3": cols(f["L3_attn_b2"]), "fb1": cols(f["L3_ffn_b1"]), "fb2": cols(f["L3_ffn_b2"]),
    }
    k = np.arange(P)
    w["ident"] = np.eye(P, dtype=np.float32)
    for at_, name in ((0, "q"), (NH, "k")):
        w["mean_" + name] = (k[:, None] // HD + at_ == k[None, :2 * NH]).astype(np.float32) / HD
        w["spread_" + name] = rows((k[:2 * NH, None] == k[None, :] // HD + at_).astype(np.float32))
    w["iota"] = np.tile(np.arange(16, dtype=np.float32), (P, 1))
    w["head_mask"] = (k[:, None] // HD == np.arange(NH)[None, :]).astype(np.float32)
    w["head_of_4"] = (k[:, None] // HD % 4 == np.arange(4)[None, :]).astype(np.float32)
    w["sel16"] = rows(((k[:2 * NH, None] % NH) == np.arange(8 * P)[None, :] // (P // 2)).astype(np.float32))

    def pack(names, table):
        sizes = dict(table)
        for n in names:
            assert w[n].shape == (P, sizes[n]), (n, w[n].shape, sizes[n])
        return np.ascontiguousarray(np.concatenate([w[n] for n in names], axis=1))

    order = [n for g in GROUPS for n in g]
    arrays = {
        "in_x": np.ascontiguousarray(f["L0_attn_x"].reshape(T, P)),
        "in_w_split": pack([n for n in order if n not in EXACT_AT], SPLIT),
        "in_w_exact": pack([n for n in order if n in EXACT_AT], EXACT),
        "in_w_raw": pack([n for n, _ in RAW], RAW),
    }
    nc = _bacc.Bacc("TRN2", target_bir_lowering=False, num_devices=1)
    args = [nc.dram_tensor(n, a.shape, mybir.dt.from_np(a.dtype), kind="ExternalInput").ap()
            for n, a in arrays.items()]
    out = nc.dram_tensor("out_0", (T, P), F32, kind="ExternalOutput").ap()
    build(nc, *args, out)
    r = _run(nc, [arrays], core_ids=[0])
    return r.results[0]["out_0"].reshape(1, T, P)
```
